# Optimizing a Trainium2 kernel written in Bass

```python
import numpy as np
import jax
import jax.numpy as jnp

def _softmax(x, axis=-1):
    return jax.nn.softmax(x, axis=axis)

def _gelu(x):
    return jax.nn.gelu(x, approximate=True)

def _silu(x):
    return jax.nn.silu(x)

def _sigmoid(x):
    return jax.nn.sigmoid(x)

def _layernorm(x, axis=-1, eps=1e-05):
    m = jnp.mean(x, axis=axis, keepdims=True)
    v = jnp.var(x, axis=axis, keepdims=True)
    return (x - m) / jnp.sqrt(v + eps)

def _scatter_add(tgt, idx, src, axis=0):
    return tgt.at[idx].add(src)

def _segment_sum(src, seg, n):
    return jax.ops.segment_sum(src, seg, n)
kernel_name = 'mk_adaln_ffn_d4_seqx_r4_25267e'

def setup_inputs(seed: int=0):
    np.random.seed(seed)
    _w = jnp.asarray

    def _rec_inputs():
        import jax
        import jax.numpy as jnp
        _rk = jax.random.key(seed)
        x = -0.0002928 + 1 * jax.random.normal(jax.random.fold_in(_rk, 1), (4, 512, 256), jnp.float32)
        _lenS = 512 - jax.random.randint(jax.random.fold_in(_rk, 7), (4,), 0, max(1, 512 // 4) + 1, jnp.int32)
        _lenS2 = 512 - jax.random.randint(jax.random.fold_in(_rk, 8), (4,), 0, max(1, 512 // 4) + 1, jnp.int32)
        fside_16xSxS_0 = -5.72187e-05 + 0.999849 * jax.random.normal(jax.random.fold_in(_rk, 11), (16, 512, 512), jnp.float32)
        cond_64 = -0.0265395 + 0.99382 * jax.random.normal(jax.random.fold_in(_rk, 13), (4, 64), jnp.float32)
        _validS = jnp.arange(512)[None, :] < _lenS[:, None]
        _validS2 = jnp.arange(512)[None, :] < _lenS2[:, None]
        _causal = jnp.tril(jnp.ones((512, 512), dtype=bool))
        mask_BxS_bk0 = jnp.logical_not(jnp.broadcast_to(_validS[:, :], (4, 512)))
        mask_BxS_bf1 = jnp.ones((4, 512), dtype=bool)
        return (x, fside_16xSxS_0, cond_64, mask_BxS_bk0, mask_BxS_bf1)
    x, fside_16xSxS_0, cond_64, mask_BxS_bk0, mask_BxS_bf1 = _rec_inputs()

    def _L0_cond_setup():
        import jax, jax.numpy as jnp
        import numpy as np
        B, N, DIM, H, DH = (2, 512, 256, 16, 64)
        INNER = H * DH
        EPS = 1e-05

        def layernorm(x, g):
            mean = jnp.mean(x, axis=-1, keepdims=True)
            var = jnp.var(x, axis=-1, keepdims=True)
            return (x - mean) * jax.lax.rsqrt(var + EPS) * g
        key = jax.random.key(seed)
        ks = jax.random.split(key, 10)
        x = jax.random.normal(ks[0], (B, N, DIM), dtype=jnp.float32)
        attn_bias = jax.random.normal(ks[1], (H, N, N), dtype=jnp.float32)
        mask = jax.random.randint(ks[2], (B, N), 0, 2).astype(bool)
        g_in = jnp.ones((DIM,), dtype=jnp.float32)
        null_attn_bias = jax.random.normal(ks[3], (H,), dtype=jnp.float32)
        null_kv = jax.random.normal(ks[4], (2, DH), dtype=jnp.float32)
        Wq = jax.random.normal(ks[5], (DIM, INNER), dtype=jnp.float32) * 0.02
        Wkv = jax.random.normal(ks[6], (DIM, 2 * DH), dtype=jnp.float32) * 0.02
        Wo = jax.random.normal(ks[7], (INNER, DIM), dtype=jnp.float32) * 0.02
        g_out = jnp.ones((DIM,), dtype=jnp.float32)
        return {'x': x, 'attn_bias': attn_bias, 'mask': mask, 'g_in': g_in, 'null_attn_bias': null_attn_bias, 'null_kv': null_kv, 'Wq': Wq, 'Wkv': Wkv, 'Wo': Wo, 'g_out': g_out}
    _L0_cond_all = _L0_cond_setup()
    _L0_cond_in = {k: v for k, v in _L0_cond_all.items() if k in ('g_in', 'null_attn_bias', 'Wq', 'Wkv', 'Wo', 'g_out')}
    del _L0_cond_all

    def _L0_ffn_setup():
        import jax, jax.numpy as jnp
        import numpy as np
        EPS = 1e-05

        @jax.custom_vjp
        def ste_quantize(w):
            scale = jnp.maximum(jnp.mean(jnp.abs(w)), EPS)
            return jnp.clip(jnp.round(w / scale), -1.0, 1.0)

        def _ste_fwd(w):
            return (ste_quantize(w), None)

        def _ste_bwd(_, g):
            return (g,)
        ste_quantize.defvjp(_ste_fwd, _ste_bwd)
        key = jax.random.key(seed)
        k1, k2 = jax.random.split(key)
        x = jax.random.normal(k1, (8, 2048, 256), dtype=jnp.float32)
        weight = jax.random.normal(k2, (256, 256), dtype=jnp.float32) * 0.02
        return {'x': x, 'weight': weight}
    _L0_ffn_all = _L0_ffn_setup()
    _L0_ffn_in = {k: v for k, v in _L0_ffn_all.items() if k in ('weight',)}
    del _L0_ffn_all

    def _L1_cond_setup():
        import jax, jax.numpy as jnp
        import numpy as np
        DIM = 256
        HEADS = 16
        DIM_HEAD = 64
        SCALE = 8.0

        def ln(x, g, eps=1e-05):
            mean = x.mean(axis=-1, keepdims=True)
            var = ((x - mean) ** 2).mean(axis=-1, keepdims=True)
            return (x - mean) * jax.lax.rsqrt(var + eps) * g

        def l2norm(t):
            n = jnp.maximum(jnp.linalg.norm(t, axis=-1, keepdims=True), 1e-12)
            return t / n

        def rel_pos_bias(n, w0, b0, g0, w1, b1, g1, w2, b2, dtype):
            pos = jnp.arange(-n + 1, n, dtype=dtype)[:, None]
            h = jax.nn.silu(ln(pos @ w0 + b0, g0))
            h = jax.nn.silu(ln(h @ w1 + b1, g1))
            h = h @ w2 + b2
            i = jnp.arange(n)
            idx = i[:, None] - i[None, :] + n - 1
            bias = h[idx]
            return jnp.transpose(bias, (2, 0, 1))
        key = jax.random.key(seed)
        ks = jax.random.split(key, 16)
        b, n = (2, 512)
        inner = HEADS * DIM_HEAD
        s = 0.02
        return {'x': jax.random.normal(ks[0], (b, n, DIM), jnp.float32), 'mask': jnp.ones((b, n), dtype=bool), 'g_norm': jnp.ones((DIM,), jnp.float32), 'Wq': jax.random.normal(ks[1], (DIM, inner), jnp.float32) * s, 'Wkv': jax.random.normal(ks[2], (DIM, 2 * DIM_HEAD), jnp.float32) * s, 'q_scale': jnp.ones((DIM_HEAD,), jnp.float32), 'k_scale': jnp.ones((DIM_HEAD,), jnp.float32), 'null_kv': jax.random.normal(ks[3], (2, DIM_HEAD), jnp.float32), 'null_attn_bias': jax.random.normal(ks[4], (HEADS,), jnp.float32), 'w0': jax.random.normal(ks[5], (1, DIM), jnp.float32) * s, 'b0': jnp.zeros((DIM,), jnp.float32), 'g0': jnp.ones((DIM,), jnp.float32), 'w1': jax.random.normal(ks[6], (DIM, DIM), jnp.float32) * s, 'b1': jnp.zeros((DIM,), jnp.float32), 'g1': jnp.ones((DIM,), jnp.float32), 'w2': jax.random.normal(ks[7], (DIM, HEADS), jnp.float32) * s, 'b2': jnp.zeros((HEADS,), jnp.float32), 'Wout': jax.random.normal(ks[8], (inner, DIM), jnp.float32) * s, 'g_out': jnp.ones((DIM,), jnp.float32)}
    _L1_cond_all = _L1_cond_setup()
    _L1_cond_in = {k: v for k, v in _L1_cond_all.items() if k in ('g_norm', 'Wq', 'Wkv', 'q_scale', 'k_scale', 'null_attn_bias', 'w0', 'b0', 'g0', 'w1', 'b1', 'g1', 'w2', 'b2', 'Wout', 'g_out')}
    del _L1_cond_all

    def _L1_ffn_setup():
        import jax, jax.numpy as jnp
        import numpy as np
        TOP_K = 2
        CAPACITY_FACTOR = 1.0
        key = jax.random.key(seed)
        ks = jax.random.split(key, 4)
        sl, bs, hs, ffn, E = (512, 8, 256, 1024, 8)
        x = jax.random.normal(ks[0], (sl, bs, hs), dtype=jnp.float32)
        w_router = jax.random.normal(ks[1], (hs, E), dtype=jnp.float32) * 0.02
        w1 = jax.random.normal(ks[2], (E, hs, ffn), dtype=jnp.float32) * 0.02
        w2 = jax.random.normal(ks[3], (E, ffn, hs), dtype=jnp.float32) * 0.02
        bias = jnp.zeros((1, 1, hs), dtype=jnp.float32)
        return {'x': x, 'w_router': w_router, 'w1': w1, 'w2': w2, 'bias': bias}
    _L1_ffn_all = _L1_ffn_setup()
    _L1_ffn_in = {k: v for k, v in _L1_ffn_all.items() if k in ('w_router', 'w1', 'w2', 'bias')}
    del _L1_ffn_all

    def _L2_cond_setup():
        import jax, jax.numpy as jnp
        import numpy as np
        B, S, H = (4, 512, 256)
        E = 8
        M = 128
        K = 2
        N_SHARED = 2
        SM = M * N_SHARED
        G = 64
        GE_TEMP = 1.0
        ALPHA = 0.001
        SEQ_AUX = True
        NORM_TOPK = True
        COS_TEMP = 0.78
        CONS_ALPHA = 0.01
        LEAKY_SLOPE = 0.01
        EPS_COS = 1e-08

        def _leaky(x):
            return jnp.where(x >= 0, x, LEAKY_SLOPE * x)

        def _moe_forward(hidden_states, g, wt, wg, w_gate, w_up, w_down, sw_gate, sw_up, sw_down):
            b, s, h = hidden_states.shape
            x = hidden_states.reshape(-1, h)
            T = x.shape[0]
            logits_h = x @ wt.T
            logits_g = g @ wg.T
            logits_g = jnp.repeat(logits_g, s, axis=0)
            logits = (logits_h + logits_g / GE_TEMP) / (1.0 + 1.0 / GE_TEMP)
            scores = jax.nn.softmax(logits, axis=-1)
            topk_w, topk_idx = jax.lax.top_k(scores, K)
            if K > 1 and NORM_TOPK:
                topk_w = topk_w / (topk_w.sum(-1, keepdims=True) + 1e-20)
            onehot = jax.nn.one_hot(topk_idx.reshape(b, s * K), E, dtype=jnp.float32)
            ce = onehot.sum(1) / (s * K / E)
            aux_loss = (ce * scores.reshape(b, s, E).mean(1)).sum(1).mean() * ALPHA
            gp = _leaky(jnp.einsum('th,ehm->etm', x, w_gate))
            up = jnp.einsum('th,ehm->etm', x, w_up)
            y_all = jnp.einsum('etm,emh->eth', gp * up, w_down)
            y_sel = y_all[topk_idx, jnp.arange(T)[:, None], :]
            y = (y_sel * topk_w[..., None]).sum(1).reshape(b, s, h)
            p = _leaky(hidden_states @ sw_gate) * (hidden_states @ sw_up) @ sw_down
            y = y + p
            num = jnp.sum(y * p, -1)
            den = jnp.maximum(jnp.linalg.norm(y, axis=-1), EPS_COS) * jnp.maximum(jnp.linalg.norm(p, axis=-1), EPS_COS)
            closs = CONS_ALPHA * jnp.mean(num / den / (1.0 + COS_TEMP))
            return (y, aux_loss + closs)
        key = jax.random.key(seed)
        ks = jax.random.split(key, 12)
        sh = 1.0 / np.sqrt(H)
        sm = 1.0 / np.sqrt(M)
        ssm = 1.0 / np.sqrt(SM)
        sg = 1.0 / np.sqrt(G)
        return {'hidden_states': jax.random.normal(ks[0], (B, S, H), jnp.float32), 'g': jax.random.normal(ks[1], (B, G), jnp.float32), 'wt': jax.random.uniform(ks[2], (E, H), jnp.float32, -sh, sh), 'wg': jax.random.uniform(ks[3], (E, G), jnp.float32, -sg, sg), 'w_gate': jax.random.uniform(ks[4], (E, H, M), jnp.float32, -sh, sh), 'w_up': jax.random.uniform(ks[5], (E, H, M), jnp.float32, -sh, sh), 'w_down': jax.random.uniform(ks[6], (E, M, H), jnp.float32, -sm, sm), 'sw_gate': jax.random.uniform(ks[7], (H, SM), jnp.float32, -sh, sh), 'sw_up': jax.random.uniform(ks[8], (H, SM), jnp.float32, -sh, sh), 'sw_down': jax.random.uniform(ks[9], (SM, H), jnp.float32, -ssm, ssm)}
    _L2_cond_all = _L2_cond_setup()
    _L2_cond_in = {k: v for k, v in _L2_cond_all.items() if k in ('wt', 'wg', 'w_gate', 'w_up', 'w_down', 'sw_gate', 'sw_up', 'sw_down')}
    del _L2_cond_all

    def _L2_ffn_setup():
        import math
        import jax, jax.numpy as jnp
        import numpy as np
        B, S, D, F, E = (8, 512, 256, 1024, 8)
        CAPACITY_FACTOR = 1.0
        key = jax.random.key(seed)
        k1, k2, k3, k4 = jax.random.split(key, 4)
        x = jax.random.normal(k1, (B, S, D), dtype=jnp.float32)
        Wr = jax.random.normal(k2, (D, E), dtype=jnp.float32) * (1.0 / math.sqrt(D))
        W1 = jax.random.normal(k3, (E, D, F), dtype=jnp.float32) * (1.0 / math.sqrt(D))
        W2 = jax.random.normal(k4, (E, F, D), dtype=jnp.float32) * (1.0 / math.sqrt(F))
        return {'x': x, 'Wr': Wr, 'W1': W1, 'W2': W2}
    _L2_ffn_all = _L2_ffn_setup()
    _L2_ffn_in = {k: v for k, v in _L2_ffn_all.items() if k in ('Wr', 'W1', 'W2')}
    del _L2_ffn_all

    def _L3_cond_setup():
        import jax, jax.numpy as jnp
        import numpy as np
        DIM = 256
        HEADS = 16
        DIM_HEAD = 64
        SCALE = 8.0

        def ln(x, g, eps=1e-05):
            mean = x.mean(axis=-1, keepdims=True)
            var = ((x - mean) ** 2).mean(axis=-1, keepdims=True)
            return (x - mean) * jax.lax.rsqrt(var + eps) * g

        def l2norm(t):
            n = jnp.maximum(jnp.linalg.norm(t, axis=-1, keepdims=True), 1e-12)
            return t / n

        def rel_pos_bias(n, w0, b0, g0, w1, b1, g1, w2, b2, dtype):
            pos = jnp.arange(-n + 1, n, dtype=dtype)[:, None]
            h = jax.nn.silu(ln(pos @ w0 + b0, g0))
            h = jax.nn.silu(ln(h @ w1 + b1, g1))
            h = h @ w2 + b2
            i = jnp.arange(n)
            idx = i[:, None] - i[None, :] + n - 1
            bias = h[idx]
            return jnp.transpose(bias, (2, 0, 1))
        key = jax.random.key(seed)
        ks = jax.random.split(key, 16)
        b, n = (2, 512)
        inner = HEADS * DIM_HEAD
        s = 0.02
        return {'x': jax.random.normal(ks[0], (b, n, DIM), jnp.float32), 'mask': jnp.ones((b, n), dtype=bool), 'g_norm': jnp.ones((DIM,), jnp.float32), 'Wq': jax.random.normal(ks[1], (DIM, inner), jnp.float32) * s, 'Wkv': jax.random.normal(ks[2], (DIM, 2 * DIM_HEAD), jnp.float32) * s, 'q_scale': jnp.ones((DIM_HEAD,), jnp.float32), 'k_scale': jnp.ones((DIM_HEAD,), jnp.float32), 'null_kv': jax.random.normal(ks[3], (2, DIM_HEAD), jnp.float32), 'null_attn_bias': jax.random.normal(ks[4], (HEADS,), jnp.float32), 'w0': jax.random.normal(ks[5], (1, DIM), jnp.float32) * s, 'b0': jnp.zeros((DIM,), jnp.float32), 'g0': jnp.ones((DIM,), jnp.float32), 'w1': jax.random.normal(ks[6], (DIM, DIM), jnp.float32) * s, 'b1': jnp.zeros((DIM,), jnp.float32), 'g1': jnp.ones((DIM,), jnp.float32), 'w2': jax.random.normal(ks[7], (DIM, HEADS), jnp.float32) * s, 'b2': jnp.zeros((HEADS,), jnp.float32), 'Wout': jax.random.normal(ks[8], (inner, DIM), jnp.float32) * s, 'g_out': jnp.ones((DIM,), jnp.float32)}
    _L3_cond_all = _L3_cond_setup()
    _L3_cond_in = {k: v for k, v in _L3_cond_all.items() if k in ('g_norm', 'Wq', 'Wkv', 'q_scale', 'k_scale', 'null_attn_bias', 'w0', 'b0', 'g0', 'w1', 'b1', 'g1', 'w2', 'b2', 'Wout', 'g_out')}
    del _L3_cond_all

    def _L3_ffn_setup():
        import jax, jax.numpy as jnp
        import numpy as np
        E, K, D, H = (8, 2, 256, 512)
        B, S = (1, 256)

        def _grouped_swiglu(x_sorted, counts, w1, w2, w3):
            if hasattr(jax.lax, 'ragged_dot'):
                gs = counts.astype(jnp.int32)
                h = jax.nn.silu(jax.lax.ragged_dot(x_sorted, w1, gs)) * jax.lax.ragged_dot(x_sorted, w3, gs)
                return jax.lax.ragged_dot(h, w2, gs)
            pos = jnp.arange(x_sorted.shape[0])
            eid = jnp.searchsorted(jnp.cumsum(counts), pos, side='right')
            out = jnp.zeros((x_sorted.shape[0], w2.shape[-1]), x_sorted.dtype)
            for e in range(w1.shape[0]):
                xm = jnp.where((eid == e)[:, None], x_sorted, 0.0)
                he = jax.nn.silu(xm @ w1[e]) * (xm @ w3[e])
                out = out + he @ w2[e]
            return out
        key = jax.random.key(seed)
        k0, k1, k2, k3, k4 = jax.random.split(key, 5)
        sD = 1.0 / np.sqrt(D)
        sH = 1.0 / np.sqrt(H)
        return {'hidden_states': jax.random.normal(k0, (B, S, D), jnp.float32), 'gate_w': jax.random.normal(k1, (E, D), jnp.float32) * sD, 'w1': jax.random.normal(k2, (E, D, H), jnp.float32) * sD, 'w2': jax.random.normal(k3, (E, H, D), jnp.float32) * sH, 'w3': jax.random.normal(k4, (E, D, H), jnp.float32) * sD}
    _L3_ffn_all = _L3_ffn_setup()
    _L3_ffn_in = {k: v for k, v in _L3_ffn_all.items() if k in ('gate_w', 'w1', 'w2', 'w3')}
    del _L3_ffn_all
    return {'x': x, 'fside_16xSxS_0': fside_16xSxS_0, 'cond_64': cond_64, 'mask_BxS_bk0': mask_BxS_bk0, 'mask_BxS_bf1': mask_BxS_bf1, 'L0_cond_g_in': _L0_cond_in['g_in'], 'L0_cond_null_attn_bias': _L0_cond_in['null_attn_bias'], 'L0_cond_Wq': _L0_cond_in['Wq'], 'L0_cond_Wkv': _L0_cond_in['Wkv'], 'L0_cond_Wo': _L0_cond_in['Wo'], 'L0_cond_g_out': _L0_cond_in['g_out'], 'L0_ffn_weight': _L0_ffn_in['weight'], 'L1_cond_g_norm': _L1_cond_in['g_norm'], 'L1_cond_Wq': _L1_cond_in['Wq'], 'L1_cond_Wkv': _L1_cond_in['Wkv'], 'L1_cond_q_scale': _L1_cond_in['q_scale'], 'L1_cond_k_scale': _L1_cond_in['k_scale'], 'L1_cond_null_attn_bias': _L1_cond_in['null_attn_bias'], 'L1_cond_w0': _L1_cond_in['w0'], 'L1_cond_b0': _L1_cond_in['b0'], 'L1_cond_g0': _L1_cond_in['g0'], 'L1_cond_w1': _L1_cond_in['w1'], 'L1_cond_b1': _L1_cond_in['b1'], 'L1_cond_g1': _L1_cond_in['g1'], 'L1_cond_w2': _L1_cond_in['w2'], 'L1_cond_b2': _L1_cond_in['b2'], 'L1_cond_Wout': _L1_cond_in['Wout'], 'L1_cond_g_out': _L1_cond_in['g_out'], 'L1_ffn_w_router': _L1_ffn_in['w_router'], 'L1_ffn_w1': _L1_ffn_in['w1'], 'L1_ffn_w2': _L1_ffn_in['w2'], 'L1_ffn_bias': _L1_ffn_in['bias'], 'L2_cond_wt': _L2_cond_in['wt'], 'L2_cond_wg': _L2_cond_in['wg'], 'L2_cond_w_gate': _L2_cond_in['w_gate'], 'L2_cond_w_up': _L2_cond_in['w_up'], 'L2_cond_w_down': _L2_cond_in['w_down'], 'L2_cond_sw_gate': _L2_cond_in['sw_gate'], 'L2_cond_sw_up': _L2_cond_in['sw_up'], 'L2_cond_sw_down': _L2_cond_in['sw_down'], 'L2_ffn_Wr': _L2_ffn_in['Wr'], 'L2_ffn_W1': _L2_ffn_in['W1'], 'L2_ffn_W2': _L2_ffn_in['W2'], 'L3_cond_g_norm': _L3_cond_in['g_norm'], 'L3_cond_Wq': _L3_cond_in['Wq'], 'L3_cond_Wkv': _L3_cond_in['Wkv'], 'L3_cond_q_scale': _L3_cond_in['q_scale'], 'L3_cond_k_scale': _L3_cond_in['k_scale'], 'L3_cond_null_attn_bias': _L3_cond_in['null_attn_bias'], 'L3_cond_w0': _L3_cond_in['w0'], 'L3_cond_b0': _L3_cond_in['b0'], 'L3_cond_g0': _L3_cond_in['g0'], 'L3_cond_w1': _L3_cond_in['w1'], 'L3_cond_b1': _L3_cond_in['b1'], 'L3_cond_g1': _L3_cond_in['g1'], 'L3_cond_w2': _L3_cond_in['w2'], 'L3_cond_b2': _L3_cond_in['b2'], 'L3_cond_Wout': _L3_cond_in['Wout'], 'L3_cond_g_out': _L3_cond_in['g_out'], 'L3_ffn_gate_w': _L3_ffn_in['gate_w'], 'L3_ffn_w1': _L3_ffn_in['w1'], 'L3_ffn_w2': _L3_ffn_in['w2'], 'L3_ffn_w3': _L3_ffn_in['w3']}

def reference(x, fside_16xSxS_0, cond_64, mask_BxS_bk0, mask_BxS_bf1, L0_cond_g_in, L0_cond_null_attn_bias, L0_cond_Wq, L0_cond_Wkv, L0_cond_Wo, L0_cond_g_out, L0_ffn_weight, L1_cond_g_norm, L1_cond_Wq, L1_cond_Wkv, L1_cond_q_scale, L1_cond_k_scale, L1_cond_null_attn_bias, L1_cond_w0, L1_cond_b0, L1_cond_g0, L1_cond_w1, L1_cond_b1, L1_cond_g1, L1_cond_w2, L1_cond_b2, L1_cond_Wout, L1_cond_g_out, L1_ffn_w_router, L1_ffn_w1, L1_ffn_w2, L1_ffn_bias, L2_cond_wt, L2_cond_wg, L2_cond_w_gate, L2_cond_w_up, L2_cond_w_down, L2_cond_sw_gate, L2_cond_sw_up, L2_cond_sw_down, L2_ffn_Wr, L2_ffn_W1, L2_ffn_W2, L3_cond_g_norm, L3_cond_Wq, L3_cond_Wkv, L3_cond_q_scale, L3_cond_k_scale, L3_cond_null_attn_bias, L3_cond_w0, L3_cond_b0, L3_cond_g0, L3_cond_w1, L3_cond_b1, L3_cond_g1, L3_cond_w2, L3_cond_b2, L3_cond_Wout, L3_cond_g_out, L3_ffn_gate_w, L3_ffn_w1, L3_ffn_w2, L3_ffn_w3):
    import jax
    import jax.numpy as jnp

    def _L0_cond_ref(x, attn_bias, mask, g_in, null_attn_bias, null_kv, Wq, Wkv, Wo, g_out):
        import jax, jax.numpy as jnp
        import numpy as np
        B, N, DIM, H, DH = (2, 512, 256, 16, 64)
        INNER = H * DH
        EPS = 1e-05

        def layernorm(x, g):
            mean = jnp.mean(x, axis=-1, keepdims=True)
            var = jnp.var(x, axis=-1, keepdims=True)
            return (x - mean) * jax.lax.rsqrt(var + EPS) * g
        b, n, _ = x.shape
        scale = DH ** (-0.5)
        xn = layernorm(x, g_in)
        q = (xn @ Wq).reshape(b, n, H, DH).transpose(0, 2, 1, 3) * scale
        kv = xn @ Wkv
        k, v = (kv[..., :DH], kv[..., DH:])
        nk = jnp.broadcast_to(null_kv[0], (b, 1, DH))
        nv = jnp.broadcast_to(null_kv[1], (b, 1, DH))
        k = jnp.concatenate([nk, k], axis=1)
        v = jnp.concatenate([nv, v], axis=1)
        sim = jnp.einsum('bhid,bjd->bhij', q, k)
        null_col = jnp.broadcast_to(null_attn_bias[:, None, None], (H, n, 1))
        bias = jnp.concatenate([null_col, attn_bias], axis=-1)
        sim = sim + bias
        neg = -jnp.finfo(sim.dtype).max
        j = n + 1
        causal_mask = jnp.triu(jnp.ones((n, j), dtype=bool), k=j - n + 1)
        sim = jnp.where(causal_mask, neg, sim)
        mask_p = jnp.pad(mask, ((0, 0), (1, 0)), constant_values=True)
        sim = jnp.where(mask_p[:, None, None, :], sim, neg)
        attn = jax.nn.softmax(sim, axis=-1)
        out = jnp.einsum('bhij,bjd->bhid', attn, v)
        out = out.transpose(0, 2, 1, 3).reshape(b, n, INNER)
        out = out @ Wo
        return layernorm(out, g_out)

    def _L0_ffn_ref(x, weight):
        import jax, jax.numpy as jnp
        import numpy as np
        EPS = 1e-05

        @jax.custom_vjp
        def ste_quantize(w):
            scale = jnp.maximum(jnp.mean(jnp.abs(w)), EPS)
            return jnp.clip(jnp.round(w / scale), -1.0, 1.0)

        def _ste_fwd(w):
            return (ste_quantize(w), None)

        def _ste_bwd(_, g):
            return (g,)
        ste_quantize.defvjp(_ste_fwd, _ste_bwd)
        w_ternary = ste_quantize(weight)
        scale = jnp.maximum(jnp.mean(jnp.abs(weight)), EPS)
        return jnp.einsum('bsi,oi->bso', x, w_ternary * scale)

    def _L1_cond_ref(x, mask, g_norm, Wq, Wkv, q_scale, k_scale, null_kv, null_attn_bias, w0, b0, g0, w1, b1, g1, w2, b2, Wout, g_out):
        import jax, jax.numpy as jnp
        import numpy as np
        DIM = 256
        HEADS = 16
        DIM_HEAD = 64
        SCALE = 8.0

        def ln(x, g, eps=1e-05):
            mean = x.mean(axis=-1, keepdims=True)
            var = ((x - mean) ** 2).mean(axis=-1, keepdims=True)
            return (x - mean) * jax.lax.rsqrt(var + eps) * g

        def l2norm(t):
            n = jnp.maximum(jnp.linalg.norm(t, axis=-1, keepdims=True), 1e-12)
            return t / n

        def rel_pos_bias(n, w0, b0, g0, w1, b1, g1, w2, b2, dtype):
            pos = jnp.arange(-n + 1, n, dtype=dtype)[:, None]
            h = jax.nn.silu(ln(pos @ w0 + b0, g0))
            h = jax.nn.silu(ln(h @ w1 + b1, g1))
            h = h @ w2 + b2
            i = jnp.arange(n)
            idx = i[:, None] - i[None, :] + n - 1
            bias = h[idx]
            return jnp.transpose(bias, (2, 0, 1))
        b, n, _ = x.shape
        xn = ln(x, g_norm)
        q = (xn @ Wq).reshape(b, n, HEADS, DIM_HEAD).transpose(0, 2, 1, 3)
        kv = xn @ Wkv
        k, v = (kv[..., :DIM_HEAD], kv[..., DIM_HEAD:])
        nk = jnp.broadcast_to(null_kv[0], (b, 1, DIM_HEAD))
        nv = jnp.broadcast_to(null_kv[1], (b, 1, DIM_HEAD))
        k = jnp.concatenate([nk, k], axis=1)
        v = jnp.concatenate([nv, v], axis=1)
        q = l2norm(q) * q_scale
        k = l2norm(k) * k_scale
        sim = jnp.einsum('bhid,bjd->bhij', q, k) * SCALE
        bias = rel_pos_bias(n, w0, b0, g0, w1, b1, g1, w2, b2, q.dtype)
        null_bias = jnp.broadcast_to(null_attn_bias[:, None, None], (HEADS, n, 1))
        attn_bias = jnp.concatenate([null_bias, bias], axis=-1)
        sim = sim + attn_bias
        neg = -jnp.finfo(sim.dtype).max
        causal = jnp.triu(jnp.ones((n, n + 1), dtype=bool), k=2)
        sim = jnp.where(causal, neg, sim)
        m = jnp.pad(mask, ((0, 0), (1, 0)), constant_values=True)[:, None, None, :]
        sim = jnp.where(m, sim, neg)
        attn = jax.nn.softmax(sim, axis=-1)
        out = jnp.einsum('bhij,bjd->bhid', attn, v)
        out = out.transpose(0, 2, 1, 3).reshape(b, n, HEADS * DIM_HEAD)
        return ln(out @ Wout, g_out)

    def _L1_ffn_ref(x, w_router, w1, w2, bias):
        import jax, jax.numpy as jnp
        import numpy as np
        TOP_K = 2
        CAPACITY_FACTOR = 1.0
        sl, bs, hs = x.shape
        E = w_router.shape[1]
        xf = x.reshape(-1, hs)
        T = xf.shape[0]
        capacity = int(CAPACITY_FACTOR * TOP_K * T / E)
        scores = jax.nn.softmax(xf @ w_router, axis=-1)
        expert_weights, top_experts = jax.lax.top_k(scores, TOP_K)
        flat_e = top_experts.reshape(-1)
        flat_w = expert_weights.reshape(-1)
        N = flat_e.shape[0]
        order = jnp.argsort(flat_e, stable=True)
        bin_ids = flat_e[order]
        tpe = jnp.zeros((E,), jnp.int32).at[flat_e].add(1)
        starts = jnp.cumsum(tpe) - tpe
        offsets = jnp.arange(N) - starts[bin_ids]
        valid = offsets < capacity
        slot = jnp.where(valid, bin_ids * capacity + offsets, E * capacity)
        src = order // TOP_K
        xb = jnp.zeros((E * capacity + 1, hs), x.dtype).at[slot].set(xf[src])
        xb = xb[:-1].reshape(E, capacity, hs)
        h = jax.nn.gelu(jnp.einsum('ech,ehf->ecf', xb, w1))
        y = jnp.einsum('ecf,efh->ech', h, w2).reshape(E * capacity, hs)
        yv = jnp.where(valid[:, None], y[jnp.minimum(slot, E * capacity - 1)], 0.0)
        out = jnp.zeros((T, hs), x.dtype).at[src].add(flat_w[order][:, None] * yv)
        return out.reshape(sl, bs, hs) + bias

    def _L2_cond_ref(hidden_states, g, wt, wg, w_gate, w_up, w_down, sw_gate, sw_up, sw_down):
        import jax, jax.numpy as jnp
        import numpy as np
        B, S, H = (4, 512, 256)
        E = 8
        M = 128
        K = 2
        N_SHARED = 2
        SM = M * N_SHARED
        G = 64
        GE_TEMP = 1.0
        ALPHA = 0.001
        SEQ_AUX = True
        NORM_TOPK = True
        COS_TEMP = 0.78
        CONS_ALPHA = 0.01
        LEAKY_SLOPE = 0.01
        EPS_COS = 1e-08

        def _leaky(x):
            return jnp.where(x >= 0, x, LEAKY_SLOPE * x)

        def _moe_forward(hidden_states, g, wt, wg, w_gate, w_up, w_down, sw_gate, sw_up, sw_down):
            b, s, h = hidden_states.shape
            x = hidden_states.reshape(-1, h)
            T = x.shape[0]
            logits_h = x @ wt.T
            logits_g = g @ wg.T
            logits_g = jnp.repeat(logits_g, s, axis=0)
            logits = (logits_h + logits_g / GE_TEMP) / (1.0 + 1.0 / GE_TEMP)
            scores = jax.nn.softmax(logits, axis=-1)
            topk_w, topk_idx = jax.lax.top_k(scores, K)
            if K > 1 and NORM_TOPK:
                topk_w = topk_w / (topk_w.sum(-1, keepdims=True) + 1e-20)
            onehot = jax.nn.one_hot(topk_idx.reshape(b, s * K), E, dtype=jnp.float32)
            ce = onehot.sum(1) / (s * K / E)
            aux_loss = (ce * scores.reshape(b, s, E).mean(1)).sum(1).mean() * ALPHA
            gp = _leaky(jnp.einsum('th,ehm->etm', x, w_gate))
            up = jnp.einsum('th,ehm->etm', x, w_up)
            y_all = jnp.einsum('etm,emh->eth', gp * up, w_down)
            y_sel = y_all[topk_idx, jnp.arange(T)[:, None], :]
            y = (y_sel * topk_w[..., None]).sum(1).reshape(b, s, h)
            p = _leaky(hidden_states @ sw_gate) * (hidden_states @ sw_up) @ sw_down
            y = y + p
            num = jnp.sum(y * p, -1)
            den = jnp.maximum(jnp.linalg.norm(y, axis=-1), EPS_COS) * jnp.maximum(jnp.linalg.norm(p, axis=-1), EPS_COS)
            closs = CONS_ALPHA * jnp.mean(num / den / (1.0 + COS_TEMP))
            return (y, aux_loss + closs)
        y, _ = _moe_forward(hidden_states, g, wt, wg, w_gate, w_up, w_down, sw_gate, sw_up, sw_down)
        return y

    def _L2_ffn_ref(x, Wr, W1, W2):
        import math
        import jax, jax.numpy as jnp
        import numpy as np
        B, S, D, F, E = (8, 512, 256, 1024, 8)
        CAPACITY_FACTOR = 1.0
        b, s, d = x.shape
        t = b * s
        cap = max(math.ceil(t * CAPACITY_FACTOR / E), 1)
        xf = x.reshape(t, d)
        probs = jax.nn.softmax(xf.astype(jnp.float32) @ Wr, axis=-1)
        eidx = jnp.argmax(probs, axis=-1)
        p_tok = jnp.take_along_axis(probs, eidx[:, None], axis=1)[:, 0]
        onehot = jax.nn.one_hot(eidx, E, dtype=jnp.int32)
        rank_all = jnp.cumsum(onehot, axis=0) - onehot
        rank = jnp.take_along_axis(rank_all, eidx[:, None], axis=1)[:, 0]
        keep = rank < cap
        slot = jnp.where(keep, rank, cap)
        dispatch = jnp.zeros((E, cap + 1), dtype=jnp.int32).at[eidx, slot].set(jnp.arange(t, dtype=jnp.int32))
        valid = jnp.zeros((E, cap + 1), dtype=bool).at[eidx, slot].set(keep)
        dispatch = dispatch[:, :cap]
        valid = valid[:, :cap]
        xe = xf[dispatch]
        h = jnp.maximum(jnp.einsum('ecd,edf->ecf', xe, W1), 0.0)
        ye = jnp.einsum('ecf,efd->ecd', h, W2)
        pe = p_tok[dispatch]
        ye = ye * (pe * valid.astype(ye.dtype))[:, :, None]
        y = jnp.zeros((t, d), dtype=x.dtype).at[dispatch.reshape(-1)].add(ye.reshape(E * cap, d).astype(x.dtype))
        return y.reshape(b, s, d)

    def _L3_cond_ref(x, mask, g_norm, Wq, Wkv, q_scale, k_scale, null_kv, null_attn_bias, w0, b0, g0, w1, b1, g1, w2, b2, Wout, g_out):
        import jax, jax.numpy as jnp
        import numpy as np
        DIM = 256
        HEADS = 16
        DIM_HEAD = 64
        SCALE = 8.0

        def ln(x, g, eps=1e-05):
            mean = x.mean(axis=-1, keepdims=True)
            var = ((x - mean) ** 2).mean(axis=-1, keepdims=True)
            return (x - mean) * jax.lax.rsqrt(var + eps) * g

        def l2norm(t):
            n = jnp.maximum(jnp.linalg.norm(t, axis=-1, keepdims=True), 1e-12)
            return t / n

        def rel_pos_bias(n, w0, b0, g0, w1, b1, g1, w2, b2, dtype):
            pos = jnp.arange(-n + 1, n, dtype=dtype)[:, None]
            h = jax.nn.silu(ln(pos @ w0 + b0, g0))
            h = jax.nn.silu(ln(h @ w1 + b1, g1))
            h = h @ w2 + b2
            i = jnp.arange(n)
            idx = i[:, None] - i[None, :] + n - 1
            bias = h[idx]
            return jnp.transpose(bias, (2, 0, 1))
        b, n, _ = x.shape
        xn = ln(x, g_norm)
        q = (xn @ Wq).reshape(b, n, HEADS, DIM_HEAD).transpose(0, 2, 1, 3)
        kv = xn @ Wkv
        k, v = (kv[..., :DIM_HEAD], kv[..., DIM_HEAD:])
        nk = jnp.broadcast_to(null_kv[0], (b, 1, DIM_HEAD))
        nv = jnp.broadcast_to(null_kv[1], (b, 1, DIM_HEAD))
        k = jnp.concatenate([nk, k], axis=1)
        v = jnp.concatenate([nv, v], axis=1)
        q = l2norm(q) * q_scale
        k = l2norm(k) * k_scale
        sim = jnp.einsum('bhid,bjd->bhij', q, k) * SCALE
        bias = rel_pos_bias(n, w0, b0, g0, w1, b1, g1, w2, b2, q.dtype)
        null_bias = jnp.broadcast_to(null_attn_bias[:, None, None], (HEADS, n, 1))
        attn_bias = jnp.concatenate([null_bias, bias], axis=-1)
        sim = sim + attn_bias
        neg = -jnp.finfo(sim.dtype).max
        causal = jnp.triu(jnp.ones((n, n + 1), dtype=bool), k=2)
        sim = jnp.where(causal, neg, sim)
        m = jnp.pad(mask, ((0, 0), (1, 0)), constant_values=True)[:, None, None, :]
        sim = jnp.where(m, sim, neg)
        attn = jax.nn.softmax(sim, axis=-1)
        out = jnp.einsum('bhij,bjd->bhid', attn, v)
        out = out.transpose(0, 2, 1, 3).reshape(b, n, HEADS * DIM_HEAD)
        return ln(out @ Wout, g_out)

    def _L3_ffn_ref(hidden_states, gate_w, w1, w2, w3):
        import jax, jax.numpy as jnp
        import numpy as np
        E, K, D, H = (8, 2, 256, 512)
        B, S = (1, 256)

        def _grouped_swiglu(x_sorted, counts, w1, w2, w3):
            if hasattr(jax.lax, 'ragged_dot'):
                gs = counts.astype(jnp.int32)
                h = jax.nn.silu(jax.lax.ragged_dot(x_sorted, w1, gs)) * jax.lax.ragged_dot(x_sorted, w3, gs)
                return jax.lax.ragged_dot(h, w2, gs)
            pos = jnp.arange(x_sorted.shape[0])
            eid = jnp.searchsorted(jnp.cumsum(counts), pos, side='right')
            out = jnp.zeros((x_sorted.shape[0], w2.shape[-1]), x_sorted.dtype)
            for e in range(w1.shape[0]):
                xm = jnp.where((eid == e)[:, None], x_sorted, 0.0)
                he = jax.nn.silu(xm @ w1[e]) * (xm @ w3[e])
                out = out + he @ w2[e]
            return out
        x = hidden_states.reshape(-1, D)
        N = x.shape[0]
        scores = jax.nn.softmax(x @ gate_w.T, axis=-1)
        top_scores, sel = jax.lax.top_k(scores, K)
        sel_flat = sel.T.reshape(-1)
        scores_flat = top_scores.T.reshape(-1)
        order = jnp.argsort(sel_flat, stable=True)
        tok_sorted = order % N
        scores_sorted = scores_flat[order]
        counts = jnp.bincount(sel_flat, length=E)
        x_sorted = x[tok_sorted]
        y = _grouped_swiglu(x_sorted, counts, w1, w2, w3)
        weighted = y * scores_sorted[:, None]
        out = jnp.zeros((N, D), x.dtype).at[tok_sorted].add(weighted)
        return out.reshape(hidden_states.shape)
    x = x + _L0_ffn_ref(_L0_cond_ref(x, fside_16xSxS_0, mask_BxS_bk0, L0_cond_g_in, L0_cond_null_attn_bias, cond_64, L0_cond_Wq, L0_cond_Wkv, L0_cond_Wo, L0_cond_g_out), L0_ffn_weight)
    x = x + _L1_ffn_ref(_L1_cond_ref(x, mask_BxS_bf1, L1_cond_g_norm, L1_cond_Wq, L1_cond_Wkv, L1_cond_q_scale, L1_cond_k_scale, cond_64, L1_cond_null_attn_bias, L1_cond_w0, L1_cond_b0, L1_cond_g0, L1_cond_w1, L1_cond_b1, L1_cond_g1, L1_cond_w2, L1_cond_b2, L1_cond_Wout, L1_cond_g_out), L1_ffn_w_router, L1_ffn_w1, L1_ffn_w2, L1_ffn_bias)
    x = x + _L2_ffn_ref(_L2_cond_ref(x, cond_64, L2_cond_wt, L2_cond_wg, L2_cond_w_gate, L2_cond_w_up, L2_cond_w_down, L2_cond_sw_gate, L2_cond_sw_up, L2_cond_sw_down), L2_ffn_Wr, L2_ffn_W1, L2_ffn_W2)
    x = x + _L3_ffn_ref(_L3_cond_ref(x, mask_BxS_bf1, L3_cond_g_norm, L3_cond_Wq, L3_cond_Wkv, L3_cond_q_scale, L3_cond_k_scale, cond_64, L3_cond_null_attn_bias, L3_cond_w0, L3_cond_b0, L3_cond_g0, L3_cond_w1, L3_cond_b1, L3_cond_g1, L3_cond_w2, L3_cond_b2, L3_cond_Wout, L3_cond_g_out), L3_ffn_gate_w, L3_ffn_w1, L3_ffn_w2, L3_ffn_w3)
    return x

_drawn_inputs = setup_inputs


def setup_inputs(seed=0):
    import zlib

    import numpy as np

    out = dict(_drawn_inputs(seed))
    spreads = {'L0_cond_g_in': (1.0, 0.6),
     'L0_cond_g_out': (1.0, 0.2),
     'L1_cond_g_norm': (1.0, 0.2),
     'L1_cond_q_scale': (1.0, 0.6),
     'L1_cond_k_scale': (1.0, 0.6),
     'L1_cond_b0': (0.0, 0.8),
     'L1_cond_g0': (1.0, 0.6),
     'L1_cond_b1': (0.0, 2.0),
     'L1_cond_g1': (1.0, 0.6),
     'L1_cond_b2': (0.0, 0.8),
     'L1_cond_g_out': (1.0, 0.552),
     'L1_ffn_bias': (0.0, 0.1),
     'L3_cond_g_norm': (1.0, 0.2),
     'L3_cond_q_scale': (1.0, 0.2),
     'L3_cond_k_scale': (1.0, 0.2),
     'L3_cond_b0': (0.0, 0.1),
     'L3_cond_g0': (1.0, 0.6),
     'L3_cond_b1': (0.0, 0.1),
     'L3_cond_g1': (1.0, 0.6),
     'L3_cond_b2': (0.0, 0.282),
     'L3_cond_g_out': (1.0, 0.2)}
    factors = {'L0_cond_Wq': 2.885, 'L1_cond_w0': 6.996, 'L1_cond_w1': 5.127, 'L1_cond_w2': 3.792}
    for name, (base, spread) in spreads.items():
        noise = np.random.default_rng([zlib.crc32(name.encode()), seed]).standard_normal(out[name].shape)
        drawn = base * np.exp(spread * noise) if base else spread * noise
        out[name] = jnp.asarray(drawn.astype(out[name].dtype))
    for name, factor in factors.items():
        out[name] = (out[name] * factor).astype(out[name].dtype)
    return out
```

```python
from contextlib import ExitStack

import concourse.bass as bass
from concourse import mybir

F32 = mybir.dt.float32
BF16 = mybir.dt.bfloat16
I32 = mybir.dt.int32
U8 = mybir.dt.uint8
ALU = mybir.AluOpType
ACT = mybir.ActivationFunctionType
AX = mybir.AxisListType
ds = bass.ds

P = 128
B, S, D = 4, 512, 256
T = B * S
NT = T // P
QT = S // P
KD = D // P
H, DH = 16, 64
HP = H // 2
E = 8
EPS = 1e-5
NEG = -1e30
REV = 640
NKEY = [1 + P * (q + 1) for q in range(QT)]


class Memory:

    cleared = []
    pool_dma_semaphores = {}

    def __init__(self, nc, stack, prefix):
        self.nc, self.stack, self.prefix = nc, stack, prefix
        self.semaphores = []
        stack.callback(self.release)

    def release(self):
        for semaphore in Memory.cleared:
            self.nc.release_semaphore(semaphore)
        for run in runs(self.semaphores):
            self.nc.gpsimd.sem_clear(run)
        Memory.cleared = self.semaphores

    def sb(self, name, shape, dt=F32):
        return self.stack.enter_context(self.nc.sbuf_tensor(f"{self.prefix}_{name}", shape, dt))

    def ps(self, name, shape, dt=F32):
        return self.stack.enter_context(self.nc.psum_tensor(f"{self.prefix}_{name}", shape, dt))

    def sem(self, name):
        self.semaphores.append(self.nc.alloc_semaphore(name=f"{self.prefix}_{name}"))
        return self.semaphores[-1]

    def start_at_one(self, *semaphores):
        for semaphore in semaphores:
            self.nc.gpsimd.sem_inc(semaphore, 1)
        self.nc.all_engine_barrier()

    def pool_dma_sem(self, name, dmas):
        kept = Memory.pool_dma_semaphores
        semaphore, value = kept.get(name) or (self.nc.alloc_semaphore(name=name), 0)
        kept[name] = semaphore, value + 16 * dmas
        return semaphore, value


def runs(semaphores):
    numbers = sorted(s.num for s in semaphores)
    starts = [n for n in numbers if n - 1 not in numbers]
    ends = [n + 1 for n in numbers if n + 1 not in numbers]
    return [range(a, b) for a, b in zip(starts, ends)]


def inverse_root(pool, c, value, op, constant, summed, n, ready):
    pool.tensor_scalar(value, value, constant, None, op).then_inc(summed, 1)
    pool.wait_ge(summed, n)
    pool.tensor_tensor(value, value, c.minus_half[0:value.shape[0], 0:1].to_broadcast(list(value.shape)), ALU.pow).then_inc(ready, 1)


def row(ap_1d, partitions=P):
    n = ap_1d.shape[0]
    return ap_1d.rearrange("(a n) -> a n", a=1).to_broadcast([partitions, n])


def make_constants(nc, c):
    with ExitStack() as stack:
        m = Memory(nc, stack, "const")
        filled = m.sem("filled")
        done = m.sem("done")
        block = stack.enter_context(nc.Block())

        @block.gpsimd
        def _(pool):
            pool.memset(c.ident[:], 0.0).then_inc(filled, 1)
            pool.memset(c.before[:], 1.0).then_inc(filled, 1)
            pool.memset(c.row0[:], 1.0).then_inc(filled, 1)
            pool.memset(c.ones_b[:], 1.0).then_inc(done, 1)
            pool.memset(c.ones_f[:], 1.0).then_inc(done, 1)
            pool.memset(c.minus_half[:], -0.5).then_inc(done, 1)
            pool.wait_ge(filled, 3)
            pool.affine_select(out=c.ident[:], in_=c.ident[:], compare_op=ALU.not_equal, fill=1.0, base=0,
                               pattern=[[-1, P]], channel_multiplier=1).then_inc(done, 1)
            pool.affine_select(out=c.before[:], in_=c.before[:], compare_op=ALU.is_gt, fill=0.0, base=0,
                               pattern=[[1, P]], channel_multiplier=-1).then_inc(done, 1)
            pool.affine_select(out=c.row0[:], in_=c.row0[:], compare_op=ALU.is_ge, fill=0.0, base=0,
                               pattern=[[0, P]], channel_multiplier=-1).then_inc(done, 1)
            pool.wait_ge(done, 6)


def relative_bias(nc, c, l, w, rev, band):
    with ExitStack() as stack:
        m = Memory(nc, stack, f"rel{l}")
        w0, b0, g0 = m.sb("w0", [P, D]), m.sb("b0", [P, D]), m.sb("g0", [P, D])
        b1, g1 = m.sb("b1", [P, D]), m.sb("g1", [P, D])
        w1, w2 = m.sb("w1", [P, KD, D]), m.sb("w2", [P, KD, H])
        b2 = m.sb("b2", [H, 1])
        dist_i, dist = m.sb("dist_i", [P, QT], I32), m.sb("dist", [P, QT])
        hid = m.sb("hid", [P, QT, D])
        act = m.sb("act", [P, QT, D])
        act_t = m.sb("act_t", [P, KD, S])
        stats, mv = m.sb("stats", [P, QT, 6]), m.sb("mv", [P, QT, 2])
        out_row = m.sb("out_row", [H, REV])
        t_ps = m.ps("t_ps", [P, KD, S])
        h_ps = m.ps("h_ps", [P, QT, D])
        o_ps = m.ps("o_ps", [P, S])
        loaded, dist_made, link_s = m.sem("loaded"), m.sem("dist_made"), m.sem("link")
        mv_ready, rooting, rstd_ready = m.sem("mv_ready"), m.sem("rooting"), m.sem("rstd_ready")
        pre_ready, act_ready, t_ready, t_copied = (m.sem(x) for x in ("pre_ready", "act_ready", "t_ready", "t_copied"))
        h_ready, o_ready, row_ready, stored = (m.sem(x) for x in ("h_ready", "o_ready", "row_ready", "stored"))
        block = stack.enter_context(nc.Block())

        @block.sync
        def _(sp):
            for dst, src in ((w0, w["w0"].rearrange("a n -> (a n)")), (b0, w["b0"]), (g0, w["g0"]), (b1, w["b1"]), (g1, w["g1"])):
                sp.dma_start(dst[:], row(src)).then_inc(loaded, 16)
            sp.dma_start(w1[:], w["w1"].rearrange("(k p) n -> p k n", p=P)).then_inc(loaded, 16)
            sp.dma_start(w2[:], w["w2"].rearrange("(k p) n -> p k n", p=P)).then_inc(loaded, 16)
            sp.dma_start(b2[:], w["b2"].rearrange("(n a) -> n a", a=1)).then_inc(loaded, 16)
            sp.wait_ge(row_ready, 2)
            sp.dma_start(rev, out_row[:]).then_inc(stored, 16)
            sp.wait_ge(stored, 16)
            sp.dma_start(band, bass.AP(tensor=rev.tensor, offset=P - 1, ap=[[REV, H], [-1, P], [1, S]])).then_inc(stored, 16)
            sp.wait_ge(stored, 32)

        @block.gpsimd
        def _(pool):
            pool.iota(dist_i[:], pattern=[[-P, QT]], base=S - 1, channel_multiplier=-1).then_inc(dist_made, 1)
            for n in range(2):
                pool.wait_ge(mv_ready, QT * (n + 1))
                inverse_root(pool, c, mv[:, :, 1], ALU.add, EPS, rooting, n + 1, rstd_ready)

        @block.vector
        def _(dve):
            linked, rooted = [0], [0]

            def link(ins):
                linked[0] += 1
                ins.then_inc(link_s, 1)
                dve.wait_ge(link_s, linked[0])

            def normed(g):
                for t in range(QT):
                    nc.vector.bn_stats(stats[:, t, :], hid[:, t, :]).then_inc(link_s, 1)
                linked[0] += QT
                dve.wait_ge(link_s, linked[0])
                for t in range(QT):
                    nc.vector.bn_aggr(mv[:, t, :], stats[:, t, :]).then_inc(mv_ready, 1)
                rooted[0] += 1
                dve.wait_ge(rstd_ready, rooted[0])
                for t in range(QT):
                    nc.vector.tensor_scalar(hid[:, t, :], hid[:, t, :], mv[:, t, 0:1], mv[:, t, 1:2],
                                            ALU.subtract, ALU.mult).then_inc(link_s, 1)
                linked[0] += QT
                dve.wait_ge(link_s, linked[0])
                nc.vector.tensor_tensor(hid[:], hid[:], g[:].unsqueeze(1).to_broadcast([P, QT, D]), ALU.mult).then_inc(pre_ready, 1)

            dve.wait_ge(dist_made, 1)
            link(nc.vector.tensor_copy(dist[:], dist_i[:]))
            dve.wait_ge(loaded, 16 * 8)
            for t in range(QT):
                nc.vector.scalar_tensor_tensor(out=hid[:, t, :], in0=w0[:], scalar=dist[:, t:t + 1], in1=b0[:],
                                               op0=ALU.mult, op1=ALU.add).then_inc(link_s, 1)
            linked[0] += QT
            dve.wait_ge(link_s, linked[0])
            normed(g0)
            for k in range(KD):
                dve.wait_ge(t_ready, 1)
                nc.vector.tensor_copy(act_t[:, k, :], t_ps[:, k, :]).then_inc(t_copied, 1)
            dve.wait_ge(h_ready, 1)
            dve.wait_ge(act_ready, 1)
            link(nc.vector.tensor_tensor(hid[:], h_ps[:], b1[:].unsqueeze(1).to_broadcast([P, QT, D]), ALU.add))
            normed(g1)
            dve.wait_ge(t_ready, 2)
            for k in range(KD):
                nc.vector.tensor_copy(act_t[:, k, :], t_ps[:, k, :]).then_inc(t_copied, 1)
            nc.vector.memset(out_row[:, S:REV], NEG).then_inc(row_ready, 1)
            dve.wait_ge(o_ready, 1)
            nc.vector.tensor_scalar(out_row[:, 0:S], o_ps[0:H, :], b2[:, 0:1], None, ALU.add).then_inc(row_ready, 1)

        @block.scalar
        def _(a):
            for n in range(2):
                a.wait_ge(pre_ready, n + 1)
                if n:
                    a.wait_ge(t_ready, n)
                nc.scalar.activation(act[:], hid[:], ACT.Silu).then_inc(act_ready, 1)

        @block.tensor
        def _(pe):
            for n in range(2):
                pe.wait_ge(act_ready, n + 1)
                if n:
                    pe.wait_ge(t_copied, KD)
                for k in range(KD):
                    for t in range(QT):
                        last = nc.tensor.transpose(t_ps[:, k, t * P:(t + 1) * P], act[:, t, k * P:(k + 1) * P], c.ident[:])
                last.then_inc(t_ready, 1)
                pe.wait_ge(t_copied, KD * (n + 1))
                if n == 0:
                    pe.wait_ge(loaded, 16 * 8)
                    for t in range(QT):
                        for k in range(KD):
                            last = nc.tensor.matmul(h_ps[:, t, :], act_t[:, k, t * P:(t + 1) * P], w1[:, k, :],
                                                    start=(k == 0), stop=(k == KD - 1))
                    last.then_inc(h_ready, 1)
                else:
                    for k in range(KD):
                        last = nc.tensor.matmul(o_ps[0:H, :], w2[:, k, :], act_t[:, k, :], start=(k == 0), stop=(k == KD - 1))
                    last.then_inc(o_ready, 1)


def attention_inputs(nc, c, l, w, cond, mask, x_in=None):
    cosine = l != 0
    with ExitStack() as stack:
        m = Memory(nc, stack, f"in{l}")
        g = m.sb("g", [P, KD])
        wkv = m.sb("wkv", [P, KD, 2 * DH])
        mask_w = m.sb("mask_w", [1, T // 4], mybir.dt.uint32)
        mask_u = mask_w[:].bitcast(U8)
        null_k = m.sb("null_k", [1, DH])
        qs, ks = m.sb("qs", [P, DH]), m.sb("ks", [P, DH])
        stats, mv = m.sb("stats", [P, QT, 6]), m.sb("mv", [P, QT, 2])
        xn = m.sb("xn", [P, 2, QT, D])
        kf, ksq, kn = m.sb("kf", [P, QT, DH]), m.sb("ksq", [P, QT, DH]), m.sb("kn", [P, QT])
        kdup = m.sb("kdup", [P, QT, 2, DH])
        nsq, nn, nkdup = m.sb("nsq", [1, DH]), m.sb("nn", [1, 1]), m.sb("nkdup", [1, 2, DH])
        x_ps = [m.ps(f"x_ps{n}", [P, KD, S]) for n in range(2)]
        kv_ps = m.ps("kv_ps", [P, QT, 2 * DH])
        kt_ps = m.ps("kt_ps", [P, S])
        nk_ps = m.ps("nk_ps", [P, 1])
        loaded, cleared, link_s = m.sem("loaded"), m.sem("cleared"), m.sem("link")
        x_loaded = [m.sem(f"x_loaded{b}") for b in range(B)]
        xn_ready, xt_ready, xt_copied = m.sem("xn_ready"), m.sem("xt_ready"), m.sem("xt_copied")
        kv_ready, kv_read, kdup_ready = m.sem("kv_ready"), m.sem("kv_read"), m.sem("kdup_ready")
        kt_ready, kt_copied, null_ready, nk_ready, nk_copied = (m.sem(s) for s in ("kt_ready", "kt_copied", "null_ready", "nk_ready", "nk_copied"))
        done, mv_ready, rooting, rstd_ready, square_ready, floored, root_ready = (m.sem(s) for s in ("done", "mv_ready", "rooting", "rstd_ready", "square_ready", "floored", "root_ready"))
        block = stack.enter_context(nc.Block())
        n_loads = 6 + (2 if cosine else 0)

        @block.sync
        def _(sp):
            if x_in is not None:
                for b in range(B):
                    sp.dma_start(c.x[:, QT * b:QT * (b + 1), :], x_in[b].rearrange("(t p) d -> p t d", p=P)).then_inc(x_loaded[b], 16)
            sp.dma_start(g[:], w["g"].rearrange("(k p) -> p k", p=P)).then_inc(loaded, 16)
            sp.dma_start(wkv[:], w["Wkv"].rearrange("(k p) n -> p k n", p=P)).then_inc(loaded, 16)
            sp.dma_start(mask_w[:], mask.rearrange("b s -> (b s)").rearrange("(a n) -> a n", a=1)).then_inc(loaded, 16)
            sp.dma_start(null_k[:], cond[0:1, :]).then_inc(loaded, 16)
            if cosine:
                sp.dma_start(qs[:], row(w["q_scale"])).then_inc(loaded, 16)
                sp.dma_start(ks[:], row(w["k_scale"])).then_inc(loaded, 16)
            sp.dma_start(c.null_bias[:], row(w["null_attn_bias"])).then_inc(loaded, 16)
            sp.dma_start(c.wq[:, :, 0:H * DH], w["Wq"].rearrange("(k p) n -> p k n", p=P)).then_inc(loaded, 16)

        @block.gpsimd
        def _(pool):
            pool.memset(c.kt[:], 0.0).then_inc(cleared, 1)
            pool.memset(c.kmask[:], 0.0).then_inc(cleared, 1)
            pool.memset(c.wq[:, :, H * DH:], 0.0).then_inc(done, 1)

            def root(n, t):
                pool.wait_ge(square_ready, n)
                inverse_root(pool, c, t[:], ALU.max, 1e-24, floored, n, root_ready)

            for b in range(B + 1):
                if b < B:
                    pool.wait_ge(mv_ready, QT * (b + 1))
                    inverse_root(pool, c, mv[:, :, 1], ALU.add, EPS, rooting, b + 1, rstd_ready)
                if cosine and b == 0:
                    root(1, nn)
                if cosine and b >= 1:
                    root(b + 1, kn)
            pool.wait_ge(done, 1)

        @block.vector
        def _(dve):
            linked = [0]

            def link(ins):
                linked[0] += 1
                ins.then_inc(link_s, 1)
                dve.wait_ge(link_s, linked[0])

            def null_and_mask():
                dve.wait_ge(loaded, 16 * n_loads)
                dve.wait_ge(cleared, 2)
                link(nc.vector.tensor_scalar(c.kmask[0:1, :, 1:], mask_u.rearrange("a (b s) -> a b s", b=B), 1.0, -NEG,
                                             ALU.subtract, ALU.mult))
                pair = null_k[:].unsqueeze(1).to_broadcast([1, 2, DH])
                if cosine:
                    link(nc.vector.scalar_tensor_tensor(out=ks[:], in0=qs[:], scalar=8.0, in1=ks[:], op0=ALU.mult, op1=ALU.mult))
                    link(nc.vector.tensor_tensor(nsq[:], null_k[:], null_k[:], ALU.mult))
                    nc.vector.tensor_reduce(nn[:], nsq[:], AX.X, ALU.add).then_inc(square_ready, 1)
                    dve.wait_ge(root_ready, 1)
                    link(nc.vector.tensor_scalar(null_k[:], null_k[:], nn[:, 0:1], None, ALU.mult))
                    nc.vector.tensor_tensor(nkdup[:], pair, ks[0:1, :].unsqueeze(1).to_broadcast([1, 2, DH]), ALU.mult).then_inc(null_ready, 1)
                else:
                    nc.vector.tensor_scalar(nkdup[:], pair, DH ** -0.5, None, ALU.mult).then_inc(null_ready, 1)

            def layernorm(b):
                tiles = c.x[:, QT * b:QT * (b + 1), :]
                if x_in is not None:
                    dve.wait_ge(x_loaded[b], 16)
                for t in range(QT):
                    nc.vector.bn_stats(stats[:, t, :], tiles[:, t, :]).then_inc(link_s, 1)
                linked[0] += QT
                dve.wait_ge(link_s, linked[0])
                for t in range(QT):
                    nc.vector.bn_aggr(mv[:, t, :], stats[:, t, :]).then_inc(mv_ready, 1)
                dve.wait_ge(rstd_ready, b + 1)
                if b >= 2:
                    dve.wait_ge(xt_ready, b - 1)
                for t in range(QT):
                    last = nc.vector.tensor_scalar(xn[:, b % 2, t, :], tiles[:, t, :], mv[:, t, 0:1], mv[:, t, 1:2],
                                                   ALU.subtract, ALU.mult)
                    last.then_inc(xn_ready, 1)

            def keys(b):
                dve.wait_ge(kv_ready, b + 1)
                nc.vector.tensor_copy(c.v[:, QT * b:QT * (b + 1), :], kv_ps[:, :, DH:]).then_inc(kv_read, 1)
                dve.wait_ge(kdup_ready, 2 * b)
                nc.vector.tensor_copy(kf[:], kv_ps[:, :, 0:DH]).then_inc(kv_read, 1)
                dve.wait_ge(kv_read, 2 * (b + 1))
                if cosine:
                    link(nc.vector.tensor_tensor(ksq[:], kf[:], kf[:], ALU.mult))
                    nc.vector.tensor_reduce(kn[:], ksq[:], AX.X, ALU.add).then_inc(square_ready, 1)
                    dve.wait_ge(root_ready, b + 2)
                    link(nc.vector.tensor_tensor(kf[:], kf[:], kn[:].unsqueeze(2).to_broadcast([P, QT, DH]), ALU.mult))
                if b >= 1:
                    dve.wait_ge(kt_ready, b)
                for n in range(2):
                    if cosine:
                        nc.vector.tensor_tensor(kdup[:, :, n, :], kf[:], ks[:].unsqueeze(1).to_broadcast([P, QT, DH]), ALU.mult).then_inc(kdup_ready, 1)
                    else:
                        nc.vector.tensor_scalar(kdup[:, :, n, :], kf[:], DH ** -0.5, None, ALU.mult).then_inc(kdup_ready, 1)

            layernorm(0)
            null_and_mask()
            for b in range(1, B + 1):
                if b < B:
                    layernorm(b)
                keys(b - 1)

        @block.scalar
        def _(a):
            a.wait_ge(loaded, 16 * n_loads)
            a.wait_ge(cleared, 2)
            for b in range(B + 2):
                if b < B:
                    a.wait_ge(xt_ready, b + 1)
                    for k in range(KD):
                        nc.scalar.activation(c.xt[:, k, S * b:S * (b + 1)], x_ps[b % 2][:, k, :], ACT.Copy,
                                             scale=g[:, k:k + 1]).then_inc(xt_copied, 1)
                if b == 1:
                    a.wait_ge(nk_ready, 1)
                    for n in range(2):
                        h = slice(DH * n, DH * (n + 1))
                        nc.scalar.activation(c.kt[h, n, :, 0], nk_ps[h, :].to_broadcast([DH, B]), ACT.Copy).then_inc(nk_copied, 1)
                if b >= 2:
                    a.wait_ge(kt_ready, b - 1)
                    for n in range(2):
                        h = slice(DH * n, DH * (n + 1))
                        nc.scalar.activation(c.kt[h, n, b - 2, 1:], kt_ps[h, :], ACT.Copy).then_inc(kt_copied, 1)
            a.wait_ge(kt_copied, 2 * B)
            a.wait_ge(nk_copied, 2)

        @block.tensor
        def _(pe):
            for b in range(B + 2):
                if b < B:
                    pe.wait_ge(xn_ready, QT * (b + 1))
                    if b >= 2:
                        pe.wait_ge(xt_copied, KD * (b - 1))
                    for k in range(KD):
                        for t in range(QT):
                            last = nc.tensor.transpose(x_ps[b % 2][:, k, t * P:(t + 1) * P], xn[:, b % 2, t, k * P:(k + 1) * P], c.ident[:])
                    last.then_inc(xt_ready, 1)
                if b == 1:
                    pe.wait_ge(null_ready, 1)
                    nc.tensor.matmul(nk_ps[:], nkdup[:].rearrange("a n d -> a (n d)"), c.ident[0:1, 0:1], start=True, stop=True).then_inc(nk_ready, 1)
                if 1 <= b <= B:
                    pe.wait_ge(xt_copied, KD * b)
                    if b == 1:
                        pe.wait_ge(loaded, 16 * n_loads)
                    else:
                        pe.wait_ge(kv_read, 2 * (b - 1))
                    for t in range(QT):
                        tok = slice(S * (b - 1) + t * P, S * (b - 1) + (t + 1) * P)
                        for k in range(KD):
                            last = nc.tensor.matmul(kv_ps[:, t, :], c.xt[:, k, tok], wkv[:, k, :], start=(k == 0), stop=(k == KD - 1))
                    last.then_inc(kv_ready, 1)
                if b >= 2:
                    pe.wait_ge(kdup_ready, 2 * (b - 1))
                    if b >= 3:
                        pe.wait_ge(kt_copied, 2 * (b - 2))
                    for t in range(QT):
                        last = nc.tensor.transpose(kt_ps[:, t * P:(t + 1) * P], kdup[:, t, :, :].rearrange("p n d -> p (n d)"), c.ident[:])
                    last.then_inc(kt_ready, 1)


def attention(nc, c, l, bias_of, causal_select):
    cosine = l != 0
    U = QT * B * 2
    SU = B * 2
    with ExitStack() as stack:
        m = Memory(nc, stack, f"att{l}")
        bias = [[m.sb(f"bias{hh}{q}", [P, NKEY[q]]) for q in range(QT)] for hh in range(2)]
        q_sb, sq = m.sb("q_sb", [P, B, 2, DH]), m.sb("sq", [P, B, 2, DH])
        qn = m.sb("qn", [P, B, 2])
        q_t = [m.sb(f"q_t{n}", [P, B, P]) for n in range(2)]
        sc = [m.sb(f"sc{n}", [P, NKEY[-1]]) for n in range(3)]
        pr = [m.sb(f"pr{n}", [P, NKEY[-1]]) for n in range(3)]
        pt = [m.sb(f"pt{n}", [P, S]) for n in range(4)]
        nmax, rsum = m.sb("nmax", [P, 2, SU]), m.sb("rsum", [P, 2, SU])
        pnull = m.sb("pnull", [P, 2, SU])
        rinv = m.sb("rinv", [P, 2, SU])
        rexp = m.sb("rexp", [P, B, 2, DH])
        rb_sb = m.sb("rb_sb", [P, B, P])
        s_ps = [m.ps(f"s_ps{n}", [P, 1024]) for n in range(2)]
        pt_ps = [m.ps(f"pt_ps{n}", [P, S]) for n in range(2)]
        o_ps = m.ps("o_ps", [P, B, P])
        q_ps = m.ps("q_ps", [P, B, P])
        bias_loaded = [[m.sem(f"bias_loaded{hh}{q}") for q in range(QT)] for hh in range(2)]
        names = ("bias_ready s_ready s_read p_ready pt_ready pt_copied_a pt_copied_v pv_done q_ready q_squared q_kept "
                 "qt_ready qt_copied rinv_ready rexp_ready rb_ready rb_copied out_ready null_kept null_out qn_summed qn_floored qn_ready").split()
        (bias_ready, s_ready, s_read, p_ready, pt_ready, pt_copied_a, pt_copied_v, pv_done, q_ready, q_squared, q_kept,
         qt_ready, qt_copied, rinv_ready, rexp_ready, rb_ready, rb_copied, out_ready, null_kept, null_out, qn_summed, qn_floored, qn_ready) = (m.sem(x) for x in names)
        m.start_at_one(s_read, p_ready, pt_ready, pt_copied_a, pt_copied_v, pv_done, rb_ready, rb_copied, out_ready, null_kept, null_out)
        block = stack.enter_context(nc.Block())
        units = [(u // SU, (u % SU) // 2, u % 2) for u in range(U)]

        def scores_ap(u, q):
            first = 512 - 257 if q == QT - 1 else 0
            return s_ps[u % 2][:, first:first + NKEY[q]]

        @block.sync
        def _(sp):
            def load(i, hh, q):
                sp.dma_start(bias[hh][q][:, 1:], bias_of(i, hh, q)).then_inc(bias_loaded[hh][q], 16)

            for q in range(QT):
                for hh in range(2):
                    load(0, hh, q)
            with sp.Fori(0, HP - 1) as i:
                for q in range(QT):
                    uses = sp.to_reg(i * U + SU * (q + 1) + 1)
                    sp.wait_ge(s_read, 1)
                    sp.wait_ge(s_read, uses)
                    for hh in range(2):
                        load(i + 1, hh, q)

        @block.gpsimd
        def _(pool):
            def finish_bias(i, q):
                for hh in range(2):
                    loads = pool.to_reg(i * 16 + 16)
                    pool.wait_ge(bias_loaded[hh][q], 16)
                    pool.wait_ge(bias_loaded[hh][q], loads)
                    if causal_select:
                        diag = bias[hh][q][:, 1 + P * q:1 + P * (q + 1)]
                        pool.affine_select(out=diag, in_=diag, compare_op=ALU.is_ge, fill=NEG, base=0,
                                           pattern=[[-1, P]], channel_multiplier=1).then_inc(bias_ready, 1)
                    pool.tensor_copy(bias[hh][q][:, 0:1], c.null_bias[:, ds(i * 2 + hh, 1)]).then_inc(bias_ready, 1)

            def root_q(n):
                if cosine:
                    sums, floors = pool.to_reg(n + 1), pool.to_reg(n + 1)
                    pool.wait_ge(p_ready, 1)
                    pool.wait_ge(qn_summed, sums)
                    inverse_root(pool, c, qn[:], ALU.max, 1e-24, qn_floored, n + 1, qn_ready)

            root_q(0)
            with pool.Fori(0, HP) as i:
                finish_bias(i, 0)
                for u, (q, b, hh) in enumerate(units):
                    if u % SU == 0:
                        pool.wait_ge(null_out, i * QT + q + 1)
                    if u % SU == 2 and q + 1 < QT:
                        finish_bias(i, q + 1)
                    if u % SU == 3:
                        root_q(i * QT + (q + 1))
                    made = pool.to_reg(i * U + u + 2)
                    pool.wait_ge(p_ready, 1)
                    pool.wait_ge(p_ready, made)
                    pool.tensor_copy(pnull[:, q % 2, u % SU:u % SU + 1], pr[u % 3][:, 0:1]).then_inc(null_kept, 1)
                    if u % SU == SU - 1:
                        pool.wait_ge(rinv_ready, i * QT + q + 1)
                        pool.wait_ge(null_kept, i * U + u + 1 + 1)
                        pool.tensor_tensor(c.p_null[:, :, q, ds(i * 2, 2)],
                                           pnull[:, q % 2, :].rearrange("p (b n) -> p b n", n=2),
                                           rinv[:, q % 2, :].rearrange("p (b n) -> p b n", n=2), ALU.mult).then_inc(null_out, 1)
            pool.wait_ge(null_out, HP * QT + 1)

        per_step_bias = 4 if causal_select else 2

        @block.vector
        def _(dve):
            def finish(i, q):
                dve.wait_ge(rb_copied, i * QT + q + 1 + 1)
                dve.wait_ge(pv_done, i * (U // 2) + B * (q + 1) + 1)
                nc.vector.tensor_tensor(c.out_t[:, ds(i, 1), :].rearrange("p a (b q s) -> p (a b) q s", b=B, q=QT)[:, :, q, :],
                                        o_ps[:], rb_sb[:], ALU.mult).then_inc(out_ready, 1)

            def keep_q(n, i=0):
                if not cosine:
                    return
                dve.wait_ge(q_squared, n + 1)
                nc.vector.tensor_reduce(qn[:], sq[:], AX.X, ALU.add).then_inc(qn_summed, 1)
                dve.wait_ge(qn_ready, n + 1)
                nc.vector.tensor_tensor(q_sb[:], q_ps[:].rearrange("p b (n d) -> p b n d", n=2),
                                        qn[:].unsqueeze(3).to_broadcast([P, B, 2, DH]), ALU.mult).then_inc(q_kept, 1)

            keep_q(0)
            with dve.Fori(0, HP) as i:
                for u in range(U + 5):
                    if u < U:
                        q, b, hh = units[u]
                        if u % SU == 0:
                            biases = dve.to_reg(i * (QT * per_step_bias) + per_step_bias * (q + 1))
                        scored, read = dve.to_reg(i * U + u + 1), dve.to_reg(i * U + max(u - 2, 0) + 1)
                        dve.wait_ge(s_ready, 1)
                        if u % SU == 0:
                            dve.wait_ge(bias_ready, biases)
                        dve.wait_ge(s_ready, scored)
                        dve.wait_ge(p_ready, read)
                        nc.vector.tensor_tensor_reduce(sc[u % 3][:, 0:NKEY[q]], scores_ap(u, q), bias[hh][q][:], -1.0, 3e38,
                                                       ALU.add, ALU.min, nmax[:, q % 2, u % SU:u % SU + 1]).then_inc(s_read, 1)
                    if u % SU == 3 and u < U:
                        keep_q(i * QT + (q + 1))
                    if u >= 2 and (u - 2) % SU == SU - 1:
                        qv = (u - 2) // SU
                        dve.wait_ge(p_ready, i * U + SU * (qv + 1) + 1)
                        dve.wait_ge(null_out, i * QT + qv + 1)
                        nc.vector.reciprocal(rinv[:, qv % 2, :], rsum[:, qv % 2, :]).then_inc(rinv_ready, 1)
                        dve.wait_ge(rinv_ready, i * QT + qv + 1)
                        dve.wait_ge(rb_ready, i * QT + qv + 1)
                        nc.vector.tensor_copy(rexp[:], rinv[:, qv % 2, :].rearrange("p (b n) -> p b n", n=2).unsqueeze(3)
                                              .to_broadcast([P, B, 2, DH])).then_inc(rexp_ready, 1)
                    if 3 <= u < U + 3 and (u - 3) % 2:
                        v = u - 3
                        n = P * (units[v][0] + 1)
                        dve.wait_ge(pt_ready, i * U + v + 1 + 1)
                        dve.wait_ge(pv_done, i * (U // 2) + max(v // 2 - 1, 0) + 1)
                        nc.vector.tensor_copy(pt[v % 4][:, 0:n], pt_ps[v % 2][:, 0:n]).then_inc(pt_copied_v, 1)
                    if u >= 12 and (u - 12) % SU == 0:
                        finish(i, (u - 12) // SU)

            dve.wait_ge(out_ready, HP * QT + 1)

        @block.scalar
        def _(a):
            def copy_rb(i, q):
                a.wait_ge(rb_ready, i * QT + q + 1 + 1)
                a.wait_ge(out_ready, i * QT + q + 1)
                nc.scalar.activation(rb_sb[:], q_ps[:], ACT.Copy).then_inc(rb_copied, 1)

            def take_q(n):
                a.wait_ge(q_ready, n + 1)
                if cosine:
                    nc.scalar.activation(sq[:], q_ps[:].rearrange("p b (n d) -> p b n d", n=2), ACT.Square).then_inc(q_squared, 1)
                else:
                    nc.scalar.activation(q_sb[:], q_ps[:].rearrange("p b (n d) -> p b n d", n=2), ACT.Copy).then_inc(q_kept, 1)

            def take_qt(n, half):
                a.wait_ge(qt_ready, n + 1)
                nc.scalar.activation(q_t[half][:], q_ps[:], ACT.Copy).then_inc(qt_copied, 1)

            take_q(0)
            take_qt(0, 0)
            with a.Fori(0, HP) as i:
                for u in range(U + 3):
                    if u < U:
                        q, b, hh = units[u]
                        a.wait_ge(s_read, i * U + u + 1 + 1)
                        a.wait_ge(null_kept, i * U + max(u - 2, 0) + 1)
                        a.wait_ge(pt_ready, i * U + max(u - 2, 0) + 1)
                        nc.scalar.activation(pr[u % 3][:, 0:NKEY[q]], sc[u % 3][:, 0:NKEY[q]], ACT.Exp, scale=-1.0,
                                             bias=nmax[:, q % 2, u % SU:u % SU + 1],
                                             accum_out=rsum[:, q % 2, u % SU:u % SU + 1]).then_inc(p_ready, 1)
                    if u % SU == 3 and u < U:
                        take_q(i * QT + (q + 1))
                    if u % SU == 6 and u < U:
                        take_qt(i * QT + (q + 1), (q + 1) % 2)
                    if u >= 3 and (u - 3) % 2 == 0:
                        v = u - 3
                        n = P * (units[v][0] + 1)
                        a.wait_ge(pt_ready, i * U + v + 1 + 1)
                        a.wait_ge(pv_done, i * (U // 2) + max(v // 2 - 1, 0) + 1)
                        nc.scalar.activation(pt[v % 4][:, 0:n], pt_ps[v % 2][:, 0:n], ACT.Copy).then_inc(pt_copied_a, 1)
                    if u >= 10 and (u - 10) % SU == 0:
                        copy_rb(i, (u - 10) // SU)

        @block.tensor
        def _(pe):
            def turn_r(i, q):
                pe.wait_ge(rexp_ready, i * QT + q + 1)
                pe.wait_ge(qt_copied, i * QT + q + 2)
                for b in range(B):
                    last = nc.tensor.transpose(q_ps[:, b, :], rexp[:, b, :, :].rearrange("p n d -> p (n d)"), c.ident[:])
                last.then_inc(rb_ready, 1)

            def project_q(i, q):
                for b in range(B):
                    tok = slice(S * b + P * q, S * b + P * (q + 1))
                    for k in range(KD):
                        last = nc.tensor.matmul(q_ps[:, b, :], c.xt[:, k, tok], c.wq[:, k, ds(i * P, P)], start=(k == 0), stop=(k == KD - 1))
                last.then_inc(q_ready, 1)

            def turn_q(n):
                pe.wait_ge(q_kept, n + 1)
                for b in range(B):
                    last = nc.tensor.transpose(q_ps[:, b, :], q_sb[:, b, :, :].rearrange("p n d -> p (n d)"), c.ident[:])
                last.then_inc(qt_ready, 1)

            project_q(0, 0)
            turn_q(0)
            with pe.Fori(0, HP) as i:
                for u in range(U + 5):
                    if u < U:
                        q, b, hh = units[u]
                        if u % SU == 0:
                            pe.wait_ge(qt_copied, i * QT + q + 1)
                        pe.wait_ge(s_read, i * U + max(u - 1, 0) + 1)
                        out = scores_ap(u, q)
                        cuts = [0, 257, NKEY[q]] if q == QT - 1 else [0, NKEY[q]]
                        for lo, hi in zip(cuts, cuts[1:]):
                            nc.tensor.matmul(out[:, lo:hi], c.row0[:], c.kmask[:, b, lo:hi], start=True, stop=False)
                            last = nc.tensor.matmul(out[:, lo:hi], q_t[q % 2][:, b, :], c.kt[:, hh, b, lo:hi], start=False, stop=True)
                        last.then_inc(s_ready, 1)
                    if u >= 2 and u - 2 < U:
                        v = u - 2
                        qv, bv, hv = units[v]
                        pe.wait_ge(p_ready, i * U + v + 1 + 1)
                        pe.wait_ge(pt_copied_v if v % 2 else pt_copied_a, i * (U // 2) + v // 2 + 1)
                        for kb in range(qv + 1):
                            last = nc.tensor.transpose(pt_ps[v % 2][:, P * kb:P * (kb + 1)], pr[v % 3][:, 1 + P * kb:1 + P * (kb + 1)], c.ident[:])
                        last.then_inc(pt_ready, 1)
                    if u >= 5 and u % 2:
                        v = u - 4
                        if v < U:
                            qv, bv, _ = units[v]
                            pe.wait_ge(pt_copied_a, i * (U // 2) + v // 2 + 1 + 1)
                            pe.wait_ge(pt_copied_v, i * (U // 2) + v // 2 + 1 + 1)
                            if v % SU == 1:
                                pe.wait_ge(out_ready, i * QT + qv + 1)
                            for kb in range(qv + 1):
                                for hv in range(2):
                                    last = nc.tensor.matmul(o_ps[DH * hv:DH * (hv + 1), bv, :], c.v[:, QT * bv + kb, :],
                                                            pt[(v - 1 + hv) % 4][:, P * kb:P * (kb + 1)], start=(kb == 0), stop=(kb == qv))
                            last.then_inc(pv_done, 1)
                    if u < U and u % SU == 3:
                        pe.wait_ge(rb_copied, i * QT + q + 1)
                        project_q(i + 1 if q == QT - 1 else i, (q + 1) % QT)
                    if u < U and u % SU == 5:
                        turn_q(i * QT + q + 1)
                    if u >= 10 and (u - 10) % SU == 0:
                        turn_r(i, (u - 10) // SU)


def attention_output(nc, c, l, w_out, g_out, cond):
    with ExitStack() as stack:
        m = Memory(nc, stack, f"out{l}")
        wo = m.sb("wo", [P, HP, D])
        g = m.sb("g", [P, D])
        null_v = m.sb("null_v", [P, 1])
        null_cols = m.sb("null_cols", [P, HP, H])
        null_w = m.sb("null_w", [H, D])
        pn_t = m.sb("pn_t", [H, 2, S])
        yn = m.sb("yn", [P, 2, QT, D])
        stats, mv = m.sb("stats", [P, QT, 6]), m.sb("mv", [P, QT, 2])
        y_ps = [m.ps(f"y_ps{n}", [P, QT, D]) for n in range(2)]
        pn_ps = m.ps("pn_ps", [P, S])
        nw_ps = m.ps("nw_ps", [P, D])
        loaded, cleared, cols_ready, nw_ready, nw_copied = (m.sem(x) for x in ("loaded", "cleared", "cols_ready", "nw_ready", "nw_copied"))
        pn_ready, pn_copied, y_ready, yn_ready, h_ready, link_s = (m.sem(x) for x in ("pn_ready", "pn_copied", "y_ready", "yn_ready", "h_ready", "link"))
        mv_ready, rooting, rstd_ready = m.sem("mv_ready"), m.sem("rooting"), m.sem("rstd_ready")
        block = stack.enter_context(nc.Block())

        @block.sync
        def _(sp):
            sp.dma_start(wo[:], w_out.rearrange("(c p) n -> p c n", p=P)).then_inc(loaded, 16)
            sp.dma_start(g[:], row(g_out)).then_inc(loaded, 16)
            for n in range(2):
                sp.dma_start(null_v[DH * n:DH * (n + 1), :], cond[1:2, :].rearrange("a d -> d a")).then_inc(loaded, 16)

        @block.gpsimd
        def _(pool):
            pool.memset(null_cols[:], 0.0).then_inc(cleared, 1)
            pool.wait_ge(loaded, 64)
            for b in range(B):
                pool.wait_ge(mv_ready, QT * (b + 1))
                inverse_root(pool, c, mv[:, :, 1], ALU.add, EPS, rooting, b + 1, rstd_ready)
                pool.wait_ge(yn_ready, QT * (b + 1))
                pool.tensor_tensor(c.h[:, QT * b:QT * (b + 1), :], yn[:, b % 2, :, :], g[:].unsqueeze(1).to_broadcast([P, QT, D]),
                                   ALU.mult).then_inc(h_ready, 1)
            pool.wait_ge(h_ready, B)

        @block.scalar
        def _(a):
            a.wait_ge(nw_ready, 1)
            nc.scalar.activation(null_w[:], nw_ps[0:H, :], ACT.Copy).then_inc(nw_copied, 1)
            for b in range(B):
                a.wait_ge(pn_ready, b + 1)
                if b >= 2:
                    a.wait_ge(y_ready, b - 1)
                nc.scalar.activation(pn_t[:, b % 2, :], pn_ps[0:H, :], ACT.Copy).then_inc(pn_copied, 1)

        @block.vector
        def _(dve):
            linked = [0]

            def link(ins):
                linked[0] += 1
                ins.then_inc(link_s, 1)
                dve.wait_ge(link_s, linked[0])

            dve.wait_ge(loaded, 64)
            dve.wait_ge(cleared, 1)
            flat = null_cols[:].rearrange("p c h -> p (c h)")
            for n in range(2):
                rows = slice(DH * n, DH * (n + 1))
                nc.vector.tensor_copy(flat[rows, n:n + (H + 2) * (HP - 1) + 1:H + 2], null_v[rows, :].to_broadcast([DH, HP])).then_inc(cols_ready, 1)
            for b in range(B):
                dve.wait_ge(y_ready, b + 1)
                for t in range(QT):
                    nc.vector.bn_stats(stats[:, t, :], y_ps[b % 2][:, t, :]).then_inc(link_s, 1)
                linked[0] += QT
                dve.wait_ge(link_s, linked[0])
                for t in range(QT):
                    nc.vector.bn_aggr(mv[:, t, :], stats[:, t, :]).then_inc(mv_ready, 1)
                dve.wait_ge(rstd_ready, b + 1)
                if b >= 2:
                    dve.wait_ge(h_ready, b - 1)
                for t in range(QT):
                    nc.vector.tensor_scalar(yn[:, b % 2, t, :], y_ps[b % 2][:, t, :], mv[:, t, 0:1], mv[:, t, 1:2],
                                            ALU.subtract, ALU.mult).then_inc(yn_ready, 1)

        @block.tensor
        def _(pe):
            pe.wait_ge(loaded, 64)
            pe.wait_ge(cols_ready, 2)
            for p in range(HP):
                last = nc.tensor.matmul(nw_ps[0:H, :], null_cols[:, p, :], wo[:, p, :], start=(p == 0), stop=(p == HP - 1))
            last.then_inc(nw_ready, 1)
            for b in range(B):
                if b >= 1:
                    pe.wait_ge(pn_copied, b)
                for q in range(QT):
                    last = nc.tensor.transpose(pn_ps[0:H, P * q:P * (q + 1)], c.p_null[:, b, q, :], c.ident[:])
                last.then_inc(pn_ready, 1)
                if b >= 2:
                    pe.wait_ge(yn_ready, QT * (b - 1))
                if b == 0:
                    pe.wait_ge(nw_copied, 1)
                pe.wait_ge(pn_copied, b + 1)
                for q in range(QT):
                    for p in range(HP):
                        nc.tensor.matmul(y_ps[b % 2][:, q, :], c.out_t[:, p, S * b + P * q:S * b + P * (q + 1)], wo[:, p, :],
                                         start=(p == 0), stop=False)
                    last = nc.tensor.matmul(y_ps[b % 2][:, q, :], pn_t[:, b % 2, P * q:P * (q + 1)], null_w[:], start=False, stop=True)
                last.then_inc(y_ready, 1)


def ternary_linear(nc, c, weight):
    with ExitStack() as stack:
        m = Memory(nc, stack, "ter")
        w = m.sb("w", [P, KD, D])
        w_t = m.sb("w_t", [P, KD, D])
        part, scale = m.sb("part", [P, 1]), m.sb("scale", [P, 1])
        h_t = m.sb("h_t", [P, 2, KD, S])
        s_ps = m.ps("s_ps", [P, 1])
        h_ps = m.ps("h_ps", [P, KD, S])
        y_ps = [m.ps(f"y_ps{n}", [P, QT, D]) for n in range(2)]
        names = "loaded part_ready sum_ready scale_ready w_ready wt_ready wt_copied ht_ready ht_copied y_ready x_ready link".split()
        (loaded, part_ready, sum_ready, scale_ready, w_ready, wt_ready, wt_copied, ht_ready, ht_copied, y_ready, x_ready, link_s) = (m.sem(x) for x in names)
        block = stack.enter_context(nc.Block())
        ROUND = 12582912.0

        @block.sync
        def _(sp):
            sp.dma_start(w[:], weight.rearrange("(k p) n -> p k n", p=P)).then_inc(loaded, 16)

        @block.vector
        def _(dve):
            linked = [0]

            def link(ins):
                linked[0] += 1
                ins.then_inc(link_s, 1)
                dve.wait_ge(link_s, linked[0])

            dve.wait_ge(loaded, 16)
            nc.vector.tensor_reduce(part[:], w[:], AX.XY, ALU.add, apply_absolute_value=True).then_inc(part_ready, 1)
            dve.wait_ge(sum_ready, 1)
            link(nc.vector.tensor_scalar(scale[:], s_ps[:], 1.0 / (D * D), EPS, ALU.mult, ALU.max))
            link(nc.vector.reciprocal(part[:], scale[:]))
            link(nc.vector.tensor_scalar(w[:], w[:], part[:, 0:1], ROUND, ALU.mult, ALU.add))
            link(nc.vector.tensor_scalar(w[:], w[:], ROUND, -1.0, ALU.subtract, ALU.max))
            nc.vector.tensor_scalar(w[:], w[:], 1.0, None, ALU.min).then_inc(w_ready, 1)
            for b in range(B):
                dve.wait_ge(y_ready, b + 1)
                nc.vector.scalar_tensor_tensor(out=c.x[:, QT * b:QT * (b + 1), :], in0=y_ps[b % 2][:], scalar=scale[:, 0:1],
                                               in1=c.x[:, QT * b:QT * (b + 1), :], op0=ALU.mult, op1=ALU.add).then_inc(x_ready, 1)
            dve.wait_ge(x_ready, B)

        @block.scalar
        def _(a):
            a.wait_ge(wt_ready, 1)
            for k in range(KD):
                nc.scalar.activation(w_t[:, k, :], h_ps[:, k, 0:D], ACT.Copy).then_inc(wt_copied, 1)
            for b in range(B):
                a.wait_ge(ht_ready, b + 1)
                if b >= 2:
                    a.wait_ge(y_ready, b - 1)
                for k in range(KD):
                    nc.scalar.activation(h_t[:, b % 2, k, :], h_ps[:, k, :], ACT.Copy).then_inc(ht_copied, 1)

        @block.tensor
        def _(pe):
            pe.wait_ge(part_ready, 1)
            nc.tensor.matmul(s_ps[:], c.ones_f[:], part[:], start=True, stop=True).then_inc(sum_ready, 1)
            pe.wait_ge(w_ready, 1)
            for k in range(KD):
                for o in range(KD):
                    last = nc.tensor.transpose(h_ps[:, k, P * o:P * (o + 1)], w[:, o, P * k:P * (k + 1)], c.ident[:])
            last.then_inc(wt_ready, 1)
            pe.wait_ge(wt_copied, KD)
            for b in range(B):
                if b >= 1:
                    pe.wait_ge(ht_copied, KD * b)
                for k in range(KD):
                    for t in range(QT):
                        last = nc.tensor.transpose(h_ps[:, k, P * t:P * (t + 1)], c.h[:, QT * b + t, P * k:P * (k + 1)], c.ident[:])
                last.then_inc(ht_ready, 1)
                pe.wait_ge(ht_copied, KD * (b + 1))
                if b >= 2:
                    pe.wait_ge(x_ready, b - 1)
                for t in range(QT):
                    for k in range(KD):
                        last = nc.tensor.matmul(y_ps[b % 2][:, t, :], h_t[:, b % 2, k, P * t:P * (t + 1)], w_t[:, k, :],
                                                start=(k == 0), stop=(k == KD - 1))
                last.then_inc(y_ready, 1)


class Shared:
    pass


def shared(nc, stack):
    c = Shared()
    m = Memory(nc, stack, "all")
    c.ident, c.ones_f, c.minus_half = m.sb("ident", [P, P]), m.sb("ones_f", [P, P]), m.sb("minus_half", [P, 1])
    c.before, c.row0, c.ones_b = m.sb("before", [P, P], BF16), m.sb("row0", [P, P], BF16), m.sb("ones_b", [P, P], BF16)
    c.x, c.h = m.sb("x", [P, NT, D]), m.sb("h", [P, NT, D])
    c.xt = m.sb("xt", [P, KD, T])
    return c


def attention_memory(nc, stack, c, l):
    m = Memory(nc, stack, f"mem{l}")
    c.kt = m.sb("kt", [P, 2, B, NKEY[-1]])
    c.v = m.sb("v", [P, NT, DH])
    c.wq = m.sb("wq", [P, KD, (HP + 1) * P])
    c.kmask = m.sb("kmask", [P, B, NKEY[-1]], BF16)
    c.null_bias = m.sb("null_bias", [P, H])
    c.p_null = m.sb("p_null", [P, B, QT, H])
    c.out_t = m.sb("out_t", [P, HP, T])


def band_bias(band):
    def bias_of(i, hh, q):
        return band[ds(i * 2 + hh, 1), :, P * (QT - 1 - q):S].rearrange("a p n -> (a p) n")
    return bias_of


class Mixture:

    def __init__(self, name, top, cap, hidden, temperature=1.0, normalised=False, by_rows=False, gate=False):
        self.name, self.top, self.cap, self.hidden = name, top, cap, hidden
        self.temperature, self.normalised, self.by_rows, self.gate = temperature, normalised, by_rows, gate
        self.tiles = E * cap // P if cap else top * NT + E
        self.rows = self.tiles * P


def route(nc, c, mx, src, w_router, sorted_rows, r, cond=None, w_cond=None):
    with ExitStack() as stack:
        m = Memory(nc, stack, f"route_{mx.name}")
        wr = m.sb("wr", [P, KD, E])
        wr_rows = m.sb("wr_rows", [E, D])
        g_t, wg_t = m.sb("g_t", [DH, B]), m.sb("wg_t", [DH, E])
        lg, ex = m.sb("lg", [P, NT, E]), m.sb("ex", [P, NT, E])
        top = [m.sb(f"top{k}", [P, NT]) for k in range(mx.top)]
        hot = [m.sb(f"hot{k}", [P, NT, E]) for k in range(mx.top)]
        tmp, tmp2, red, total = m.sb("tmp", [P, NT, E]), m.sb("tmp2", [P, NT, E]), m.sb("red", [P, NT]), m.sb("total", [P, NT])
        sel = m.sb("sel", [P, NT + 1, E], BF16)
        desc_i, desc = m.sb("desc_i", [P, E], I32), m.sb("desc", [P, E])
        base_i, base = m.sb("base_i", [P, E], I32), m.sb("base", [P, E])
        edge_i, edge = m.sb("edge_i", [P, NT], I32), m.sb("edge", [P, NT])
        tile_i, tile_n = m.sb("tile_i", [P, mx.tiles], I32), m.sb("tile_n", [P, mx.tiles])
        over, ntile, cum = m.sb("over", [P, E, NT]), m.sb("ntile", [P, E]), m.sb("cum", [P, E])
        before_t, owner = m.sb("before_t", [P, mx.tiles, E]), m.sb("owner", [P, mx.tiles])
        rank = m.sb("rank", [P, NT, E])
        pos_f = m.sb("pos_f", [P, NT])
        x_ps = [m.ps(f"x_ps{n}", [P, S]) for n in range(2)]
        w_ps = m.ps("w_ps", [P, KD, E])
        l_ps, r_ps = m.ps("l_ps", [P, NT, E]), m.ps("r_ps", [P, NT + 1, E])
        names = "loaded iota_ready iota_f wt_ready wr_ready xt_ready xt_copied logits_ready lg_ready exp_ready sel_ready rank_ready pos_ready link".split()
        (loaded, iota_ready, iota_f, wt_ready, wr_ready, xt_ready, xt_copied, logits_ready, lg_ready, exp_ready, sel_ready, rank_ready,
         pos_ready, link_s) = (m.sem(x) for x in names)
        scattered, scattered_0 = m.pool_dma_sem("scattered", NT * mx.top)
        block = stack.enter_context(nc.Block())
        n_loads = 3 if cond is not None else 1

        @block.sync
        def _(sp):
            if mx.by_rows:
                sp.dma_start(wr_rows[:], w_router).then_inc(loaded, 16)
            else:
                sp.dma_start(wr[:], w_router.rearrange("(k p) e -> p k e", p=P)).then_inc(loaded, 16)
            if cond is not None:
                sp.dma_start(g_t[:], cond.rearrange("b g -> g b")).then_inc(loaded, 16)
                sp.dma_start(wg_t[:], w_cond.rearrange("e g -> g e")).then_inc(loaded, 16)

        @block.gpsimd
        def _(pool):
            pool.iota(desc_i[:], pattern=[[-1, E]], base=E, channel_multiplier=0).then_inc(iota_ready, 1)
            pool.iota(base_i[:], pattern=[[mx.cap, E]], base=0, channel_multiplier=0).then_inc(iota_ready, 1)
            pool.iota(edge_i[:], pattern=[[P, NT]], base=0, channel_multiplier=0).then_inc(iota_ready, 1)
            pool.iota(tile_i[:], pattern=[[1, mx.tiles]], base=0, channel_multiplier=0).then_inc(iota_ready, 1)
            pool.memset(sel[:], 0.0).then_inc(iota_ready, 1)
            pool.wait_ge(iota_ready, 5)
            for dst, s in ((desc, desc_i), (base, base_i), (edge, edge_i), (tile_n, tile_i)):
                pool.tensor_copy(dst[:], s[:]).then_inc(iota_f, 1)
            for k in range(mx.top):
                pool.wait_ge(pos_ready, k + 1)
                for t in range(NT):
                    pool.indirect_dma_start(sorted_rows, bass.IndirectOffsetOnAxis(ap=r.pos[k][:, t:t + 1], axis=0), src[:, t, :], None,
                                            bounds_check=mx.rows - 1, oob_is_err=False).then_inc(scattered, 16)
            pool.wait_ge(scattered, scattered_0 + 16 * NT * mx.top)

        @block.scalar
        def _(a):
            if mx.by_rows:
                a.wait_ge(wt_ready, 1)
                nc.scalar.activation(wr[:], w_ps[:], ACT.Copy).then_inc(wr_ready, 1)
            for b in range(B):
                for k in range(KD):
                    a.wait_ge(xt_ready, KD * b + k + 1)
                    nc.scalar.activation(c.xt[:, k, S * b:S * (b + 1)], x_ps[k][:], ACT.Copy).then_inc(xt_copied, 1)
            a.wait_ge(lg_ready, 1)
            nc.scalar.activation(ex[:], ex[:], ACT.Exp, scale=mx.temperature).then_inc(exp_ready, 1)

        @block.tensor
        def _(pe):
            if mx.by_rows:
                pe.wait_ge(loaded, 16 * n_loads)
                for k in range(KD):
                    last = nc.tensor.transpose(w_ps[:, k, :], wr_rows[:, P * k:P * (k + 1)], c.ident[0:E, 0:E])
                last.then_inc(wt_ready, 1)
            for b in range(B + 1):
                if b < B:
                    for k in range(KD):
                        if b >= 1:
                            pe.wait_ge(xt_copied, KD * (b - 1) + k + 1)
                        for t in range(QT):
                            last = nc.tensor.transpose(x_ps[k][:, P * t:P * (t + 1)], src[:, QT * b + t, P * k:P * (k + 1)], c.ident[:])
                        last.then_inc(xt_ready, 1)
                if b >= 1:
                    pe.wait_ge(xt_copied, KD * b)
                    if b == 1:
                        pe.wait_ge(loaded, 16 * n_loads)
                        if mx.by_rows:
                            pe.wait_ge(wr_ready, 1)
                    for t in range(QT * (b - 1), QT * b):
                        for k in range(KD):
                            last = nc.tensor.matmul(l_ps[:, t, :], c.xt[:, k, P * t:P * (t + 1)], wr[:, k, :], start=(k == 0),
                                                    stop=(k == KD - 1 and cond is None))
                        if cond is not None:
                            last = nc.tensor.matmul(l_ps[:, t, :], g_t[:, b - 1:b].to_broadcast([DH, P]), wg_t[:], start=False, stop=True)
            last.then_inc(logits_ready, 1)
            pe.wait_ge(sel_ready, 1)
            nc.tensor.matmul(r_ps[:], c.before[:], sel[:], start=True, stop=False)
            for t in range(NT):
                last = nc.tensor.matmul(r_ps[:, t + 1:, :], c.ones_b[:], sel[:, t:t + 1, :].to_broadcast([P, NT - t, E]), start=False, stop=(t == NT - 1))
            last.then_inc(rank_ready, 1)

        @block.vector
        def _(dve):
            linked = [0]
            V = nc.vector

            def link(ins):
                linked[0] += 1
                ins.then_inc(link_s, 1)
                dve.wait_ge(link_s, linked[0])

            def wide(t):
                return t[:].unsqueeze(2).to_broadcast([P, NT, E])

            def per_expert(t):
                return t[:].unsqueeze(1).to_broadcast([P, NT, E])

            dve.wait_ge(logits_ready, 1)
            dve.wait_ge(iota_f, 4)
            link(V.tensor_copy(lg[:], l_ps[:]))
            for k in range(mx.top):
                link(V.tensor_reduce(top[k][:], lg[:], AX.X, ALU.max))
                if k == 0:
                    link(V.tensor_tensor(ex[:], lg[:], wide(top[0]), ALU.subtract))
                    dve.sem_inc(lg_ready, 1)
                link(V.tensor_tensor(tmp[:], lg[:], wide(top[k]), ALU.is_ge))
                link(V.tensor_tensor(tmp[:], tmp[:], per_expert(desc), ALU.mult))
                link(V.tensor_reduce(red[:], tmp[:], AX.X, ALU.max))
                link(V.tensor_tensor(hot[k][:], tmp[:], wide(red), ALU.is_equal))
                if k + 1 < mx.top:
                    link(V.scalar_tensor_tensor(out=lg[:], in0=hot[k][:], scalar=2 * NEG, in1=lg[:], op0=ALU.mult, op1=ALU.add))
            if mx.top == 2:
                V.tensor_tensor(sel[:, 0:NT, :], hot[0][:], hot[1][:], ALU.add).then_inc(sel_ready, 1)
            else:
                V.tensor_copy(sel[:, 0:NT, :], hot[0][:]).then_inc(sel_ready, 1)
            dve.wait_ge(exp_ready, 1)
            link(V.tensor_reduce(total[:], ex[:], AX.X, ALU.add))
            link(V.reciprocal(total[:], total[:]))
            for k in range(mx.top):
                link(V.tensor_tensor(tmp[:], ex[:], hot[k][:], ALU.mult))
                link(V.tensor_reduce(red[:], tmp[:], AX.X, ALU.add))
                link(V.tensor_tensor(r.weight[k][:], red[:], total[:], ALU.mult))
            if mx.normalised:
                link(V.scalar_tensor_tensor(out=total[:], in0=r.weight[0][:], scalar=1e-20, in1=r.weight[1][:], op0=ALU.add, op1=ALU.add))
                link(V.reciprocal(total[:], total[:]))
                for k in range(mx.top):
                    link(V.tensor_tensor(r.weight[k][:], r.weight[k][:], total[:], ALU.mult))
            dve.wait_ge(rank_ready, 1)
            link(V.tensor_copy(rank[:], r_ps[:, 0:NT, :]))
            if not mx.cap:
                link(V.tensor_copy(base[:], r_ps[:, NT, :]))
                link(V.tensor_tensor(over[:], base[:].unsqueeze(2).to_broadcast([P, E, NT]), edge[:].unsqueeze(1).to_broadcast([P, E, NT]), ALU.is_gt))
                link(V.tensor_reduce(ntile[:], over[:], AX.X, ALU.add))
                link(V.tensor_copy(cum[:], ntile[:]))
                for e in range(1, E):
                    link(V.tensor_tensor(cum[:, e:e + 1], cum[:, e:e + 1], cum[:, e - 1:e], ALU.add))
                link(V.tensor_tensor(base[:], cum[:], ntile[:], ALU.subtract))
                link(V.tensor_scalar(base[:], base[:], float(P), None, ALU.mult))
                link(V.tensor_tensor(before_t[:], tile_n[:].unsqueeze(2).to_broadcast([P, mx.tiles, E]), cum[:].unsqueeze(1).to_broadcast([P, mx.tiles, E]), ALU.is_ge))
                link(V.tensor_reduce(owner[:], before_t[:], AX.X, ALU.add))
                link(V.tensor_scalar(owner[:], owner[:], float(E - 1), None, ALU.min))
                link(V.tensor_copy(r.owner[:], owner[:]))
            link(V.tensor_tensor(tmp2[:], rank[:], per_expert(base), ALU.add))
            for k in range(mx.top):
                link(V.tensor_tensor(tmp[:], tmp2[:], hot[k][:], ALU.mult))
                link(V.tensor_reduce(pos_f[:], tmp[:], AX.X, ALU.add))
                if mx.cap:
                    link(V.tensor_tensor(tmp[:], rank[:], hot[k][:], ALU.mult))
                    link(V.tensor_reduce(red[:], tmp[:], AX.X, ALU.add))
                    link(V.tensor_scalar(red[:], red[:], float(mx.cap), None, ALU.is_ge))
                    link(V.scalar_tensor_tensor(out=pos_f[:], in0=red[:], scalar=float(1 << 20), in1=pos_f[:], op0=ALU.mult, op1=ALU.add))
                    link(V.tensor_scalar(red[:], red[:], -1.0, 1.0, ALU.mult, ALU.add))
                    link(V.tensor_tensor(r.weight[k][:], r.weight[k][:], red[:], ALU.mult))
                V.tensor_copy(r.pos[k][:], pos_f[:]).then_inc(pos_ready, 1)
                dve.wait_ge(pos_ready, k + 1)


def experts_by_capacity(nc, c, mx, w1, w2, sorted_rows, expert_rows, func):
    cap, F = mx.cap, mx.hidden
    FC, CT = F // P, cap // P
    with ExitStack() as stack:
        m = Memory(nc, stack, f"exp_{mx.name}")
        w1_sb = [m.sb(f"w1_{n}", [P, KD, F]) for n in range(2)]
        w2_sb = [m.sb(f"w2_{n}", [P, FC, D]) for n in range(2)]
        xs = [m.sb(f"xs{n}", [P, CT, D]) for n in range(2)]
        xs_t = [m.sb(f"xs_t{n}", [P, KD, cap]) for n in range(2)]
        hid = [m.sb(f"hid{n}", [P, FC, cap]) for n in range(2)]
        ys = [m.sb(f"ys{n}", [P, CT, D]) for n in range(2)]
        x_ps = [m.ps(f"x_ps{k}", [P, S]) for k in range(KD)]
        h_ps = [m.ps(f"h_ps{n}", [P, S]) for n in range(4)]
        y_ps = [m.ps(f"y_ps{n}", [P, 2, D]) for n in range(2)]
        xs_loaded, w1_loaded, w2_loaded = ([m.sem(f"{x}_loaded{n}") for n in range(2)] for x in ("xs", "w1", "w2"))
        names = "xt_ready xt_copied h_ready hid_ready y_ready y_copied".split()
        (xt_ready, xt_copied, h_ready, hid_ready, y_ready, y_copied) = (m.sem(x) for x in names)
        m.start_at_one(xt_copied, h_ready, hid_ready, y_ready, y_copied)
        stored, stored_0 = zip(*(m.pool_dma_sem(f"stored{n}", E // 2) for n in range(2)))
        block = stack.enter_context(nc.Block())
        R = E // 2
        YT = max(CT // 2, 1)
        x_rows = sorted_rows[0:mx.rows, :].rearrange("(e t p) d -> e p t d", e=E, p=P)
        y_rows = expert_rows[0:mx.rows, :].rearrange("(e t p) d -> e p t d", e=E, p=P)
        w1_v = w1.rearrange("e (k p) f -> e p k f", p=P)
        w2_v = w2.rearrange("e (k p) f -> e p k f", p=P)

        @block.sync
        def _(sp):
            def load(e, n):
                sp.dma_start(xs[n][:], x_rows[ds(e, 1)].rearrange("a p t d -> (a p) t d")).then_inc(xs_loaded[n], 16)
                sp.dma_start(w1_sb[n][:], w1_v[ds(e, 1)].rearrange("a p k f -> (a p) k f")).then_inc(w1_loaded[n], 16)
                sp.dma_start(w2_sb[n][:], w2_v[ds(e, 1)].rearrange("a p k f -> (a p) k f")).then_inc(w2_loaded[n], 16)

            for n in range(2):
                load(n, n)
            with sp.Fori(0, R - 1) as i:
                for n in range(2):
                    done = sp.to_reg(i * (2 * YT) + YT * (n + 1) + 1)
                    sp.wait_ge(y_ready, 1)
                    sp.wait_ge(y_ready, done)
                    load(i * 2 + 2 + n, n)

        @block.gpsimd
        def _(pool):
            with pool.Fori(0, R) as i:
                for n in range(2):
                    done = pool.to_reg(i * (2 * YT) + YT * (n + 1) + 1)
                    pool.wait_ge(y_copied, 1)
                    pool.wait_ge(y_copied, done)
                    pool.dma_start(y_rows[ds(i * 2 + n, 1)].rearrange("a p t d -> (a p) t d"), ys[n][:]).then_inc(stored[n], 16)
            for n in range(2):
                pool.wait_ge(stored[n], stored_0[n] + 16 * R)

        @block.tensor
        def _(pe):
            def turn(i, n):
                pe.wait_ge(xs_loaded[n], i * 16 + 16)
                for k in range(KD):
                    pe.wait_ge(xt_copied, i * (2 * KD) + KD * n + 1)
                    for t in range(CT):
                        last = nc.tensor.transpose(x_ps[k][:, P * t:P * (t + 1)], xs[n][:, t, P * k:P * (k + 1)], c.ident[:])
                    last.then_inc(xt_ready, 1)

            with pe.Fori(0, R) as i:
                for n in range(2):
                    turn(i, n)
                    pe.wait_ge(w1_loaded[n], i * 16 + 16)
                    pe.wait_ge(xt_copied, i * (2 * KD) + KD * (n + 1) + 1)
                    for f in range(FC):
                        pe.wait_ge(hid_ready, i * (2 * FC) + max(FC * n + f - 3, 0) + 1)
                        for k in range(KD):
                            last = nc.tensor.matmul(h_ps[f % 4][:, 0:cap], w1_sb[n][:, k, P * f:P * (f + 1)], xs_t[n][:, k, :],
                                                    start=(k == 0), stop=(k == KD - 1))
                        last.then_inc(h_ready, 1)
                    pe.wait_ge(w2_loaded[n], i * 16 + 16)
                    for t in range(CT):
                        if t % 2 == 0:
                            pe.wait_ge(y_copied, i * (2 * YT) + max(YT * n + t // 2 - 1, 0) + 1)
                        for f in range(FC):
                            if t == 0:
                                pe.wait_ge(hid_ready, i * (2 * FC) + FC * n + f + 1 + 1)
                            last = nc.tensor.matmul(y_ps[(YT * n + t // 2) % 2][:, t % 2, :], hid[n][:, f, P * t:P * (t + 1)], w2_sb[n][:, f, :],
                                                    start=(f == 0), stop=(f == FC - 1))
                        if t % 2:
                            last.then_inc(y_ready, 1)

        @block.vector
        def _(dve):
            with dve.Fori(0, R) as i:
                for n in range(2):
                    for k in range(KD):
                        dve.wait_ge(xt_ready, i * (2 * KD) + KD * n + k + 1)
                        dve.wait_ge(h_ready, i * (2 * FC) + 1)
                        nc.vector.tensor_copy(xs_t[n][:, k, :], x_ps[k][:, 0:cap]).then_inc(xt_copied, 1)
                    for y in range(YT):
                        dve.wait_ge(y_ready, i * (2 * YT) + YT * n + y + 1 + 1)
                        dve.wait_ge(stored[n], i * 16 + stored_0[n])
                        nc.vector.tensor_copy(ys[n][:, 2 * y:2 * y + 2, :], y_ps[(YT * n + y) % 2][:]).then_inc(y_copied, 1)

        @block.scalar
        def _(a):
            with a.Fori(0, R) as i:
                for n in range(2):
                    for f in range(FC):
                        a.wait_ge(h_ready, i * (2 * FC) + FC * n + f + 1 + 1)
                        a.wait_ge(y_ready, i * (2 * YT) + 1)
                        nc.scalar.activation(hid[n][:, f, :], h_ps[f % 4][:, 0:cap], func).then_inc(hid_ready, 1)


def experts_by_tile(nc, c, mx, weights, sorted_rows, expert_rows, r):
    F = mx.hidden
    FC = F // P
    wide = F == 512
    with ExitStack() as stack:
        m = Memory(nc, stack, f"til_{mx.name}")
        wa = m.sb("wa", [P, E * KD, F])
        wb = m.sb("wb", [P, E * KD, F])
        wd = m.sb("wd", [P, E * FC, D])
        xs = [m.sb(f"xs{n}", [P, D]) for n in range(2)]
        xs_t = [m.sb(f"xs_t{n}", [P, KD, P]) for n in range(2)]
        act = [m.sb(f"act{n}", [P, F]) for n in range(2)]
        lin = [m.sb(f"lin{n}", [P, F]) for n in range(2)]
        hid = [m.sb(f"hid{n}", [P, F]) for n in range(2)]
        hid_t = [m.sb(f"hid_t{n}", [P, FC, P]) for n in range(2)]
        ys = [m.sb(f"ys{n}", [P, D]) for n in range(2)]
        a_ps = [m.ps(f"a_ps{n}", [P, 512]) for n in range(2)]
        b_ps = [m.ps(f"b_ps{n}", [P, 512]) for n in range(2)]
        x_ps = m.ps("x_ps", [P, KD, P])
        t_ps = m.ps("t_ps", [P, FC, P])
        y_ps = [m.ps(f"y_ps{n}", [P, D]) for n in range(2)]
        w_loaded = m.sem("w_loaded")
        xs_loaded = [m.sem(f"xs_loaded{n}") for n in range(2)]
        stored, stored_0 = zip(*(m.pool_dma_sem(f"stored{n}", mx.tiles // 2) for n in range(2)))
        names = "xt_ready xt_copied ab_ready act_ready lin_ready hid_ready ht_ready ht_copied y_ready y_copied".split()
        (xt_ready, xt_copied, ab_ready, act_ready, lin_ready, hid_ready, ht_ready, ht_copied, y_ready, y_copied) = (m.sem(x) for x in names)
        m.start_at_one(xt_copied, ab_ready, hid_ready, ht_ready, ht_copied, y_ready, y_copied)
        block = stack.enter_context(nc.Block())
        R = mx.tiles // 2
        x_rows = sorted_rows[0:mx.rows, :].rearrange("(t p) d -> t p d", p=P)
        y_rows = expert_rows[0:mx.rows, :].rearrange("(t p) d -> t p d", p=P)

        @block.sync
        def _(sp):
            def load(t, n):
                sp.dma_start(xs[n][:], x_rows[ds(t, 1)].rearrange("a p d -> (a p) d")).then_inc(xs_loaded[n], 16)

            for n in range(2):
                load(n, n)
            for t, w in ((wa, weights[0]), (wb, weights[1]), (wd, weights[2])):
                sp.dma_start(t[:], w.rearrange("e (k p) f -> p (e k) f", p=P)).then_inc(w_loaded, 16)
            with sp.Fori(0, R - 1) as i:
                for n in range(2):
                    turned = sp.to_reg(i * 2 + n + 1)
                    sp.wait_ge(xt_ready, 1)
                    sp.wait_ge(xt_ready, turned)
                    load(i * 2 + 2 + n, n)

        @block.gpsimd
        def _(pool):
            with pool.Fori(0, R) as i:
                for n in range(2):
                    done = pool.to_reg(i * 2 + n + 2)
                    pool.wait_ge(y_copied, 1)
                    pool.wait_ge(y_copied, done)
                    pool.dma_start(y_rows[ds(i * 2 + n, 1)].rearrange("a p d -> (a p) d"), ys[n][:]).then_inc(stored[n], 16)
            for n in range(2):
                pool.wait_ge(stored[n], stored_0[n] + 16 * R)

        @block.tensor
        def _(pe):
            pe.wait_ge(w_loaded, 48)
            with pe.Fori(0, R) as i:
                for n in range(2):
                    expert = pe.value_load(r.owner[0:1, ds(i * 2 + n, 1)], min_val=0, max_val=E - 1)
                    pe.wait_ge(xs_loaded[n], i * 16 + 16)
                    pe.wait_ge(xt_copied, i * 2 + n + 1)
                    for k in range(KD):
                        last = nc.tensor.transpose(x_ps[:, k, :], xs[n][:, P * k:P * (k + 1)], c.ident[:])
                    last.then_inc(xt_ready, 1)
                    pe.wait_ge(xt_copied, i * 2 + n + 1 + 1)
                    pe.wait_ge(hid_ready, i * 2 + max(n - 1, 0) + 1)
                    for ps, w in ((a_ps, wa), (b_ps, wb)):
                        for k in range(KD):
                            last = nc.tensor.matmul(ps[n][:, 0:F], xs_t[n][:, k, :], w[:, ds(expert * KD + k, 1), :].rearrange("p a f -> p (a f)"),
                                                    start=(k == 0), stop=(k == KD - 1))
                    last.then_inc(ab_ready, 1)
                    pe.wait_ge(hid_ready, i * 2 + n + 1 + 1)
                    pe.wait_ge(ht_copied, i * 2 + n + 1)
                    for f in range(FC):
                        last = nc.tensor.transpose(t_ps[:, f, :], hid[n][:, P * f:P * (f + 1)], c.ident[:])
                    last.then_inc(ht_ready, 1)
                    pe.wait_ge(ht_copied, i * 2 + n + 1 + 1)
                    pe.wait_ge(y_copied, i * 2 + max(n - 1, 0) + 1)
                    for f in range(FC):
                        last = nc.tensor.matmul(y_ps[n][:], hid_t[n][:, f, :], wd[:, ds(expert * FC + f, 1), :].rearrange("p a f -> p (a f)"),
                                                start=(f == 0), stop=(f == FC - 1))
                    last.then_inc(y_ready, 1)

        @block.scalar
        def _(a):
            with a.Fori(0, R) as i:
                for n in range(2):
                    a.wait_ge(ab_ready, i * 2 + n + 1 + 1)
                    a.wait_ge(hid_ready, i * 2 + max(n - 1, 0) + 1)
                    nc.scalar.activation(act[n][:], a_ps[n][:, 0:F], ACT.Copy if mx.gate else ACT.Silu).then_inc(act_ready, 1)
                    a.wait_ge(ht_ready, i * 2 + n + 1 + 1)
                    a.wait_ge(y_ready, i * 2 + max(n - 1, 0) + 1)
                    nc.scalar.activation(hid_t[n][:], t_ps[:], ACT.Copy).then_inc(ht_copied, 1)

        @block.vector
        def _(dve):
            with dve.Fori(0, R) as i:
                for n in range(2):
                    dve.wait_ge(xt_ready, i * 2 + n + 1)
                    dve.wait_ge(ab_ready, i * 2 + max(n - 1, 0) + 1)
                    nc.vector.tensor_copy(xs_t[n][:], x_ps[:]).then_inc(xt_copied, 1)
                    dve.wait_ge(act_ready, i * 2 + n + 1)
                    if mx.gate:
                        dve.wait_ge(hid_ready, i * 2 + max(n - 1, 0) + 1)
                        nc.vector.scalar_tensor_tensor(out=lin[n][:], in0=act[n][:], scalar=0.01, in1=act[n][:], op0=ALU.mult,
                                                       op1=ALU.max).then_inc(lin_ready, 1)
                        dve.wait_ge(lin_ready, i * 2 + n + 1)
                    dve.wait_ge(ht_ready, i * 2 + max(n - 1, 0) + 1)
                    nc.vector.tensor_tensor(hid[n][:], (lin if mx.gate else act)[n][:], b_ps[n][:, 0:F], ALU.mult).then_inc(hid_ready, 1)
                    dve.wait_ge(y_ready, i * 2 + n + 1 + 1)
                    dve.wait_ge(stored[n], i * 16 + stored_0[n])
                    nc.vector.tensor_copy(ys[n][:], y_ps[n][:]).then_inc(y_copied, 1)


def combine(nc, c, mx, expert_rows, r, start, dst, bias=None):
    with ExitStack() as stack:
        m = Memory(nc, stack, f"com_{mx.name}")
        rows = [m.sb(f"rows{k}", [P, NT, D]) for k in range(mx.top)]
        bias_sb = m.sb("bias", [P, D])
        cleared, loaded, biased, added = m.sem("cleared"), m.sem("loaded"), m.sem("biased"), m.sem("added")
        G = 4
        got = [m.pool_dma_sem(f"got{g}", G * mx.top) for g in range(NT // G)]
        block = stack.enter_context(nc.Block())

        @block.sync
        def _(sp):
            if bias is not None:
                sp.dma_start(bias_sb[:], row(bias.rearrange("a b d -> (a b d)"))).then_inc(loaded, 16)

        @block.gpsimd
        def _(pool):
            if mx.cap:
                pool.wait_ge(cleared, mx.top)
            for t in range(NT):
                for k in range(mx.top):
                    pool.indirect_dma_start(rows[k][:, t, :], None, expert_rows, bass.IndirectOffsetOnAxis(ap=r.pos[k][:, t:t + 1], axis=0),
                                            bounds_check=mx.rows - 1, oob_is_err=False).then_inc(got[t // G][0], 16)

        @block.vector
        def _(dve):
            if mx.cap:
                for k in range(mx.top):
                    nc.vector.memset(rows[k][:], 0.0).then_inc(cleared, 1)
            if bias is not None:
                dve.wait_ge(loaded, 16)
                nc.vector.tensor_tensor(dst[:], start[:], bias_sb[:].unsqueeze(1).to_broadcast([P, NT, D]), ALU.add).then_inc(biased, 1)
                dve.wait_ge(biased, 1)
            for t in range(NT):
                if t % G == 0:
                    dve.wait_ge(got[t // G][0], got[t // G][1] + 16 * G * mx.top)
                for k in range(mx.top):
                    nc.vector.scalar_tensor_tensor(out=dst[:, t, :], in0=rows[k][:, t, :], scalar=r.weight[k][:, t:t + 1],
                                                   in1=(start if k == 0 and bias is None else dst)[:, t, :], op0=ALU.mult,
                                                   op1=ALU.add).then_inc(added, 1)
                    dve.wait_ge(added, mx.top * t + k + 1)


def shared_expert(nc, c, w_gate, w_up, w_down):
    with ExitStack() as stack:
        m = Memory(nc, stack, "shx")
        wgu = m.sb("wgu", [P, KD, 2, D])
        wd = m.sb("wd", [P, KD, D])
        act = [m.sb(f"act{n}", [P, D]) for n in range(2)]
        lin = [m.sb(f"lin{n}", [P, D]) for n in range(2)]
        hid = [m.sb(f"hid{n}", [P, D]) for n in range(2)]
        hid_t = [m.sb(f"hid_t{n}", [P, KD, P]) for n in range(2)]
        gu_ps = [m.ps(f"gu_ps{n}", [P, 2, D]) for n in range(2)]
        t_ps = [m.ps(f"t_ps{n}", [P, KD, P]) for n in range(2)]
        y_ps = [m.ps(f"y_ps{n}", [P, D]) for n in range(2)]
        names = "loaded gu_ready act_ready lin_ready hid_ready ht_ready ht_copied y_ready h_ready".split()
        (loaded, gu_ready, act_ready, lin_ready, hid_ready, ht_ready, ht_copied, y_ready, h_ready) = (m.sem(x) for x in names)
        block = stack.enter_context(nc.Block())

        @block.sync
        def _(sp):
            sp.dma_start(wgu[:, :, 0, :], w_gate.rearrange("(k p) f -> p k f", p=P)).then_inc(loaded, 16)
            sp.dma_start(wgu[:, :, 1, :], w_up.rearrange("(k p) f -> p k f", p=P)).then_inc(loaded, 16)
            sp.dma_start(wd[:], w_down.rearrange("(k p) f -> p k f", p=P)).then_inc(loaded, 16)

        @block.tensor
        def _(pe):
            pe.wait_ge(loaded, 48)
            for t in range(NT + 1):
                if t < NT:
                    if t >= 2:
                        pe.wait_ge(hid_ready, t - 1)
                    for k in range(KD):
                        last = nc.tensor.matmul(gu_ps[t % 2][:], c.xt[:, k, P * t:P * (t + 1)], wgu[:, k, :, :], start=(k == 0), stop=(k == KD - 1))
                    last.then_inc(gu_ready, 1)
                if t >= 1:
                    v = t - 1
                    pe.wait_ge(hid_ready, v + 1)
                    if v >= 2:
                        pe.wait_ge(ht_copied, v - 1)
                    for f in range(KD):
                        last = nc.tensor.transpose(t_ps[v % 2][:, f, :], hid[v % 2][:, P * f:P * (f + 1)], c.ident[:])
                    last.then_inc(ht_ready, 1)
                    pe.wait_ge(ht_copied, v + 1)
                    if v >= 2:
                        pe.wait_ge(h_ready, v - 1)
                    for f in range(KD):
                        last = nc.tensor.matmul(y_ps[v % 2][:], hid_t[v % 2][:, f, :], wd[:, f, :], start=(f == 0), stop=(f == KD - 1))
                    last.then_inc(y_ready, 1)

        @block.scalar
        def _(a):
            for t in range(NT + 1):
                if t < NT:
                    a.wait_ge(gu_ready, t + 1)
                    if t >= 2:
                        a.wait_ge(lin_ready, t - 1)
                    nc.scalar.activation(act[t % 2][:], gu_ps[t % 2][:, 0, :], ACT.Copy).then_inc(act_ready, 1)
                if t >= 1:
                    a.wait_ge(ht_ready, t)
                    if t >= 3:
                        a.wait_ge(y_ready, t - 2)
                    nc.scalar.activation(hid_t[(t - 1) % 2][:], t_ps[(t - 1) % 2][:], ACT.Copy).then_inc(ht_copied, 1)

        @block.vector
        def _(dve):
            for t in range(NT + 1):
                if t < NT:
                    dve.wait_ge(act_ready, t + 1)
                    if t >= 2:
                        dve.wait_ge(hid_ready, t - 1)
                    nc.vector.scalar_tensor_tensor(out=lin[t % 2][:], in0=act[t % 2][:], scalar=0.01, in1=act[t % 2][:], op0=ALU.mult,
                                                   op1=ALU.max).then_inc(lin_ready, 1)
                    dve.wait_ge(lin_ready, t + 1)
                    if t >= 2:
                        dve.wait_ge(ht_ready, t - 1)
                    nc.vector.tensor_tensor(hid[t % 2][:], lin[t % 2][:], gu_ps[t % 2][:, 1, :], ALU.mult).then_inc(hid_ready, 1)
                if t >= 1:
                    dve.wait_ge(y_ready, t)
                    nc.vector.tensor_copy(c.h[:, t - 1, :], y_ps[(t - 1) % 2][:]).then_inc(h_ready, 1)


class Routing:

    def __init__(self, nc, stack, mx):
        m = Memory(nc, stack, f"r_{mx.name}")
        self.pos = [m.sb(f"pos{k}", [P, NT], I32) for k in range(mx.top)]
        self.weight = [m.sb(f"weight{k}", [P, NT]) for k in range(mx.top)]
        self.owner = m.sb("owner", [P, mx.tiles], I32)


def clear_rows(nc, c, buffers):
    with ExitStack() as stack:
        m = Memory(nc, stack, "clr")
        zero = m.sb("zero", [P, 8 * D])
        cleared, stored = m.sem("cleared"), m.sem("stored")
        by_pool = [m.pool_dma_sem(f"stored{n}", 1)[0] for n in range(2)]
        block = stack.enter_context(nc.Block())
        parts = [b[lo:min(lo + 8 * P, b.shape[0]), :] for b in buffers for lo in range(0, b.shape[0], 8 * P)]

        @block.vector
        def _(dve):
            nc.vector.memset(zero[:], 0.0).then_inc(cleared, 1)

        @block.gpsimd
        def _(pool):
            pool.wait_ge(cleared, 1)
            for part, semaphore in zip(parts[:2], by_pool):
                pool.dma_start(part.rearrange("(p t) d -> p (t d)", p=P), zero[:, 0:part.shape[0] // P * D]).then_inc(semaphore, 16)
            for semaphore in by_pool:
                pool.wait_ge(semaphore, 16)

        @block.sync
        def _(sp):
            sp.wait_ge(cleared, 1)
            for part in parts[2:]:
                n = part.shape[0] // P
                sp.dma_start(part.rearrange("(p t) d -> p (t d)", p=P), zero[:, 0:n * D]).then_inc(stored, 16)
            sp.wait_ge(stored, 16 * (len(parts) - 2))


def build(nc, d, out):
    def group(prefix, **more):
        return {**{n[len(prefix):]: ap for n, ap in d.items() if n.startswith(prefix)}, **more}

    mixtures = {
        "f1": Mixture("f1", 2, 2 * T // E, 1024),
        "c2": Mixture("c2", 2, 0, 128, temperature=0.5, normalised=True, by_rows=True, gate=True),
        "f2": Mixture("f2", 1, T // E, 1024),
        "f3": Mixture("f3", 2, 0, 512, by_rows=True),
    }

    def scratch(name, shape):
        return nc.dram_tensor(name, shape, F32, kind="Internal").ap()

    Memory.cleared, Memory.pool_dma_semaphores = [], {}
    with ExitStack() as stack:
        stack.enter_context(nc.allow_non_contiguous_dma(reason="short vectors by column"))
        c = shared(nc, stack)
        rows = {n: scratch(f"sorted_{n}", [mx.rows, D]) for n, mx in mixtures.items()}
        done = {n: scratch(f"expert_{n}", [mx.rows, D]) for n, mx in mixtures.items()}
        make_constants(nc, c)
        clear_rows(nc, c, list(rows.values()))

        def attend(l, w, mask, bias_of, causal, w_out, x_in=None):
            with ExitStack() as inner:
                attention_memory(nc, inner, c, l)
                attention_inputs(nc, c, l, w, d["cond_64"], mask, x_in)
                attention(nc, c, l, bias_of, causal)
                attention_output(nc, c, l, w_out, w["g_out"], d["cond_64"])

        def relative(l, w):
            band = scratch(f"band{l}", [H, P, S])
            relative_bias(nc, c, l, w, scratch(f"rev{l}", [H, REV]), band)
            return band_bias(band)

        w = group("L0_cond_", g=d["L0_cond_g_in"])
        given = d["fside_16xSxS_0"]
        attend(0, w, d["mask_BxS_bk0"], lambda i, hh, q: given[ds(i * 2 + hh, 1), P * q:P * (q + 1), 0:P * (q + 1)].rearrange("a p n -> (a p) n"),
               True, w["Wo"], x_in=d["x"])
        ternary_linear(nc, c, d["L0_ffn_weight"])

        w = group("L1_cond_", g=d["L1_cond_g_norm"])
        attend(1, w, d["mask_BxS_bf1"], relative(1, w), False, w["Wout"])
        mx, w = mixtures["f1"], group("L1_ffn_")
        with ExitStack() as inner:
            r = Routing(nc, inner, mx)
            route(nc, c, mx, c.h, w["w_router"], rows["f1"], r)
            experts_by_capacity(nc, c, mx, w["w1"], w["w2"], rows["f1"], done["f1"], ACT.Gelu_apprx_tanh)
            combine(nc, c, mx, done["f1"], r, c.x, c.x, bias=w["bias"])

        mx, w = mixtures["c2"], group("L2_cond_")
        with ExitStack() as inner:
            r = Routing(nc, inner, mx)
            route(nc, c, mx, c.x, w["wt"], rows["c2"], r, cond=d["cond_64"], w_cond=w["wg"])
            shared_expert(nc, c, w["sw_gate"], w["sw_up"], w["sw_down"])
            experts_by_tile(nc, c, mx, (w["w_gate"], w["w_up"], w["w_down"]), rows["c2"], done["c2"], r)
            combine(nc, c, mx, done["c2"], r, c.h, c.h)
        mx, w = mixtures["f2"], group("L2_ffn_")
        with ExitStack() as inner:
            r = Routing(nc, inner, mx)
            route(nc, c, mx, c.h, w["Wr"], rows["f2"], r)
            experts_by_capacity(nc, c, mx, w["W1"], w["W2"], rows["f2"], done["f2"], ACT.Relu)
            combine(nc, c, mx, done["f2"], r, c.x, c.x)

        w = group("L3_cond_", g=d["L3_cond_g_norm"])
        attend(3, w, d["mask_BxS_bf1"], relative(3, w), False, w["Wout"])
        mx, w = mixtures["f3"], group("L3_ffn_")
        with ExitStack() as inner:
            r = Routing(nc, inner, mx)
            route(nc, c, mx, c.h, w["gate_w"], rows["f3"], r)
            experts_by_tile(nc, c, mx, (w["w1"], w["w3"], w["w2"]), rows["f3"], done["f3"], r)
            combine(nc, c, mx, done["f3"], r, c.x, c.x)

        out_stored = Memory(nc, stack, "end").sem("out_stored")
        with nc.Block() as block:
            @block.sync
            def _(sp):
                sp.dma_start(out.rearrange("b (t p) d -> p (b t) d", p=P), c.x[:]).then_inc(out_stored, 16)
                sp.wait_ge(out_stored, 16)


def kernel(**inputs):
    import numpy as _np
    import concourse.bacc as _bacc
    from concourse import mybir as _mybir
    from concourse.bass_utils import run_bass_kernel_spmd as _run

    nc = _bacc.Bacc("TRN2", target_bir_lowering=False, num_devices=1)
    arrays, args = {}, {}
    for name, a in inputs.items():
        a = _np.ascontiguousarray(a)
        if a.dtype == bool:
            a = a.view(_np.uint32)
        arrays[f"in_{name}_dram"] = a
        args[name] = nc.dram_tensor(f"in_{name}_dram", a.shape, _mybir.dt.from_np(a.dtype), kind="ExternalInput").ap()
    out = nc.dram_tensor("out_0_dram", (B, S, D), F32, kind="ExternalOutput").ap()
    build(nc, args, out)
    r = _run(nc, [arrays], core_ids=[0])
    return r.results[0]["out_0_dram"]
```

```python
from contextlib import ExitStack

import concourse.bass as bass
from concourse import mybir

F32 = mybir.dt.float32
BF16 = mybir.dt.bfloat16
I32 = mybir.dt.int32
U8 = mybir.dt.uint8
ALU = mybir.AluOpType
ACT = mybir.ActivationFunctionType
AX = mybir.AxisListType
ds = bass.ds

P = 128
B, S, D = 4, 512, 256
T = B * S
NT = T // P
QT = S // P
KD = D // P
H, DH = 16, 64
HP = H // 2
E = 8
EPS = 1e-5
NEG = -1e30
REV = 640
NKEY = [1 + P * (q + 1) for q in range(QT)]


class Memory:

    cleared = []
    pool_dma_semaphores = {}

    def __init__(self, nc, stack, prefix):
        self.nc, self.stack, self.prefix = nc, stack, prefix
        self.semaphores = []
        stack.callback(self.release)

    def release(self):
        for semaphore in Memory.cleared:
            self.nc.release_semaphore(semaphore)
        for run in runs(self.semaphores):
            self.nc.gpsimd.sem_clear(run)
        Memory.cleared = self.semaphores

    def sb(self, name, shape, dt=F32):
        return self.stack.enter_context(self.nc.sbuf_tensor(f"{self.prefix}_{name}", shape, dt))

    def ps(self, name, shape, dt=F32):
        return self.stack.enter_context(self.nc.psum_tensor(f"{self.prefix}_{name}", shape, dt))

    def sem(self, name):
        self.semaphores.append(self.nc.alloc_semaphore(name=f"{self.prefix}_{name}"))
        return self.semaphores[-1]

    def start_at_one(self, *semaphores):
        for semaphore in semaphores:
            self.nc.gpsimd.sem_inc(semaphore, 1)
        self.nc.all_engine_barrier()

    def pool_dma_sem(self, name, dmas):
        kept = Memory.pool_dma_semaphores
        semaphore, value = kept.get(name) or (self.nc.alloc_semaphore(name=name), 0)
        kept[name] = semaphore, value + 16 * dmas
        return semaphore, value


def runs(semaphores):
    numbers = sorted(s.num for s in semaphores)
    starts = [n for n in numbers if n - 1 not in numbers]
    ends = [n + 1 for n in numbers if n + 1 not in numbers]
    return [range(a, b) for a, b in zip(starts, ends)]


def inverse_root(pool, c, value, op, constant, summed, n, ready):
    pool.tensor_scalar(value, value, constant, None, op).then_inc(summed, 1)
    pool.wait_ge(summed, n)
    pool.tensor_tensor(value, value, c.minus_half[0:value.shape[0], 0:1].to_broadcast(list(value.shape)), ALU.pow).then_inc(ready, 1)


def row(ap_1d, partitions=P):
    n = ap_1d.shape[0]
    return ap_1d.rearrange("(a n) -> a n", a=1).to_broadcast([partitions, n])


def make_constants(nc, c):
    with ExitStack() as stack:
        m = Memory(nc, stack, "const")
        filled = m.sem("filled")
        done = m.sem("done")
        block = stack.enter_context(nc.Block())

        @block.gpsimd
        def _(pool):
            pool.memset(c.ident[:], 0.0).then_inc(filled, 1)
            pool.memset(c.before[:], 1.0).then_inc(filled, 1)
            pool.memset(c.row0[:], 1.0).then_inc(filled, 1)
            pool.memset(c.ones_b[:], 1.0).then_inc(done, 1)
            pool.memset(c.ones_f[:], 1.0).then_inc(done, 1)
            pool.memset(c.minus_half[:], -0.5).then_inc(done, 1)
            pool.wait_ge(filled, 3)
            pool.affine_select(out=c.ident[:], in_=c.ident[:], compare_op=ALU.not_equal, fill=1.0, base=0,
                               pattern=[[-1, P]], channel_multiplier=1).then_inc(done, 1)
            pool.affine_select(out=c.before[:], in_=c.before[:], compare_op=ALU.is_gt, fill=0.0, base=0,
                               pattern=[[1, P]], channel_multiplier=-1).then_inc(done, 1)
            pool.affine_select(out=c.row0[:], in_=c.row0[:], compare_op=ALU.is_ge, fill=0.0, base=0,
                               pattern=[[0, P]], channel_multiplier=-1).then_inc(done, 1)
            pool.wait_ge(done, 6)


def relative_bias(nc, c, l, w, rev, band):
    with ExitStack() as stack:
        m = Memory(nc, stack, f"rel{l}")
        w0, b0, g0 = m.sb("w0", [P, D]), m.sb("b0", [P, D]), m.sb("g0", [P, D])
        b1, g1 = m.sb("b1", [P, D]), m.sb("g1", [P, D])
        w1, w2 = m.sb("w1", [P, KD, D]), m.sb("w2", [P, KD, H])
        b2 = m.sb("b2", [H, 1])
        dist_i, dist = m.sb("dist_i", [P, QT], I32), m.sb("dist", [P, QT])
        hid = m.sb("hid", [P, QT, D])
        act = m.sb("act", [P, QT, D])
        act_t = m.sb("act_t", [P, KD, S])
        stats, mv = m.sb("stats", [P, QT, 6]), m.sb("mv", [P, QT, 2])
        out_row = m.sb("out_row", [H, REV])
        t_ps = m.ps("t_ps", [P, KD, S])
        h_ps = m.ps("h_ps", [P, QT, D])
        o_ps = m.ps("o_ps", [P, S])
        loaded, dist_made, link_s = m.sem("loaded"), m.sem("dist_made"), m.sem("link")
        mv_ready, rooting, rstd_ready = m.sem("mv_ready"), m.sem("rooting"), m.sem("rstd_ready")
        pre_ready, act_ready, t_ready, t_copied = (m.sem(x) for x in ("pre_ready", "act_ready", "t_ready", "t_copied"))
        h_ready, o_ready, row_ready, stored = (m.sem(x) for x in ("h_ready", "o_ready", "row_ready", "stored"))
        block = stack.enter_context(nc.Block())

        @block.sync
        def _(sp):
            for dst, src in ((w0, w["w0"].rearrange("a n -> (a n)")), (b0, w["b0"]), (g0, w["g0"]), (b1, w["b1"]), (g1, w["g1"])):
                sp.dma_start(dst[:], row(src)).then_inc(loaded, 16)
            sp.dma_start(w1[:], w["w1"].rearrange("(k p) n -> p k n", p=P)).then_inc(loaded, 16)
            sp.dma_start(w2[:], w["w2"].rearrange("(k p) n -> p k n", p=P)).then_inc(loaded, 16)
            sp.dma_start(b2[:], w["b2"].rearrange("(n a) -> n a", a=1)).then_inc(loaded, 16)
            sp.wait_ge(row_ready, 2)
            sp.dma_start(rev, out_row[:]).then_inc(stored, 16)
            sp.wait_ge(stored, 16)
            sp.dma_start(band, bass.AP(tensor=rev.tensor, offset=P - 1, ap=[[REV, H], [-1, P], [1, S]])).then_inc(stored, 16)
            sp.wait_ge(stored, 32)

        @block.gpsimd
        def _(pool):
            pool.iota(dist_i[:], pattern=[[-P, QT]], base=S - 1, channel_multiplier=-1).then_inc(dist_made, 1)
            for n in range(2):
                pool.wait_ge(mv_ready, QT * (n + 1))
                inverse_root(pool, c, mv[:, :, 1], ALU.add, EPS, rooting, n + 1, rstd_ready)

        @block.vector
        def _(dve):
            linked, rooted = [0], [0]

            def link(ins):
                linked[0] += 1
                ins.then_inc(link_s, 1)
                dve.wait_ge(link_s, linked[0])

            def normed(g):
                for t in range(QT):
                    nc.vector.bn_stats(stats[:, t, :], hid[:, t, :]).then_inc(link_s, 1)
                linked[0] += QT
                dve.wait_ge(link_s, linked[0])
                for t in range(QT):
                    nc.vector.bn_aggr(mv[:, t, :], stats[:, t, :]).then_inc(mv_ready, 1)
                rooted[0] += 1
                dve.wait_ge(rstd_ready, rooted[0])
                for t in range(QT):
                    nc.vector.tensor_scalar(hid[:, t, :], hid[:, t, :], mv[:, t, 0:1], mv[:, t, 1:2],
                                            ALU.subtract, ALU.mult).then_inc(link_s, 1)
                linked[0] += QT
                dve.wait_ge(link_s, linked[0])
                nc.vector.tensor_tensor(hid[:], hid[:], g[:].unsqueeze(1).to_broadcast([P, QT, D]), ALU.mult).then_inc(pre_ready, 1)

            dve.wait_ge(dist_made, 1)
            link(nc.vector.tensor_copy(dist[:], dist_i[:]))
            dve.wait_ge(loaded, 16 * 8)
            for t in range(QT):
                nc.vector.scalar_tensor_tensor(out=hid[:, t, :], in0=w0[:], scalar=dist[:, t:t + 1], in1=b0[:],
                                               op0=ALU.mult, op1=ALU.add).then_inc(link_s, 1)
            linked[0] += QT
            dve.wait_ge(link_s, linked[0])
            normed(g0)
            for k in range(KD):
                dve.wait_ge(t_ready, 1)
                nc.vector.tensor_copy(act_t[:, k, :], t_ps[:, k, :]).then_inc(t_copied, 1)
            dve.wait_ge(h_ready, 1)
            dve.wait_ge(act_ready, 1)
            link(nc.vector.tensor_tensor(hid[:], h_ps[:], b1[:].unsqueeze(1).to_broadcast([P, QT, D]), ALU.add))
            normed(g1)
            dve.wait_ge(t_ready, 2)
            for k in range(KD):
                nc.vector.tensor_copy(act_t[:, k, :], t_ps[:, k, :]).then_inc(t_copied, 1)
            nc.vector.memset(out_row[:, S:REV], NEG).then_inc(row_ready, 1)
            dve.wait_ge(o_ready, 1)
            nc.vector.tensor_scalar(out_row[:, 0:S], o_ps[0:H, :], b2[:, 0:1], None, ALU.add).then_inc(row_ready, 1)

        @block.scalar
        def _(a):
            for n in range(2):
                a.wait_ge(pre_ready, n + 1)
                if n:
                    a.wait_ge(t_ready, n)
                nc.scalar.activation(act[:], hid[:], ACT.Silu).then_inc(act_ready, 1)

        @block.tensor
        def _(pe):
            for n in range(2):
                pe.wait_ge(act_ready, n + 1)
                if n:
                    pe.wait_ge(t_copied, KD)
                for k in range(KD):
                    for t in range(QT):
                        last = nc.tensor.transpose(t_ps[:, k, t * P:(t + 1) * P], act[:, t, k * P:(k + 1) * P], c.ident[:])
                last.then_inc(t_ready, 1)
                pe.wait_ge(t_copied, KD * (n + 1))
                if n == 0:
                    pe.wait_ge(loaded, 16 * 8)
                    for t in range(QT):
                        for k in range(KD):
                            last = nc.tensor.matmul(h_ps[:, t, :], act_t[:, k, t * P:(t + 1) * P], w1[:, k, :],
                                                    start=(k == 0), stop=(k == KD - 1))
                    last.then_inc(h_ready, 1)
                else:
                    for k in range(KD):
                        last = nc.tensor.matmul(o_ps[0:H, :], w2[:, k, :], act_t[:, k, :], start=(k == 0), stop=(k == KD - 1))
                    last.then_inc(o_ready, 1)


def attention_inputs(nc, c, l, w, cond, mask, x_in=None):
    cosine = l != 0
    with ExitStack() as stack:
        m = Memory(nc, stack, f"in{l}")
        g = m.sb("g", [P, KD])
        wkv = m.sb("wkv", [P, KD, 2 * DH])
        mask_w = m.sb("mask_w", [1, T // 4], mybir.dt.uint32)
        mask_u = mask_w[:].bitcast(U8)
        null_k = m.sb("null_k", [1, DH])
        qs, ks = m.sb("qs", [P, DH]), m.sb("ks", [P, DH])
        stats, mv = m.sb("stats", [P, QT, 6]), m.sb("mv", [P, QT, 2])
        xn = m.sb("xn", [P, 2, QT, D])
        kf, ksq, kn = m.sb("kf", [P, QT, DH]), m.sb("ksq", [P, QT, DH]), m.sb("kn", [P, QT])
        kdup = m.sb("kdup", [P, QT, 2, DH])
        nsq, nn, nkdup = m.sb("nsq", [1, DH]), m.sb("nn", [1, 1]), m.sb("nkdup", [1, 2, DH])
        x_ps = [m.ps(f"x_ps{n}", [P, KD, S]) for n in range(2)]
        kv_ps = m.ps("kv_ps", [P, QT, 2 * DH])
        kt_ps = m.ps("kt_ps", [P, S])
        nk_ps = m.ps("nk_ps", [P, 1])
        loaded, cleared, link_s = m.sem("loaded"), m.sem("cleared"), m.sem("link")
        x_loaded = [m.sem(f"x_loaded{b}") for b in range(B)]
        xn_ready, xt_ready, xt_copied = m.sem("xn_ready"), m.sem("xt_ready"), m.sem("xt_copied")
        kv_ready, kv_read, kdup_ready = m.sem("kv_ready"), m.sem("kv_read"), m.sem("kdup_ready")
        kt_ready, kt_copied, null_ready, nk_ready, nk_copied = (m.sem(s) for s in ("kt_ready", "kt_copied", "null_ready", "nk_ready", "nk_copied"))
        done, mv_ready, rooting, rstd_ready, square_ready, floored, root_ready = (m.sem(s) for s in ("done", "mv_ready", "rooting", "rstd_ready", "square_ready", "floored", "root_ready"))
        block = stack.enter_context(nc.Block())
        n_loads = 6 + (2 if cosine else 0)

        @block.sync
        def _(sp):
            if x_in is not None:
                for b in range(B):
                    sp.dma_start(c.x[:, QT * b:QT * (b + 1), :], x_in[b].rearrange("(t p) d -> p t d", p=P)).then_inc(x_loaded[b], 16)
            sp.dma_start(g[:], w["g"].rearrange("(k p) -> p k", p=P)).then_inc(loaded, 16)
            sp.dma_start(wkv[:], w["Wkv"].rearrange("(k p) n -> p k n", p=P)).then_inc(loaded, 16)
            sp.dma_start(mask_w[:], mask.rearrange("b s -> (b s)").rearrange("(a n) -> a n", a=1)).then_inc(loaded, 16)
            sp.dma_start(null_k[:], cond[0:1, :]).then_inc(loaded, 16)
            if cosine:
                sp.dma_start(qs[:], row(w["q_scale"])).then_inc(loaded, 16)
                sp.dma_start(ks[:], row(w["k_scale"])).then_inc(loaded, 16)
            sp.dma_start(c.null_bias[:], row(w["null_attn_bias"])).then_inc(loaded, 16)
            sp.dma_start(c.wq[:, :, 0:H * DH], w["Wq"].rearrange("(k p) n -> p k n", p=P)).then_inc(loaded, 16)

        @block.gpsimd
        def _(pool):
            pool.memset(c.kt[:], 0.0).then_inc(cleared, 1)
            pool.memset(c.kmask[:], 0.0).then_inc(cleared, 1)
            pool.memset(c.wq[:, :, H * DH:], 0.0).then_inc(done, 1)

            def root(n, t):
                pool.wait_ge(square_ready, n)
                inverse_root(pool, c, t[:], ALU.max, 1e-24, floored, n, root_ready)

            for b in range(B + 1):
                if b < B:
                    pool.wait_ge(mv_ready, QT * (b + 1))
                    inverse_root(pool, c, mv[:, :, 1], ALU.add, EPS, rooting, b + 1, rstd_ready)
                if cosine and b == 0:
                    root(1, nn)
                if cosine and b >= 1:
                    root(b + 1, kn)
            pool.wait_ge(done, 1)

        @block.vector
        def _(dve):
            linked = [0]

            def link(ins):
                linked[0] += 1
                ins.then_inc(link_s, 1)
                dve.wait_ge(link_s, linked[0])

            def null_and_mask():
                dve.wait_ge(loaded, 16 * n_loads)
                dve.wait_ge(cleared, 2)
                link(nc.vector.tensor_scalar(c.kmask[0:1, :, 1:], mask_u.rearrange("a (b s) -> a b s", b=B), 1.0, -NEG,
                                             ALU.subtract, ALU.mult))
                pair = null_k[:].unsqueeze(1).to_broadcast([1, 2, DH])
                if cosine:
                    link(nc.vector.scalar_tensor_tensor(out=ks[:], in0=qs[:], scalar=8.0, in1=ks[:], op0=ALU.mult, op1=ALU.mult))
                    link(nc.vector.tensor_tensor(nsq[:], null_k[:], null_k[:], ALU.mult))
                    nc.vector.tensor_reduce(nn[:], nsq[:], AX.X, ALU.add).then_inc(square_ready, 1)
                    dve.wait_ge(root_ready, 1)
                    link(nc.vector.tensor_scalar(null_k[:], null_k[:], nn[:, 0:1], None, ALU.mult))
                    nc.vector.tensor_tensor(nkdup[:], pair, ks[0:1, :].unsqueeze(1).to_broadcast([1, 2, DH]), ALU.mult).then_inc(null_ready, 1)
                else:
                    nc.vector.tensor_scalar(nkdup[:], pair, DH ** -0.5, None, ALU.mult).then_inc(null_ready, 1)

            def layernorm(b):
                tiles = c.x[:, QT * b:QT * (b + 1), :]
                if x_in is not None:
                    dve.wait_ge(x_loaded[b], 16)
                for t in range(QT):
                    nc.vector.bn_stats(stats[:, t, :], tiles[:, t, :]).then_inc(link_s, 1)
                linked[0] += QT
                dve.wait_ge(link_s, linked[0])
                for t in range(QT):
                    nc.vector.bn_aggr(mv[:, t, :], stats[:, t, :]).then_inc(mv_ready, 1)
                dve.wait_ge(rstd_ready, b + 1)
                if b >= 2:
                    dve.wait_ge(xt_ready, b - 1)
                for t in range(QT):
                    last = nc.vector.tensor_scalar(xn[:, b % 2, t, :], tiles[:, t, :], mv[:, t, 0:1], mv[:, t, 1:2],
                                                   ALU.subtract, ALU.mult)
                    last.then_inc(xn_ready, 1)

            def keys(b):
                dve.wait_ge(kv_ready, b + 1)
                nc.vector.tensor_copy(c.v[:, QT * b:QT * (b + 1), :], kv_ps[:, :, DH:]).then_inc(kv_read, 1)
                dve.wait_ge(kdup_ready, 2 * b)
                nc.vector.tensor_copy(kf[:], kv_ps[:, :, 0:DH]).then_inc(kv_read, 1)
                dve.wait_ge(kv_read, 2 * (b + 1))
                if cosine:
                    link(nc.vector.tensor_tensor(ksq[:], kf[:], kf[:], ALU.mult))
                    nc.vector.tensor_reduce(kn[:], ksq[:], AX.X, ALU.add).then_inc(square_ready, 1)
                    dve.wait_ge(root_ready, b + 2)
                    link(nc.vector.tensor_tensor(kf[:], kf[:], kn[:].unsqueeze(2).to_broadcast([P, QT, DH]), ALU.mult))
                if b >= 1:
                    dve.wait_ge(kt_ready, b)
                for n in range(2):
                    if cosine:
                        nc.vector.tensor_tensor(kdup[:, :, n, :], kf[:], ks[:].unsqueeze(1).to_broadcast([P, QT, DH]), ALU.mult).then_inc(kdup_ready, 1)
                    else:
                        nc.vector.tensor_scalar(kdup[:, :, n, :], kf[:], DH ** -0.5, None, ALU.mult).then_inc(kdup_ready, 1)

            layernorm(0)
            null_and_mask()
            for b in range(1, B + 1):
                if b < B:
                    layernorm(b)
                keys(b - 1)

        @block.scalar
        def _(a):
            a.wait_ge(loaded, 16 * n_loads)
            a.wait_ge(cleared, 2)
            for b in range(B + 2):
                if b < B:
                    a.wait_ge(xt_ready, b + 1)
                    for k in range(KD):
                        nc.scalar.activation(c.xt[:, k, S * b:S * (b + 1)], x_ps[b % 2][:, k, :], ACT.Copy,
                                             scale=g[:, k:k + 1]).then_inc(xt_copied, 1)
                if b == 1:
                    a.wait_ge(nk_ready, 1)
                    for n in range(2):
                        h = slice(DH * n, DH * (n + 1))
                        nc.scalar.activation(c.kt[h, n, :, 0], nk_ps[h, :].to_broadcast([DH, B]), ACT.Copy).then_inc(nk_copied, 1)
                if b >= 2:
                    a.wait_ge(kt_ready, b - 1)
                    for n in range(2):
                        h = slice(DH * n, DH * (n + 1))
                        nc.scalar.activation(c.kt[h, n, b - 2, 1:], kt_ps[h, :], ACT.Copy).then_inc(kt_copied, 1)
            a.wait_ge(kt_copied, 2 * B)
            a.wait_ge(nk_copied, 2)

        @block.tensor
        def _(pe):
            for b in range(B + 2):
                if b < B:
                    pe.wait_ge(xn_ready, QT * (b + 1))
                    if b >= 2:
                        pe.wait_ge(xt_copied, KD * (b - 1))
                    for k in range(KD):
                        for t in range(QT):
                            last = nc.tensor.transpose(x_ps[b % 2][:, k, t * P:(t + 1) * P], xn[:, b % 2, t, k * P:(k + 1) * P], c.ident[:])
                    last.then_inc(xt_ready, 1)
                if b == 1:
                    pe.wait_ge(null_ready, 1)
                    nc.tensor.matmul(nk_ps[:], nkdup[:].rearrange("a n d -> a (n d)"), c.ident[0:1, 0:1], start=True, stop=True).then_inc(nk_ready, 1)
                if 1 <= b <= B:
                    pe.wait_ge(xt_copied, KD * b)
                    if b == 1:
                        pe.wait_ge(loaded, 16 * n_loads)
                    else:
                        pe.wait_ge(kv_read, 2 * (b - 1))
                    for t in range(QT):
                        tok = slice(S * (b - 1) + t * P, S * (b - 1) + (t + 1) * P)
                        for k in range(KD):
                            last = nc.tensor.matmul(kv_ps[:, t, :], c.xt[:, k, tok], wkv[:, k, :], start=(k == 0), stop=(k == KD - 1))
                    last.then_inc(kv_ready, 1)
                if b >= 2:
                    pe.wait_ge(kdup_ready, 2 * (b - 1))
                    if b >= 3:
                        pe.wait_ge(kt_copied, 2 * (b - 2))
                    for t in range(QT):
                        last = nc.tensor.transpose(kt_ps[:, t * P:(t + 1) * P], kdup[:, t, :, :].rearrange("p n d -> p (n d)"), c.ident[:])
                    last.then_inc(kt_ready, 1)


def rounds(engine, n, one):
    one(0, True, False)
    with engine.Fori(1, n - 1) as i:
        one(i, False, False)
    one(n - 1, False, True)


def counted(engine, value):
    return value if isinstance(value, int) else engine.to_reg(value)


def attention(nc, c, l, bias_of, causal_select):
    cosine = l != 0
    U = QT * B * 2
    SU = B * 2
    N = 4
    DRAIN = 6
    with ExitStack() as stack:
        m = Memory(nc, stack, f"att{l}")
        bias = [[m.sb(f"bias{hh}{q}", [P, NKEY[q]]) for q in range(QT)] for hh in range(2)]
        q_sb = m.sb("q_sb", [P, B, 2, DH])
        sq = m.sb("sq", [P, B, 2, DH]) if cosine else None
        qn = m.sb("qn", [P, B, 2])
        q_t = [m.sb(f"q_t{n}", [P, B, P]) for n in range(2)]
        sc = [c.h[:, QT * n:QT * (n + 1), :].rearrange("p t d -> p (t d)") for n in range(N)]
        pr = [m.sb(f"pr{n}", [P, NKEY[-1]]) for n in range(N)]
        pt = [m.sb(f"pt{n}", [P, S]) for n in range(N)]
        nmax, rsum = m.sb("nmax", [P, 2, SU]), m.sb("rsum", [P, 2, SU])
        pnull = m.sb("pnull", [P, 2, SU])
        rinv = m.sb("rinv", [P, 2, SU])
        rexp = m.sb("rexp", [P, B, 2, DH])
        rb_sb = m.sb("rb_sb", [P, B, P])
        s_ps = m.ps("s_ps", [P, 4 * 512])
        rb_ps = s_ps[:, 768:768 + B * P]
        pt_ps = [m.ps(f"pt_ps{n}", [P, S]) for n in range(2)]
        o_ps = m.ps("o_ps", [P, B, P])
        q_ps = m.ps("q_ps", [P, B, P])
        bias_loaded = [[m.sem(f"bias_loaded{hh}{q}") for q in range(QT)] for hh in range(2)]
        names = ("bias_ready s_ready s_read p_ready pt_ready pt_copied_a pt_copied_v pv_done q_ready q_squared q_kept "
                 "qt_ready qt_copied rinv_ready rexp_ready rb_ready rb_copied out_ready null_kept null_out qn_summed qn_floored qn_ready").split()
        (bias_ready, s_ready, s_read, p_ready, pt_ready, pt_copied_a, pt_copied_v, pv_done, q_ready, q_squared, q_kept,
         qt_ready, qt_copied, rinv_ready, rexp_ready, rb_ready, rb_copied, out_ready, null_kept, null_out, qn_summed, qn_floored, qn_ready) = (m.sem(x) for x in names)
        block = stack.enter_context(nc.Block())
        units = [(u // SU, (u % SU) // 2, u % 2) for u in range(U)]

        def scores_ap(u, q):
            first = ((512 - 257) if u % 2 == 0 else 1024 + 256) if q == QT - 1 else (0, 3 * 512)[u % 2]
            return s_ps[:, first:first + NKEY[q]]

        @block.sync
        def _(sp):
            def load(i, hh, q):
                sp.dma_start(bias[hh][q][:, 1:], bias_of(i, hh, q)).then_inc(bias_loaded[hh][q], 16)

            for q in range(QT):
                for hh in range(2):
                    load(0, hh, q)
            with sp.Fori(0, HP - 1) as i:
                for q in range(QT):
                    uses = sp.to_reg(i * U + SU * (q + 1))
                    sp.wait_ge(s_read, 1)
                    sp.wait_ge(s_read, uses)
                    for hh in range(2):
                        load(i + 1, hh, q)

        @block.gpsimd
        def _(pool):
            def finish_bias(i, q):
                for hh in range(2):
                    loads = counted(pool, i * 16 + 16)
                    pool.wait_ge(bias_loaded[hh][q], 16)
                    pool.wait_ge(bias_loaded[hh][q], loads)
                    if causal_select:
                        diag = bias[hh][q][:, 1 + P * q:1 + P * (q + 1)]
                        pool.affine_select(out=diag, in_=diag, compare_op=ALU.is_ge, fill=NEG, base=0,
                                           pattern=[[-1, P]], channel_multiplier=1).then_inc(bias_ready, 1)
                    pool.tensor_copy(bias[hh][q][:, 0:1], c.null_bias[:, ds(i * 2 + hh, 1)]).then_inc(bias_ready, 1)

            def root_q(n):
                if cosine:
                    sums = counted(pool, n + 1)
                    pool.wait_ge(qn_summed, 1)
                    pool.wait_ge(qn_summed, sums)
                    inverse_root(pool, c, qn[:], ALU.max, 1e-24, qn_floored, n + 1, qn_ready)

            def one(i, first, last):
                for u in range(U + (DRAIN if last else 0)):
                    q, at = u // SU, u % SU
                    more = u < U and not (last and q == QT - 1)
                    if u < U:
                        if at == 0 and not (first and q < 2):
                            pool.wait_ge(null_out, i * QT + q - 1)
                        if at == 1 and more:
                            finish_bias(i + (q + 1) // QT, (q + 1) % QT)
                        if at == 2 and more:
                            root_q(i * QT + (q + 1))
                        made = counted(pool, i * U + u + 1)
                        pool.wait_ge(p_ready, 1)
                        pool.wait_ge(p_ready, made)
                        pool.tensor_copy(pnull[:, q % 2, at:at + 1], pr[u % N][:, 0:1]).then_inc(null_kept, 1)
                    if at == 5 and not (first and q == 0):
                        p, half = q - 1, (q - 1) % 2
                        pool.wait_ge(rinv_ready, i * QT + q)
                        pool.wait_ge(null_kept, i * U + SU * q)
                        pool.tensor_tensor(c.p_null[:, :, p % QT, ds((i + p // QT) * 2, 2)],
                                           pnull[:, half, :].rearrange("p (b n) -> p b n", n=2),
                                           rinv[:, half, :].rearrange("p (b n) -> p b n", n=2), ALU.mult).then_inc(null_out, 1)

            root_q(0)
            finish_bias(0, 0)
            rounds(pool, HP, one)
            pool.wait_ge(null_out, HP * QT)

        per_step_bias = 4 if causal_select else 2

        @block.vector
        def _(dve):
            def sum_q(n):
                if cosine:
                    dve.wait_ge(q_squared, n + 1)
                    nc.vector.tensor_reduce(qn[:], sq[:], AX.X, ALU.add).then_inc(qn_summed, 1)

            def keep_q(n):
                if cosine:
                    dve.wait_ge(qn_ready, n + 1)
                    nc.vector.tensor_tensor(q_sb[:], q_ps[:].rearrange("p b (n d) -> p b n d", n=2),
                                            qn[:].unsqueeze(3).to_broadcast([P, B, 2, DH]), ALU.mult).then_inc(q_kept, 1)

            def one(i, first, last):
                for u in range(U + (DRAIN if last else 0)):
                    q, at = u // SU, u % SU
                    more = u < U and not (last and q == QT - 1)
                    if u < U:
                        hh = units[u][2]
                        if at == 0:
                            biases = counted(dve, i * (QT * per_step_bias) + per_step_bias * (q + 1))
                        scored, read = counted(dve, i * U + u + 1), counted(dve, i * U + u - N + 1)
                        dve.wait_ge(s_ready, 1)
                        if at == 0:
                            dve.wait_ge(bias_ready, biases)
                        dve.wait_ge(s_ready, scored)
                        if not (first and u < N):
                            dve.wait_ge(p_ready, read)
                        nc.vector.tensor_tensor_reduce(sc[u % N][:, 0:NKEY[q]], scores_ap(u, q), bias[hh][q][:], -1.0, 3e38,
                                                       ALU.add, ALU.min, nmax[:, q % 2, at:at + 1]).then_inc(s_read, 1)
                    if at == 2 and more:
                        sum_q(i * QT + (q + 1))
                    if at == 4 and more:
                        keep_q(i * QT + (q + 1))
                    if at == 1 and not (first and q == 0):
                        half = (q - 1) % 2
                        dve.wait_ge(p_ready, i * U + SU * q)
                        if not (first and q < 3):
                            dve.wait_ge(null_out, i * QT + q - 2)
                        nc.vector.reciprocal(rinv[:, half, :], rsum[:, half, :]).then_inc(rinv_ready, 1)
                        dve.wait_ge(rinv_ready, i * QT + q)
                        if not (first and q < 2):
                            dve.wait_ge(rb_ready, i * QT + q - 1)
                        nc.vector.tensor_copy(rexp[:], rinv[:, half, :].rearrange("p (b n) -> p b n", n=2).unsqueeze(3)
                                              .to_broadcast([P, B, 2, DH])).then_inc(rexp_ready, 1)
                    v = u - 3
                    if v % 2 and v < U and not (first and v < 0):
                        n = P * (v % U // SU + 1)
                        dve.wait_ge(pt_ready, i * U + v + 1)
                        if not (first and v < N):
                            dve.wait_ge(pv_done, i * (U // 2) + v // 2 - 1)
                        nc.vector.tensor_copy(pt[v % N][:, 0:n], pt_ps[v % 2][:, 0:n]).then_inc(pt_copied_v, 1)
                    if at == 4 and not (first and q == 0):
                        p = q - 1
                        dve.wait_ge(rb_copied, i * QT + q)
                        dve.wait_ge(pv_done, i * (U // 2) + B * q)
                        nc.vector.tensor_tensor(c.out_t[:, ds(i + p // QT, 1), :].rearrange("p a (b q s) -> p (a b) q s", b=B, q=QT)[:, :, p % QT, :],
                                                o_ps[:], rb_sb[:], ALU.mult).then_inc(out_ready, 1)

            sum_q(0)
            keep_q(0)
            rounds(dve, HP, one)
            dve.wait_ge(out_ready, HP * QT)

        @block.scalar
        def _(a):
            def take_q(n):
                a.wait_ge(q_ready, n + 1)
                if cosine:
                    nc.scalar.activation(sq[:], q_ps[:].rearrange("p b (n d) -> p b n d", n=2), ACT.Square).then_inc(q_squared, 1)
                else:
                    nc.scalar.activation(q_sb[:], q_ps[:].rearrange("p b (n d) -> p b n d", n=2), ACT.Copy).then_inc(q_kept, 1)

            def take_qt(n, half):
                a.wait_ge(qt_ready, n + 1)
                nc.scalar.activation(q_t[half][:], q_ps[:], ACT.Copy).then_inc(qt_copied, 1)

            def one(i, first, last):
                for u in range(U + (DRAIN if last else 0)):
                    q, at = u // SU, u % SU
                    more = u < U and not (last and q == QT - 1)
                    if u < U:
                        a.wait_ge(s_read, i * U + u + 1)
                        if not (first and u < N):
                            a.wait_ge(null_kept, i * U + u - N + 1)
                            a.wait_ge(pt_ready, i * U + u - N + 1)
                        nc.scalar.activation(pr[u % N][:, 0:NKEY[q]], sc[u % N][:, 0:NKEY[q]], ACT.Exp, scale=-1.0,
                                             bias=nmax[:, q % 2, at:at + 1],
                                             accum_out=rsum[:, q % 2, at:at + 1]).then_inc(p_ready, 1)
                    if at == 1 and more:
                        take_q(i * QT + (q + 1))
                    if at == 6 and more:
                        take_qt(i * QT + (q + 1), (q + 1) % 2)
                    v = u - 3
                    if v % 2 == 0 and v < U and not (first and v < 0):
                        n = P * (v % U // SU + 1)
                        a.wait_ge(pt_ready, i * U + v + 1)
                        if not (first and v < N):
                            a.wait_ge(pv_done, i * (U // 2) + v // 2 - 1)
                        nc.scalar.activation(pt[v % N][:, 0:n], pt_ps[v % 2][:, 0:n], ACT.Copy).then_inc(pt_copied_a, 1)
                    if at == 2 and not (first and q == 0):
                        a.wait_ge(rb_ready, i * QT + q)
                        if not (first and q < 2):
                            a.wait_ge(out_ready, i * QT + q - 1)
                        nc.scalar.activation(rb_sb[:].rearrange("p b n -> p (b n)"), rb_ps, ACT.Copy).then_inc(rb_copied, 1)

            take_q(0)
            take_qt(0, 0)
            rounds(a, HP, one)

        @block.tensor
        def _(pe):
            def project_q(i, q):
                for b in range(B):
                    tok = slice(S * b + P * q, S * b + P * (q + 1))
                    for k in range(KD):
                        last = nc.tensor.matmul(q_ps[:, b, :], c.xt[:, k, tok], c.wq[:, k, ds(i * P, P)], start=(k == 0), stop=(k == KD - 1))
                last.then_inc(q_ready, 1)

            def turn_q(n):
                pe.wait_ge(q_kept, n + 1)
                for b in range(B):
                    last = nc.tensor.transpose(q_ps[:, b, :], q_sb[:, b, :, :].rearrange("p n d -> p (n d)"), c.ident[:])
                last.then_inc(qt_ready, 1)

            def one(i, first, last_round):
                for u in range(U + (DRAIN if last_round else 0)):
                    q, at = u // SU, u % SU
                    more = u < U and not (last_round and q == QT - 1)
                    if u < U:
                        _, b, hh = units[u]
                        if at == 0:
                            pe.wait_ge(qt_copied, i * QT + q + 1)
                        if not (first and u < 2):
                            pe.wait_ge(s_read, i * U + u - 1)
                        if q == QT - 1 and at == 3:
                            pe.wait_ge(rb_copied, i * QT + q)
                        out = scores_ap(u, q)
                        cuts = [0, 257 - u % 2, NKEY[q]] if q == QT - 1 else [0, NKEY[q]]
                        for lo, hi in zip(cuts, cuts[1:]):
                            nc.tensor.matmul(out[:, lo:hi], c.row0[:], c.kmask[:, b, lo:hi], start=True, stop=False)
                            last = nc.tensor.matmul(out[:, lo:hi], q_t[q % 2][:, b, :], c.kt[:, hh, b, lo:hi], start=False, stop=True)
                        last.then_inc(s_ready, 1)
                    if at == 0 and more:
                        project_q(i + (q + 1) // QT, (q + 1) % QT)
                    v = u - 2
                    if v < U and not (first and v < 0):
                        pe.wait_ge(p_ready, i * U + v + 1)
                        if not (first and v < 2):
                            pe.wait_ge(pt_copied_v if v % 2 else pt_copied_a, i * (U // 2) + v // 2)
                        for kb in range(v % U // SU + 1):
                            last = nc.tensor.transpose(pt_ps[v % 2][:, P * kb:P * (kb + 1)], pr[v % N][:, 1 + P * kb:1 + P * (kb + 1)], c.ident[:])
                        last.then_inc(pt_ready, 1)
                    v = u - 4
                    if v % 2 and v < U and not (first and v < 0):
                        qv, bv, _ = units[v % U]
                        pe.wait_ge(pt_copied_a, i * (U // 2) + v // 2 + 1)
                        pe.wait_ge(pt_copied_v, i * (U // 2) + v // 2 + 1)
                        if v % SU == 1 and not (first and v < SU):
                            pe.wait_ge(out_ready, i * QT + v // SU)
                        for kb in range(qv + 1):
                            for hv in range(2):
                                last = nc.tensor.matmul(o_ps[DH * hv:DH * (hv + 1), bv, :], c.v[:, QT * bv + kb, :],
                                                        pt[(v - 1 + hv) % N][:, P * kb:P * (kb + 1)], start=(kb == 0), stop=(kb == qv))
                        last.then_inc(pv_done, 1)
                    if at == 5 and more:
                        turn_q(i * QT + q + 1)
                    if at == 2 and not (first and q == 0):
                        pe.wait_ge(rexp_ready, i * QT + q)
                        if q == QT - 1:
                            pe.wait_ge(s_read, i * U + u + 1)
                        if not (first and q < 2):
                            pe.wait_ge(rb_copied, i * QT + q - 1)
                        for b in range(B):
                            last = nc.tensor.transpose(rb_ps[:, P * b:P * (b + 1)], rexp[:, b, :, :].rearrange("p n d -> p (n d)"), c.ident[:])
                        last.then_inc(rb_ready, 1)

            project_q(0, 0)
            turn_q(0)
            rounds(pe, HP, one)


def attention_output(nc, c, l, w_out, g_out, cond):
    with ExitStack() as stack:
        m = Memory(nc, stack, f"out{l}")
        wo = m.sb("wo", [P, HP, D])
        g = m.sb("g", [P, D])
        null_v = m.sb("null_v", [P, 1])
        null_cols = m.sb("null_cols", [P, HP, H])
        null_w = m.sb("null_w", [H, D])
        pn_t = m.sb("pn_t", [H, 2, S])
        yn = m.sb("yn", [P, 2, QT, D])
        stats, mv = m.sb("stats", [P, QT, 6]), m.sb("mv", [P, QT, 2])
        y_ps = [m.ps(f"y_ps{n}", [P, QT, D]) for n in range(2)]
        pn_ps = m.ps("pn_ps", [P, S])
        nw_ps = m.ps("nw_ps", [P, D])
        loaded, cleared, cols_ready, nw_ready, nw_copied = (m.sem(x) for x in ("loaded", "cleared", "cols_ready", "nw_ready", "nw_copied"))
        pn_ready, pn_copied, y_ready, yn_ready, h_ready, link_s = (m.sem(x) for x in ("pn_ready", "pn_copied", "y_ready", "yn_ready", "h_ready", "link"))
        mv_ready, rooting, rstd_ready = m.sem("mv_ready"), m.sem("rooting"), m.sem("rstd_ready")
        block = stack.enter_context(nc.Block())

        @block.sync
        def _(sp):
            sp.dma_start(wo[:], w_out.rearrange("(c p) n -> p c n", p=P)).then_inc(loaded, 16)
            sp.dma_start(g[:], row(g_out)).then_inc(loaded, 16)
            for n in range(2):
                sp.dma_start(null_v[DH * n:DH * (n + 1), :], cond[1:2, :].rearrange("a d -> d a")).then_inc(loaded, 16)

        @block.gpsimd
        def _(pool):
            pool.memset(null_cols[:], 0.0).then_inc(cleared, 1)
            pool.wait_ge(loaded, 64)
            for b in range(B):
                pool.wait_ge(mv_ready, QT * (b + 1))
                inverse_root(pool, c, mv[:, :, 1], ALU.add, EPS, rooting, b + 1, rstd_ready)
                pool.wait_ge(yn_ready, QT * (b + 1))
                pool.tensor_tensor(c.h[:, QT * b:QT * (b + 1), :], yn[:, b % 2, :, :], g[:].unsqueeze(1).to_broadcast([P, QT, D]),
                                   ALU.mult).then_inc(h_ready, 1)
            pool.wait_ge(h_ready, B)

        @block.scalar
        def _(a):
            a.wait_ge(nw_ready, 1)
            nc.scalar.activation(null_w[:], nw_ps[0:H, :], ACT.Copy).then_inc(nw_copied, 1)
            for b in range(B):
                a.wait_ge(pn_ready, b + 1)
                if b >= 2:
                    a.wait_ge(y_ready, b - 1)
                nc.scalar.activation(pn_t[:, b % 2, :], pn_ps[0:H, :], ACT.Copy).then_inc(pn_copied, 1)

        @block.vector
        def _(dve):
            linked = [0]

            def link(ins):
                linked[0] += 1
                ins.then_inc(link_s, 1)
                dve.wait_ge(link_s, linked[0])

            dve.wait_ge(loaded, 64)
            dve.wait_ge(cleared, 1)
            flat = null_cols[:].rearrange("p c h -> p (c h)")
            for n in range(2):
                rows = slice(DH * n, DH * (n + 1))
                nc.vector.tensor_copy(flat[rows, n:n + (H + 2) * (HP - 1) + 1:H + 2], null_v[rows, :].to_broadcast([DH, HP])).then_inc(cols_ready, 1)
            for b in range(B):
                dve.wait_ge(y_ready, b + 1)
                for t in range(QT):
                    nc.vector.bn_stats(stats[:, t, :], y_ps[b % 2][:, t, :]).then_inc(link_s, 1)
                linked[0] += QT
                dve.wait_ge(link_s, linked[0])
                for t in range(QT):
                    nc.vector.bn_aggr(mv[:, t, :], stats[:, t, :]).then_inc(mv_ready, 1)
                dve.wait_ge(rstd_ready, b + 1)
                if b >= 2:
                    dve.wait_ge(h_ready, b - 1)
                for t in range(QT):
                    nc.vector.tensor_scalar(yn[:, b % 2, t, :], y_ps[b % 2][:, t, :], mv[:, t, 0:1], mv[:, t, 1:2],
                                            ALU.subtract, ALU.mult).then_inc(yn_ready, 1)

        @block.tensor
        def _(pe):
            pe.wait_ge(loaded, 64)
            pe.wait_ge(cols_ready, 2)
            for p in range(HP):
                last = nc.tensor.matmul(nw_ps[0:H, :], null_cols[:, p, :], wo[:, p, :], start=(p == 0), stop=(p == HP - 1))
            last.then_inc(nw_ready, 1)
            for b in range(B):
                if b >= 1:
                    pe.wait_ge(pn_copied, b)
                for q in range(QT):
                    last = nc.tensor.transpose(pn_ps[0:H, P * q:P * (q + 1)], c.p_null[:, b, q, :], c.ident[:])
                last.then_inc(pn_ready, 1)
                if b >= 2:
                    pe.wait_ge(yn_ready, QT * (b - 1))
                if b == 0:
                    pe.wait_ge(nw_copied, 1)
                pe.wait_ge(pn_copied, b + 1)
                for q in range(QT):
                    for p in range(HP):
                        nc.tensor.matmul(y_ps[b % 2][:, q, :], c.out_t[:, p, S * b + P * q:S * b + P * (q + 1)], wo[:, p, :],
                                         start=(p == 0), stop=False)
                    last = nc.tensor.matmul(y_ps[b % 2][:, q, :], pn_t[:, b % 2, P * q:P * (q + 1)], null_w[:], start=False, stop=True)
                last.then_inc(y_ready, 1)


def ternary_linear(nc, c, weight):
    with ExitStack() as stack:
        m = Memory(nc, stack, "ter")
        w = m.sb("w", [P, KD, D])
        w_t = m.sb("w_t", [P, KD, D])
        part, scale = m.sb("part", [P, 1]), m.sb("scale", [P, 1])
        h_t = m.sb("h_t", [P, 2, KD, S])
        s_ps = m.ps("s_ps", [P, 1])
        h_ps = m.ps("h_ps", [P, KD, S])
        y_ps = [m.ps(f"y_ps{n}", [P, QT, D]) for n in range(2)]
        names = "loaded part_ready sum_ready scale_ready w_ready wt_ready wt_copied ht_ready ht_copied y_ready x_ready link".split()
        (loaded, part_ready, sum_ready, scale_ready, w_ready, wt_ready, wt_copied, ht_ready, ht_copied, y_ready, x_ready, link_s) = (m.sem(x) for x in names)
        block = stack.enter_context(nc.Block())
        ROUND = 12582912.0

        @block.sync
        def _(sp):
            sp.dma_start(w[:], weight.rearrange("(k p) n -> p k n", p=P)).then_inc(loaded, 16)

        @block.vector
        def _(dve):
            linked = [0]

            def link(ins):
                linked[0] += 1
                ins.then_inc(link_s, 1)
                dve.wait_ge(link_s, linked[0])

            dve.wait_ge(loaded, 16)
            nc.vector.tensor_reduce(part[:], w[:], AX.XY, ALU.add, apply_absolute_value=True).then_inc(part_ready, 1)
            dve.wait_ge(sum_ready, 1)
            link(nc.vector.tensor_scalar(scale[:], s_ps[:], 1.0 / (D * D), EPS, ALU.mult, ALU.max))
            link(nc.vector.reciprocal(part[:], scale[:]))
            link(nc.vector.tensor_scalar(w[:], w[:], part[:, 0:1], ROUND, ALU.mult, ALU.add))
            link(nc.vector.tensor_scalar(w[:], w[:], ROUND, -1.0, ALU.subtract, ALU.max))
            nc.vector.tensor_scalar(w[:], w[:], 1.0, None, ALU.min).then_inc(w_ready, 1)
            for b in range(B):
                dve.wait_ge(y_ready, b + 1)
                nc.vector.scalar_tensor_tensor(out=c.x[:, QT * b:QT * (b + 1), :], in0=y_ps[b % 2][:], scalar=scale[:, 0:1],
                                               in1=c.x[:, QT * b:QT * (b + 1), :], op0=ALU.mult, op1=ALU.add).then_inc(x_ready, 1)
            dve.wait_ge(x_ready, B)

        @block.scalar
        def _(a):
            a.wait_ge(wt_ready, 1)
            for k in range(KD):
                nc.scalar.activation(w_t[:, k, :], h_ps[:, k, 0:D], ACT.Copy).then_inc(wt_copied, 1)
            for b in range(B):
                a.wait_ge(ht_ready, b + 1)
                if b >= 2:
                    a.wait_ge(y_ready, b - 1)
                for k in range(KD):
                    nc.scalar.activation(h_t[:, b % 2, k, :], h_ps[:, k, :], ACT.Copy).then_inc(ht_copied, 1)

        @block.tensor
        def _(pe):
            pe.wait_ge(part_ready, 1)
            nc.tensor.matmul(s_ps[:], c.ones_f[:], part[:], start=True, stop=True).then_inc(sum_ready, 1)
            pe.wait_ge(w_ready, 1)
            for k in range(KD):
                for o in range(KD):
                    last = nc.tensor.transpose(h_ps[:, k, P * o:P * (o + 1)], w[:, o, P * k:P * (k + 1)], c.ident[:])
            last.then_inc(wt_ready, 1)
            pe.wait_ge(wt_copied, KD)
            for b in range(B):
                if b >= 1:
                    pe.wait_ge(ht_copied, KD * b)
                for k in range(KD):
                    for t in range(QT):
                        last = nc.tensor.transpose(h_ps[:, k, P * t:P * (t + 1)], c.h[:, QT * b + t, P * k:P * (k + 1)], c.ident[:])
                last.then_inc(ht_ready, 1)
                pe.wait_ge(ht_copied, KD * (b + 1))
                if b >= 2:
                    pe.wait_ge(x_ready, b - 1)
                for t in range(QT):
                    for k in range(KD):
                        last = nc.tensor.matmul(y_ps[b % 2][:, t, :], h_t[:, b % 2, k, P * t:P * (t + 1)], w_t[:, k, :],
                                                start=(k == 0), stop=(k == KD - 1))
                last.then_inc(y_ready, 1)


class Shared:
    pass


def shared(nc, stack):
    c = Shared()
    m = Memory(nc, stack, "all")
    c.ident, c.ones_f, c.minus_half = m.sb("ident", [P, P]), m.sb("ones_f", [P, P]), m.sb("minus_half", [P, 1])
    c.before, c.row0, c.ones_b = m.sb("before", [P, P], BF16), m.sb("row0", [P, P], BF16), m.sb("ones_b", [P, P], BF16)
    c.x, c.h = m.sb("x", [P, NT, D]), m.sb("h", [P, NT, D])
    c.xt = m.sb("xt", [P, KD, T])
    return c


def attention_memory(nc, stack, c, l):
    m = Memory(nc, stack, f"mem{l}")
    c.kt = m.sb("kt", [P, 2, B, NKEY[-1]])
    c.v = m.sb("v", [P, NT, DH])
    c.wq = m.sb("wq", [P, KD, (HP + 1) * P])
    c.kmask = m.sb("kmask", [P, B, NKEY[-1]], BF16)
    c.null_bias = m.sb("null_bias", [P, H])
    c.p_null = m.sb("p_null", [P, B, QT, H])
    c.out_t = m.sb("out_t", [P, HP, T])


def band_bias(band):
    def bias_of(i, hh, q):
        return band[ds(i * 2 + hh, 1), :, P * (QT - 1 - q):S].rearrange("a p n -> (a p) n")
    return bias_of


class Mixture:

    def __init__(self, name, top, cap, hidden, temperature=1.0, normalised=False, by_rows=False, gate=False):
        self.name, self.top, self.cap, self.hidden = name, top, cap, hidden
        self.temperature, self.normalised, self.by_rows, self.gate = temperature, normalised, by_rows, gate
        self.tiles = E * cap // P if cap else top * NT + E
        self.rows = self.tiles * P


def route(nc, c, mx, src, w_router, sorted_rows, r, ahead, cond=None, w_cond=None):
    with ExitStack() as stack:
        m = Memory(nc, stack, f"route_{mx.name}")
        wr = m.sb("wr", [P, KD, E])
        wr_rows = m.sb("wr_rows", [E, D])
        g_t, wg_t = m.sb("g_t", [DH, B]), m.sb("wg_t", [DH, E])
        lg, ex = m.sb("lg", [P, NT, E]), m.sb("ex", [P, NT, E])
        top = [m.sb(f"top{k}", [P, NT]) for k in range(mx.top)]
        hot = [m.sb(f"hot{k}", [P, NT, E]) for k in range(mx.top)]
        tmp, tmp2, red, total = m.sb("tmp", [P, NT, E]), m.sb("tmp2", [P, NT, E]), m.sb("red", [P, NT]), m.sb("total", [P, NT])
        sel = m.sb("sel", [P, NT + 1, E], BF16)
        desc_i, desc = m.sb("desc_i", [P, E], I32), m.sb("desc", [P, E])
        base_i, base = m.sb("base_i", [P, E], I32), m.sb("base", [P, E])
        edge_i, edge = m.sb("edge_i", [P, NT], I32), m.sb("edge", [P, NT])
        tile_i, tile_n = m.sb("tile_i", [P, mx.tiles], I32), m.sb("tile_n", [P, mx.tiles])
        over, ntile, cum = m.sb("over", [P, E, NT]), m.sb("ntile", [P, E]), m.sb("cum", [P, E])
        before_t, owner = m.sb("before_t", [P, mx.tiles, E]), m.sb("owner", [P, mx.tiles])
        rank = m.sb("rank", [P, NT, E])
        pos_f = m.sb("pos_f", [P, NT])
        x_ps = [m.ps(f"x_ps{n}", [P, S]) for n in range(2)]
        w_ps = m.ps("w_ps", [P, KD, E])
        l_ps, r_ps = m.ps("l_ps", [P, NT, E]), m.ps("r_ps", [P, NT + 1, E])
        names = "loaded iota_ready iota_f wt_ready wr_ready xt_ready xt_copied logits_ready lg_ready exp_ready sel_ready rank_ready pos_ready link".split()
        (loaded, iota_ready, iota_f, wt_ready, wr_ready, xt_ready, xt_copied, logits_ready, lg_ready, exp_ready, sel_ready, rank_ready,
         pos_ready, link_s) = (m.sem(x) for x in names)
        scattered, scattered_0 = m.pool_dma_sem("scattered", NT * mx.top)
        block = stack.enter_context(nc.Block())
        n_loads = 3 if cond is not None else 1

        @block.sync
        def _(sp):
            if mx.by_rows:
                sp.dma_start(wr_rows[:], w_router).then_inc(loaded, 16)
            else:
                sp.dma_start(wr[:], w_router.rearrange("(k p) e -> p k e", p=P)).then_inc(loaded, 16)
            if cond is not None:
                sp.dma_start(g_t[:], cond.rearrange("b g -> g b")).then_inc(loaded, 16)
                sp.dma_start(wg_t[:], w_cond.rearrange("e g -> g e")).then_inc(loaded, 16)
            for dst, weight, semaphore in ahead:
                sp.dma_start(dst, weight).then_inc(semaphore, 16)

        @block.gpsimd
        def _(pool):
            pool.iota(desc_i[:], pattern=[[-1, E]], base=E, channel_multiplier=0).then_inc(iota_ready, 1)
            pool.iota(base_i[:], pattern=[[mx.cap, E]], base=0, channel_multiplier=0).then_inc(iota_ready, 1)
            pool.iota(edge_i[:], pattern=[[P, NT]], base=0, channel_multiplier=0).then_inc(iota_ready, 1)
            pool.iota(tile_i[:], pattern=[[1, mx.tiles]], base=0, channel_multiplier=0).then_inc(iota_ready, 1)
            pool.memset(sel[:], 0.0).then_inc(iota_ready, 1)
            pool.wait_ge(iota_ready, 5)
            for dst, s in ((desc, desc_i), (base, base_i), (edge, edge_i), (tile_n, tile_i)):
                pool.tensor_copy(dst[:], s[:]).then_inc(iota_f, 1)
            for k in range(mx.top):
                pool.wait_ge(pos_ready, k + 1)
                for t in range(NT):
                    pool.indirect_dma_start(sorted_rows, bass.IndirectOffsetOnAxis(ap=r.pos[k][:, t:t + 1], axis=0), src[:, t, :], None,
                                            bounds_check=mx.rows - 1, oob_is_err=False).then_inc(scattered, 16)
            pool.wait_ge(scattered, scattered_0 + 16 * NT * mx.top)

        @block.scalar
        def _(a):
            if mx.by_rows:
                a.wait_ge(wt_ready, 1)
                nc.scalar.activation(wr[:], w_ps[:], ACT.Copy).then_inc(wr_ready, 1)
            for b in range(B):
                for k in range(KD):
                    a.wait_ge(xt_ready, KD * b + k + 1)
                    nc.scalar.activation(c.xt[:, k, S * b:S * (b + 1)], x_ps[k][:], ACT.Copy).then_inc(xt_copied, 1)
            a.wait_ge(lg_ready, 1)
            nc.scalar.activation(ex[:], ex[:], ACT.Exp, scale=mx.temperature).then_inc(exp_ready, 1)

        @block.tensor
        def _(pe):
            if mx.by_rows:
                pe.wait_ge(loaded, 16 * n_loads)
                for k in range(KD):
                    last = nc.tensor.transpose(w_ps[:, k, :], wr_rows[:, P * k:P * (k + 1)], c.ident[0:E, 0:E])
                last.then_inc(wt_ready, 1)
            for b in range(B + 1):
                if b < B:
                    for k in range(KD):
                        if b >= 1:
                            pe.wait_ge(xt_copied, KD * (b - 1) + k + 1)
                        for t in range(QT):
                            last = nc.tensor.transpose(x_ps[k][:, P * t:P * (t + 1)], src[:, QT * b + t, P * k:P * (k + 1)], c.ident[:])
                        last.then_inc(xt_ready, 1)
                if b >= 1:
                    pe.wait_ge(xt_copied, KD * b)
                    if b == 1:
                        pe.wait_ge(loaded, 16 * n_loads)
                        if mx.by_rows:
                            pe.wait_ge(wr_ready, 1)
                    for t in range(QT * (b - 1), QT * b):
                        for k in range(KD):
                            last = nc.tensor.matmul(l_ps[:, t, :], c.xt[:, k, P * t:P * (t + 1)], wr[:, k, :], start=(k == 0),
                                                    stop=(k == KD - 1 and cond is None))
                        if cond is not None:
                            last = nc.tensor.matmul(l_ps[:, t, :], g_t[:, b - 1:b].to_broadcast([DH, P]), wg_t[:], start=False, stop=True)
            last.then_inc(logits_ready, 1)
            pe.wait_ge(sel_ready, 1)
            nc.tensor.matmul(r_ps[:], c.before[:], sel[:], start=True, stop=False)
            for t in range(NT):
                last = nc.tensor.matmul(r_ps[:, t + 1:, :], c.ones_b[:], sel[:, t:t + 1, :].to_broadcast([P, NT - t, E]), start=False, stop=(t == NT - 1))
            last.then_inc(rank_ready, 1)

        @block.vector
        def _(dve):
            linked = [0]
            V = nc.vector

            def link(ins):
                linked[0] += 1
                ins.then_inc(link_s, 1)
                dve.wait_ge(link_s, linked[0])

            def wide(t):
                return t[:].unsqueeze(2).to_broadcast([P, NT, E])

            def per_expert(t):
                return t[:].unsqueeze(1).to_broadcast([P, NT, E])

            dve.wait_ge(logits_ready, 1)
            dve.wait_ge(iota_f, 4)
            link(V.tensor_copy(lg[:], l_ps[:]))
            for k in range(mx.top):
                link(V.tensor_reduce(top[k][:], lg[:], AX.X, ALU.max))
                if k == 0:
                    link(V.tensor_tensor(ex[:], lg[:], wide(top[0]), ALU.subtract))
                    dve.sem_inc(lg_ready, 1)
                link(V.tensor_tensor(tmp[:], lg[:], wide(top[k]), ALU.is_ge))
                link(V.tensor_tensor(tmp[:], tmp[:], per_expert(desc), ALU.mult))
                link(V.tensor_reduce(red[:], tmp[:], AX.X, ALU.max))
                link(V.tensor_tensor(hot[k][:], tmp[:], wide(red), ALU.is_equal))
                if k + 1 < mx.top:
                    link(V.scalar_tensor_tensor(out=lg[:], in0=hot[k][:], scalar=2 * NEG, in1=lg[:], op0=ALU.mult, op1=ALU.add))
            if mx.top == 2:
                V.tensor_tensor(sel[:, 0:NT, :], hot[0][:], hot[1][:], ALU.add).then_inc(sel_ready, 1)
            else:
                V.tensor_copy(sel[:, 0:NT, :], hot[0][:]).then_inc(sel_ready, 1)
            dve.wait_ge(exp_ready, 1)
            link(V.tensor_reduce(total[:], ex[:], AX.X, ALU.add))
            link(V.reciprocal(total[:], total[:]))
            for k in range(mx.top):
                link(V.tensor_tensor(tmp[:], ex[:], hot[k][:], ALU.mult))
                link(V.tensor_reduce(red[:], tmp[:], AX.X, ALU.add))
                link(V.tensor_tensor(r.weight[k][:], red[:], total[:], ALU.mult))
            if mx.normalised:
                link(V.scalar_tensor_tensor(out=total[:], in0=r.weight[0][:], scalar=1e-20, in1=r.weight[1][:], op0=ALU.add, op1=ALU.add))
                link(V.reciprocal(total[:], total[:]))
                for k in range(mx.top):
                    link(V.tensor_tensor(r.weight[k][:], r.weight[k][:], total[:], ALU.mult))
            dve.wait_ge(rank_ready, 1)
            link(V.tensor_copy(rank[:], r_ps[:, 0:NT, :]))
            if not mx.cap:
                link(V.tensor_copy(base[:], r_ps[:, NT, :]))
                link(V.tensor_tensor(over[:], base[:].unsqueeze(2).to_broadcast([P, E, NT]), edge[:].unsqueeze(1).to_broadcast([P, E, NT]), ALU.is_gt))
                link(V.tensor_reduce(ntile[:], over[:], AX.X, ALU.add))
                link(V.tensor_copy(cum[:], ntile[:]))
                for e in range(1, E):
                    link(V.tensor_tensor(cum[:, e:e + 1], cum[:, e:e + 1], cum[:, e - 1:e], ALU.add))
                link(V.tensor_tensor(base[:], cum[:], ntile[:], ALU.subtract))
                link(V.tensor_scalar(base[:], base[:], float(P), None, ALU.mult))
                link(V.tensor_tensor(before_t[:], tile_n[:].unsqueeze(2).to_broadcast([P, mx.tiles, E]), cum[:].unsqueeze(1).to_broadcast([P, mx.tiles, E]), ALU.is_ge))
                link(V.tensor_reduce(owner[:], before_t[:], AX.X, ALU.add))
                link(V.tensor_scalar(owner[:], owner[:], float(E - 1), None, ALU.min))
                link(V.tensor_copy(r.owner[:], owner[:]))
            link(V.tensor_tensor(tmp2[:], rank[:], per_expert(base), ALU.add))
            for k in range(mx.top):
                link(V.tensor_tensor(tmp[:], tmp2[:], hot[k][:], ALU.mult))
                link(V.tensor_reduce(pos_f[:], tmp[:], AX.X, ALU.add))
                if mx.cap:
                    link(V.tensor_tensor(tmp[:], rank[:], hot[k][:], ALU.mult))
                    link(V.tensor_reduce(red[:], tmp[:], AX.X, ALU.add))
                    link(V.tensor_scalar(red[:], red[:], float(mx.cap), None, ALU.is_ge))
                    link(V.scalar_tensor_tensor(out=pos_f[:], in0=red[:], scalar=float(1 << 20), in1=pos_f[:], op0=ALU.mult, op1=ALU.add))
                    link(V.tensor_scalar(red[:], red[:], -1.0, 1.0, ALU.mult, ALU.add))
                    link(V.tensor_tensor(r.weight[k][:], r.weight[k][:], red[:], ALU.mult))
                V.tensor_copy(r.pos[k][:], pos_f[:]).then_inc(pos_ready, 1)
                dve.wait_ge(pos_ready, k + 1)


class CapacityWeights:

    def __init__(self, nc, stack, mx, w1, w2):
        m = Memory(nc, stack, f"cw_{mx.name}")
        self.w1_sb = [m.sb(f"w1_{n}", [P, KD, mx.hidden]) for n in range(2)]
        self.w2_sb = [m.sb(f"w2_{n}", [P, mx.hidden // P, D]) for n in range(2)]
        self.w1_loaded, self.w2_loaded = ([m.sem(f"{x}_loaded{n}") for n in range(2)] for x in ("w1", "w2"))
        self.w1, self.w2 = w1.rearrange("e (k p) f -> e p k f", p=P), w2.rearrange("e (k p) f -> e p k f", p=P)
        self.loads = []
        for n in range(2):
            self.loads += [(self.w1_sb[n][:], self.w1[n], self.w1_loaded[n]), (self.w2_sb[n][:], self.w2[n], self.w2_loaded[n])]


def experts_by_capacity(nc, c, mx, cw, sorted_rows, expert_rows, func):
    cap, F = mx.cap, mx.hidden
    FC, CT = F // P, cap // P
    w1_sb, w2_sb, w1_loaded, w2_loaded = cw.w1_sb, cw.w2_sb, cw.w1_loaded, cw.w2_loaded
    with ExitStack() as stack:
        m = Memory(nc, stack, f"exp_{mx.name}")
        xs = [m.sb(f"xs{n}", [P, CT, D]) for n in range(2)]
        xs_t = [m.sb(f"xs_t{n}", [P, KD, cap]) for n in range(2)]
        hid = [m.sb(f"hid{n}", [P, FC, cap]) for n in range(2)]
        ys = [m.sb(f"ys{n}", [P, CT, D]) for n in range(2)]
        x_ps = [m.ps(f"x_ps{k}", [P, S]) for k in range(KD)]
        h_ps = [m.ps(f"h_ps{n}", [P, S]) for n in range(4)]
        y_ps = [m.ps(f"y_ps{n}", [P, 2, D]) for n in range(2)]
        xs_loaded = [m.sem(f"xs_loaded{n}") for n in range(2)]
        names = "xt_ready xt_copied h_ready hid_ready y_ready y_copied".split()
        (xt_ready, xt_copied, h_ready, hid_ready, y_ready, y_copied) = (m.sem(x) for x in names)
        m.start_at_one(xt_copied, h_ready, hid_ready, y_ready, y_copied)
        stored, stored_0 = zip(*(m.pool_dma_sem(f"stored{n}", E // 2) for n in range(2)))
        block = stack.enter_context(nc.Block())
        R = E // 2
        YT = max(CT // 2, 1)
        x_rows = sorted_rows[0:mx.rows, :].rearrange("(e t p) d -> e p t d", e=E, p=P)
        y_rows = expert_rows[0:mx.rows, :].rearrange("(e t p) d -> e p t d", e=E, p=P)

        @block.sync
        def _(sp):
            def load_rows(e, n):
                sp.dma_start(xs[n][:], x_rows[ds(e, 1)].rearrange("a p t d -> (a p) t d")).then_inc(xs_loaded[n], 16)

            for n in range(2):
                load_rows(n, n)
            with sp.Fori(0, R - 1) as i:
                for n in range(2):
                    done = sp.to_reg(i * (2 * YT) + YT * (n + 1) + 1)
                    sp.wait_ge(y_ready, 1)
                    sp.wait_ge(y_ready, done)
                    e = i * 2 + 2 + n
                    load_rows(e, n)
                    sp.dma_start(w1_sb[n][:], cw.w1[ds(e, 1)].rearrange("a p k f -> (a p) k f")).then_inc(w1_loaded[n], 16)
                    sp.dma_start(w2_sb[n][:], cw.w2[ds(e, 1)].rearrange("a p k f -> (a p) k f")).then_inc(w2_loaded[n], 16)

        @block.gpsimd
        def _(pool):
            with pool.Fori(0, R) as i:
                for n in range(2):
                    done = pool.to_reg(i * (2 * YT) + YT * (n + 1) + 1)
                    pool.wait_ge(y_copied, 1)
                    pool.wait_ge(y_copied, done)
                    pool.dma_start(y_rows[ds(i * 2 + n, 1)].rearrange("a p t d -> (a p) t d"), ys[n][:]).then_inc(stored[n], 16)
            for n in range(2):
                pool.wait_ge(stored[n], stored_0[n] + 16 * R)

        @block.tensor
        def _(pe):
            def turn(i, n):
                pe.wait_ge(xs_loaded[n], i * 16 + 16)
                for k in range(KD):
                    pe.wait_ge(xt_copied, i * (2 * KD) + KD * n + 1)
                    for t in range(CT):
                        last = nc.tensor.transpose(x_ps[k][:, P * t:P * (t + 1)], xs[n][:, t, P * k:P * (k + 1)], c.ident[:])
                    last.then_inc(xt_ready, 1)

            with pe.Fori(0, R) as i:
                for n in range(2):
                    turn(i, n)
                    pe.wait_ge(w1_loaded[n], i * 16 + 16)
                    pe.wait_ge(xt_copied, i * (2 * KD) + KD * (n + 1) + 1)
                    for f in range(FC):
                        pe.wait_ge(hid_ready, i * (2 * FC) + max(FC * n + f - 3, 0) + 1)
                        for k in range(KD):
                            last = nc.tensor.matmul(h_ps[f % 4][:, 0:cap], w1_sb[n][:, k, P * f:P * (f + 1)], xs_t[n][:, k, :],
                                                    start=(k == 0), stop=(k == KD - 1))
                        last.then_inc(h_ready, 1)
                    pe.wait_ge(w2_loaded[n], i * 16 + 16)
                    for t in range(CT):
                        if t % 2 == 0:
                            pe.wait_ge(y_copied, i * (2 * YT) + max(YT * n + t // 2 - 1, 0) + 1)
                        for f in range(FC):
                            if t == 0:
                                pe.wait_ge(hid_ready, i * (2 * FC) + FC * n + f + 1 + 1)
                            last = nc.tensor.matmul(y_ps[(YT * n + t // 2) % 2][:, t % 2, :], hid[n][:, f, P * t:P * (t + 1)], w2_sb[n][:, f, :],
                                                    start=(f == 0), stop=(f == FC - 1))
                        if t % 2:
                            last.then_inc(y_ready, 1)

        @block.vector
        def _(dve):
            with dve.Fori(0, R) as i:
                for n in range(2):
                    for k in range(KD):
                        dve.wait_ge(xt_ready, i * (2 * KD) + KD * n + k + 1)
                        dve.wait_ge(h_ready, i * (2 * FC) + 1)
                        nc.vector.tensor_copy(xs_t[n][:, k, :], x_ps[k][:, 0:cap]).then_inc(xt_copied, 1)
                    for y in range(YT):
                        dve.wait_ge(y_ready, i * (2 * YT) + YT * n + y + 1 + 1)
                        dve.wait_ge(stored[n], i * 16 + stored_0[n])
                        nc.vector.tensor_copy(ys[n][:, 2 * y:2 * y + 2, :], y_ps[(YT * n + y) % 2][:]).then_inc(y_copied, 1)

        @block.scalar
        def _(a):
            with a.Fori(0, R) as i:
                for n in range(2):
                    for f in range(FC):
                        a.wait_ge(h_ready, i * (2 * FC) + FC * n + f + 1 + 1)
                        a.wait_ge(y_ready, i * (2 * YT) + 1)
                        nc.scalar.activation(hid[n][:, f, :], h_ps[f % 4][:, 0:cap], func).then_inc(hid_ready, 1)


class TileWeights:

    def __init__(self, nc, stack, mx, weights):
        m = Memory(nc, stack, f"tw_{mx.name}")
        F, FC = mx.hidden, mx.hidden // P
        self.wa = m.sb("wa", [P, E * KD, F])
        self.wb = m.sb("wb", [P, E * KD, F])
        self.wd = m.sb("wd", [P, E * FC, D])
        self.loaded = m.sem("loaded")
        self.loads = [(t[:], w.rearrange("e (k p) f -> p (e k) f", p=P), self.loaded)
                      for t, w in zip((self.wa, self.wb, self.wd), weights)]


def experts_by_tile(nc, c, mx, tw, sorted_rows, expert_rows, r):
    F = mx.hidden
    FC = F // P
    G = 4
    wa, wb, wd = tw.wa, tw.wb, tw.wd
    with ExitStack() as stack:
        m = Memory(nc, stack, f"til_{mx.name}")
        xs = [m.sb(f"xs{n}", [P, D]) for n in range(G)]
        xs_t = [m.sb(f"xs_t{n}", [P, KD, P]) for n in range(2)]
        act = [m.sb(f"act{n}", [P, F]) for n in range(2)]
        lin = [m.sb(f"lin{n}", [P, F]) for n in range(2)] if mx.gate else None
        hid = [m.sb(f"hid{n}", [P, F]) for n in range(2)]
        hid_t = [m.sb(f"hid_t{n}", [P, FC, P]) for n in range(2)]
        ys = [m.sb(f"ys{n}", [P, D]) for n in range(G)]
        a_ps = [m.ps(f"a_ps{n}", [P, 512]) for n in range(2)]
        b_ps = [m.ps(f"b_ps{n}", [P, 512]) for n in range(2)]
        x_ps = m.ps("x_ps", [P, KD, P])
        t_ps = m.ps("t_ps", [P, FC, P])
        y_ps = [m.ps(f"y_ps{n}", [P, D]) for n in range(2)]
        xs_loaded = [m.sem(f"xs_loaded{n}") for n in range(G)]
        R = mx.tiles // G
        stored, stored_0 = zip(*(m.pool_dma_sem(f"stored{n}", R) for n in range(G)))
        names = "xt_ready xt_copied ab_ready act_ready lin_ready hid_ready ht_ready ht_copied y_ready y_copied".split()
        (xt_ready, xt_copied, ab_ready, act_ready, lin_ready, hid_ready, ht_ready, ht_copied, y_ready, y_copied) = (m.sem(x) for x in names)
        block = stack.enter_context(nc.Block())
        x_rows = sorted_rows[0:mx.rows, :].rearrange("(t p) d -> t p d", p=P)
        y_rows = expert_rows[0:mx.rows, :].rearrange("(t p) d -> t p d", p=P)

        @block.sync
        def _(sp):
            def load(t, n):
                sp.dma_start(xs[n][:], x_rows[ds(t, 1)].rearrange("a p d -> (a p) d")).then_inc(xs_loaded[n], 16)

            for n in range(G):
                load(n, n)
            with sp.Fori(0, R - 1) as i:
                for n in range(G):
                    turned = sp.to_reg(i * G + n + 1)
                    sp.wait_ge(xt_ready, 1)
                    sp.wait_ge(xt_ready, turned)
                    load(i * G + G + n, n)

        @block.gpsimd
        def _(pool):
            with pool.Fori(0, R) as i:
                for n in range(G):
                    done = pool.to_reg(i * G + n + 1)
                    pool.wait_ge(y_copied, 1)
                    pool.wait_ge(y_copied, done)
                    pool.dma_start(y_rows[ds(i * G + n, 1)].rearrange("a p d -> (a p) d"), ys[n][:]).then_inc(stored[n], 16)
            for n in range(G):
                pool.wait_ge(stored[n], stored_0[n] + 16 * R)

        @block.tensor
        def _(pe):
            def expert_of(t):
                return pe.value_load(r.owner[0:1, ds(t, 1)], min_val=0, max_val=E - 1)

            def turn_x(i, n, first):
                pe.wait_ge(xs_loaded[n % G], i * 16 + 16 * (n // G + 1))
                if not (first and n == 0):
                    pe.wait_ge(xt_copied, i * G + n)
                for k in range(KD):
                    last = nc.tensor.transpose(x_ps[:, k, :], xs[n % G][:, P * k:P * (k + 1)], c.ident[:])
                last.then_inc(xt_ready, 1)

            def first_products(i, n, first):
                expert = expert_of(i * G + n)
                pe.wait_ge(xt_copied, i * G + n + 1)
                if not (first and n < 2):
                    pe.wait_ge(hid_ready, i * G + n - 1)
                for ps, w in ((a_ps, wa), (b_ps, wb)):
                    for k in range(KD):
                        last = nc.tensor.matmul(ps[n % 2][:, 0:F], xs_t[n % 2][:, k, :], w[:, ds(expert * KD + k, 1), :].rearrange("p a f -> p (a f)"),
                                                start=(k == 0), stop=(k == KD - 1))
                last.then_inc(ab_ready, 1)

            def turn_hidden(i, n, first):
                pe.wait_ge(hid_ready, i * G + n + 1)
                if not (first and n == 0):
                    pe.wait_ge(ht_copied, i * G + n)
                for f in range(FC):
                    last = nc.tensor.transpose(t_ps[:, f, :], hid[n % 2][:, P * f:P * (f + 1)], c.ident[:])
                last.then_inc(ht_ready, 1)

            def last_product(i, n, first):
                expert = expert_of(i * G + n)
                pe.wait_ge(ht_copied, i * G + n + 1)
                if not (first and n < 2):
                    pe.wait_ge(y_copied, i * G + n - 1)
                for f in range(FC):
                    last = nc.tensor.matmul(y_ps[n % 2][:], hid_t[n % 2][:, f, :], wd[:, ds(expert * FC + f, 1), :].rearrange("p a f -> p (a f)"),
                                            start=(f == 0), stop=(f == FC - 1))
                last.then_inc(y_ready, 1)

            def one(i, first, last):
                for n in range(G + (2 if last else 0)):
                    if n + 1 < G or not last:
                        turn_x(i, n + 1, first)
                    if n < G:
                        first_products(i, n, first)
                    if n < G + 1 and not (first and n < 1):
                        turn_hidden(i, n - 1, first)
                    if not (first and n < 2):
                        last_product(i, n - 2, first)

            turn_x(0, 0, True)
            pe.wait_ge(tw.loaded, 48)
            rounds(pe, R, one)

        @block.scalar
        def _(a):
            def one(i, first, last):
                for n in range(G + (1 if last else 0)):
                    if n < G:
                        a.wait_ge(ab_ready, i * G + n + 1)
                        if not (first and n < 2):
                            a.wait_ge(hid_ready, i * G + n - 1)
                            if mx.gate:
                                a.wait_ge(lin_ready, i * G + n - 1)
                        nc.scalar.activation(act[n % 2][:], a_ps[n % 2][:, 0:F], ACT.Copy if mx.gate else ACT.Silu).then_inc(act_ready, 1)
                    if not (first and n < 1):
                        v = n - 1
                        a.wait_ge(ht_ready, i * G + v + 1)
                        if not (first and v < 2):
                            a.wait_ge(y_ready, i * G + v - 1)
                        nc.scalar.activation(hid_t[v % 2][:], t_ps[:], ACT.Copy).then_inc(ht_copied, 1)

            rounds(a, R, one)

        @block.vector
        def _(dve):
            def take_x(i, n, first):
                dve.wait_ge(xt_ready, i * G + n + 1)
                if not (first and n < 2):
                    dve.wait_ge(ab_ready, i * G + n - 1)
                nc.vector.tensor_copy(xs_t[n % 2][:], x_ps[:]).then_inc(xt_copied, 1)

            def one(i, first, last):
                for n in range(G + (2 if last else 0)):
                    if n + 1 < G or not last:
                        take_x(i, n + 1, first)
                    if n < G:
                        dve.wait_ge(act_ready, i * G + n + 1)
                        if mx.gate:
                            if not (first and n < 2):
                                dve.wait_ge(hid_ready, i * G + n - 1)
                            nc.vector.scalar_tensor_tensor(out=lin[n % 2][:], in0=act[n % 2][:], scalar=0.01, in1=act[n % 2][:], op0=ALU.mult,
                                                           op1=ALU.max).then_inc(lin_ready, 1)
                            dve.wait_ge(lin_ready, i * G + n + 1)
                        if not (first and n < 2):
                            dve.wait_ge(ht_ready, i * G + n - 1)
                        nc.vector.tensor_tensor(hid[n % 2][:], (lin if mx.gate else act)[n % 2][:], b_ps[n % 2][:, 0:F], ALU.mult).then_inc(hid_ready, 1)
                    if not (first and n < 2):
                        v = n - 2
                        dve.wait_ge(y_ready, i * G + v + 1)
                        stores = i * 16 + (stored_0[v % G] if v >= 0 else stored_0[v % G] - 16)
                        dve.wait_ge(stored[v % G], stores)
                        nc.vector.tensor_copy(ys[v % G][:], y_ps[v % 2][:]).then_inc(y_copied, 1)

            take_x(0, 0, True)
            rounds(dve, R, one)


def combine(nc, c, mx, expert_rows, r, start, dst, bias=None):
    with ExitStack() as stack:
        m = Memory(nc, stack, f"com_{mx.name}")
        rows = [m.sb(f"rows{k}", [P, NT, D]) for k in range(mx.top)]
        bias_sb = m.sb("bias", [P, D])
        cleared, loaded, biased, added = m.sem("cleared"), m.sem("loaded"), m.sem("biased"), m.sem("added")
        G = 4
        got = [m.pool_dma_sem(f"got{g}", G * mx.top) for g in range(NT // G)]
        block = stack.enter_context(nc.Block())

        @block.sync
        def _(sp):
            if bias is not None:
                sp.dma_start(bias_sb[:], row(bias.rearrange("a b d -> (a b d)"))).then_inc(loaded, 16)

        @block.gpsimd
        def _(pool):
            if mx.cap:
                pool.wait_ge(cleared, mx.top)
            for t in range(NT):
                for k in range(mx.top):
                    pool.indirect_dma_start(rows[k][:, t, :], None, expert_rows[0:mx.rows, :], bass.IndirectOffsetOnAxis(ap=r.pos[k][:, t:t + 1], axis=0),
                                            bounds_check=mx.rows - 1, oob_is_err=False).then_inc(got[t // G][0], 16)

        @block.vector
        def _(dve):
            if mx.cap:
                for k in range(mx.top):
                    nc.vector.memset(rows[k][:], 0.0).then_inc(cleared, 1)
            if bias is not None:
                dve.wait_ge(loaded, 16)
                nc.vector.tensor_tensor(dst[:], start[:], bias_sb[:].unsqueeze(1).to_broadcast([P, NT, D]), ALU.add).then_inc(biased, 1)
                dve.wait_ge(biased, 1)
            for t in range(NT):
                if t % G == 0:
                    dve.wait_ge(got[t // G][0], got[t // G][1] + 16 * G * mx.top)
                for k in range(mx.top):
                    nc.vector.scalar_tensor_tensor(out=dst[:, t, :], in0=rows[k][:, t, :], scalar=r.weight[k][:, t:t + 1],
                                                   in1=(start if k == 0 and bias is None else dst)[:, t, :], op0=ALU.mult,
                                                   op1=ALU.add).then_inc(added, 1)
                    dve.wait_ge(added, mx.top * t + k + 1)


def shared_expert(nc, c, w_gate, w_up, w_down):
    with ExitStack() as stack:
        m = Memory(nc, stack, "shx")
        wgu = m.sb("wgu", [P, KD, 2, D])
        wd = m.sb("wd", [P, KD, D])
        act = [m.sb(f"act{n}", [P, D]) for n in range(2)]
        lin = [m.sb(f"lin{n}", [P, D]) for n in range(2)]
        hid = [m.sb(f"hid{n}", [P, D]) for n in range(2)]
        hid_t = [m.sb(f"hid_t{n}", [P, KD, P]) for n in range(2)]
        gu_ps = [m.ps(f"gu_ps{n}", [P, 2, D]) for n in range(2)]
        t_ps = [m.ps(f"t_ps{n}", [P, KD, P]) for n in range(2)]
        y_ps = [m.ps(f"y_ps{n}", [P, D]) for n in range(2)]
        names = "loaded gu_ready act_ready lin_ready hid_ready ht_ready ht_copied y_ready h_ready".split()
        (loaded, gu_ready, act_ready, lin_ready, hid_ready, ht_ready, ht_copied, y_ready, h_ready) = (m.sem(x) for x in names)
        block = stack.enter_context(nc.Block())

        @block.sync
        def _(sp):
            sp.dma_start(wgu[:, :, 0, :], w_gate.rearrange("(k p) f -> p k f", p=P)).then_inc(loaded, 16)
            sp.dma_start(wgu[:, :, 1, :], w_up.rearrange("(k p) f -> p k f", p=P)).then_inc(loaded, 16)
            sp.dma_start(wd[:], w_down.rearrange("(k p) f -> p k f", p=P)).then_inc(loaded, 16)

        @block.tensor
        def _(pe):
            pe.wait_ge(loaded, 48)
            for t in range(NT + 1):
                if t < NT:
                    if t >= 2:
                        pe.wait_ge(hid_ready, t - 1)
                    for k in range(KD):
                        last = nc.tensor.matmul(gu_ps[t % 2][:], c.xt[:, k, P * t:P * (t + 1)], wgu[:, k, :, :], start=(k == 0), stop=(k == KD - 1))
                    last.then_inc(gu_ready, 1)
                if t >= 1:
                    v = t - 1
                    pe.wait_ge(hid_ready, v + 1)
                    if v >= 2:
                        pe.wait_ge(ht_copied, v - 1)
                    for f in range(KD):
                        last = nc.tensor.transpose(t_ps[v % 2][:, f, :], hid[v % 2][:, P * f:P * (f + 1)], c.ident[:])
                    last.then_inc(ht_ready, 1)
                    pe.wait_ge(ht_copied, v + 1)
                    if v >= 2:
                        pe.wait_ge(h_ready, v - 1)
                    for f in range(KD):
                        last = nc.tensor.matmul(y_ps[v % 2][:], hid_t[v % 2][:, f, :], wd[:, f, :], start=(f == 0), stop=(f == KD - 1))
                    last.then_inc(y_ready, 1)

        @block.scalar
        def _(a):
            for t in range(NT + 1):
                if t < NT:
                    a.wait_ge(gu_ready, t + 1)
                    if t >= 2:
                        a.wait_ge(lin_ready, t - 1)
                    nc.scalar.activation(act[t % 2][:], gu_ps[t % 2][:, 0, :], ACT.Copy).then_inc(act_ready, 1)
                if t >= 1:
                    a.wait_ge(ht_ready, t)
                    if t >= 3:
                        a.wait_ge(y_ready, t - 2)
                    nc.scalar.activation(hid_t[(t - 1) % 2][:], t_ps[(t - 1) % 2][:], ACT.Copy).then_inc(ht_copied, 1)

        @block.vector
        def _(dve):
            for t in range(NT + 1):
                if t < NT:
                    dve.wait_ge(act_ready, t + 1)
                    if t >= 2:
                        dve.wait_ge(hid_ready, t - 1)
                    nc.vector.scalar_tensor_tensor(out=lin[t % 2][:], in0=act[t % 2][:], scalar=0.01, in1=act[t % 2][:], op0=ALU.mult,
                                                   op1=ALU.max).then_inc(lin_ready, 1)
                    dve.wait_ge(lin_ready, t + 1)
                    if t >= 2:
                        dve.wait_ge(ht_ready, t - 1)
                    nc.vector.tensor_tensor(hid[t % 2][:], lin[t % 2][:], gu_ps[t % 2][:, 1, :], ALU.mult).then_inc(hid_ready, 1)
                if t >= 1:
                    dve.wait_ge(y_ready, t)
                    nc.vector.tensor_copy(c.h[:, t - 1, :], y_ps[(t - 1) % 2][:]).then_inc(h_ready, 1)


class Routing:

    def __init__(self, nc, stack, mx):
        m = Memory(nc, stack, f"r_{mx.name}")
        self.pos = [m.sb(f"pos{k}", [P, NT], I32) for k in range(mx.top)]
        self.weight = [m.sb(f"weight{k}", [P, NT]) for k in range(mx.top)]
        self.owner = m.sb("owner", [P, mx.tiles], I32)


def clear_rows(nc, c, buffers):
    with ExitStack() as stack:
        m = Memory(nc, stack, "clr")
        zero = m.sb("zero", [P, 8 * D])
        cleared, stored = m.sem("cleared"), m.sem("stored")
        by_pool = [m.pool_dma_sem(f"stored{n}", 1)[0] for n in range(4)]
        block = stack.enter_context(nc.Block())
        parts = [b[lo:min(lo + 8 * P, b.shape[0]), :] for b in buffers for lo in range(0, b.shape[0], 8 * P)]

        @block.vector
        def _(dve):
            nc.vector.memset(zero[:], 0.0).then_inc(cleared, 1)

        @block.gpsimd
        def _(pool):
            pool.wait_ge(cleared, 1)
            for part, semaphore in zip(parts, by_pool):
                pool.dma_start(part.rearrange("(p t) d -> p (t d)", p=P), zero[:, 0:part.shape[0] // P * D]).then_inc(semaphore, 16)
            for semaphore in by_pool:
                pool.wait_ge(semaphore, 16)

        @block.sync
        def _(sp):
            sp.wait_ge(cleared, 1)
            for part in parts[len(by_pool):]:
                n = part.shape[0] // P
                sp.dma_start(part.rearrange("(p t) d -> p (t d)", p=P), zero[:, 0:n * D]).then_inc(stored, 16)
            sp.wait_ge(stored, 16 * (len(parts) - len(by_pool)))


def build(nc, d, out):
    def group(prefix, **more):
        return {**{n[len(prefix):]: ap for n, ap in d.items() if n.startswith(prefix)}, **more}

    mixtures = {
        "f1": Mixture("f1", 2, 2 * T // E, 1024),
        "c2": Mixture("c2", 2, 0, 128, temperature=0.5, normalised=True, by_rows=True, gate=True),
        "f2": Mixture("f2", 1, T // E, 1024),
        "f3": Mixture("f3", 2, 0, 512, by_rows=True),
    }

    def scratch(name, shape):
        return nc.dram_tensor(name, shape, F32, kind="Internal").ap()

    Memory.cleared, Memory.pool_dma_semaphores = [], {}
    with ExitStack() as stack:
        stack.enter_context(nc.allow_non_contiguous_dma(reason="short vectors by column"))
        c = shared(nc, stack)
        rows = scratch("sorted", [max(mx.rows for mx in mixtures.values()), D])
        done = scratch("expert", [max(mx.rows for mx in mixtures.values()), D])
        make_constants(nc, c)
        clear_rows(nc, c, [rows])

        def attend(l, w, mask, bias_of, causal, w_out, x_in=None):
            with ExitStack() as inner:
                attention_memory(nc, inner, c, l)
                attention_inputs(nc, c, l, w, d["cond_64"], mask, x_in)
                attention(nc, c, l, bias_of, causal)
                attention_output(nc, c, l, w_out, w["g_out"], d["cond_64"])

        def relative(l, w):
            band = scratch(f"band{l}", [H, P, S])
            relative_bias(nc, c, l, w, scratch(f"rev{l}", [H, REV]), band)
            return band_bias(band)

        w = group("L0_cond_", g=d["L0_cond_g_in"])
        given = d["fside_16xSxS_0"]
        attend(0, w, d["mask_BxS_bk0"], lambda i, hh, q: given[ds(i * 2 + hh, 1), P * q:P * (q + 1), 0:P * (q + 1)].rearrange("a p n -> (a p) n"),
               True, w["Wo"], x_in=d["x"])
        ternary_linear(nc, c, d["L0_ffn_weight"])

        w = group("L1_cond_", g=d["L1_cond_g_norm"])
        attend(1, w, d["mask_BxS_bf1"], relative(1, w), False, w["Wout"])
        mx, w = mixtures["f1"], group("L1_ffn_")
        with ExitStack() as inner:
            r = Routing(nc, inner, mx)
            cw = CapacityWeights(nc, inner, mx, w["w1"], w["w2"])
            route(nc, c, mx, c.h, w["w_router"], rows, r, cw.loads)
            experts_by_capacity(nc, c, mx, cw, rows, done, ACT.Gelu_apprx_tanh)
            combine(nc, c, mx, done, r, c.x, c.x, bias=w["bias"])

        mx, w = mixtures["c2"], group("L2_cond_")
        with ExitStack() as inner:
            r = Routing(nc, inner, mx)
            tw = TileWeights(nc, inner, mx, (w["w_gate"], w["w_up"], w["w_down"]))
            route(nc, c, mx, c.x, w["wt"], rows, r, tw.loads, cond=d["cond_64"], w_cond=w["wg"])
            shared_expert(nc, c, w["sw_gate"], w["sw_up"], w["sw_down"])
            experts_by_tile(nc, c, mx, tw, rows, done, r)
            combine(nc, c, mx, done, r, c.h, c.h)
        mx, w = mixtures["f2"], group("L2_ffn_")
        with ExitStack() as inner:
            r = Routing(nc, inner, mx)
            cw = CapacityWeights(nc, inner, mx, w["W1"], w["W2"])
            route(nc, c, mx, c.h, w["Wr"], rows, r, cw.loads)
            experts_by_capacity(nc, c, mx, cw, rows, done, ACT.Relu)
            combine(nc, c, mx, done, r, c.x, c.x)

        w = group("L3_cond_", g=d["L3_cond_g_norm"])
        attend(3, w, d["mask_BxS_bf1"], relative(3, w), False, w["Wout"])
        mx, w = mixtures["f3"], group("L3_ffn_")
        with ExitStack() as inner:
            r = Routing(nc, inner, mx)
            tw = TileWeights(nc, inner, mx, (w["w1"], w["w3"], w["w2"]))
            route(nc, c, mx, c.h, w["gate_w"], rows, r, tw.loads)
            experts_by_tile(nc, c, mx, tw, rows, done, r)
            combine(nc, c, mx, done, r, c.x, c.x)

        out_stored = Memory(nc, stack, "end").sem("out_stored")
        with nc.Block() as block:
            @block.sync
            def _(sp):
                sp.dma_start(out.rearrange("b (t p) d -> p (b t) d", p=P), c.x[:]).then_inc(out_stored, 16)
                sp.wait_ge(out_stored, 16)


def kernel(**inputs):
    import numpy as _np
    import concourse.bacc as _bacc
    from concourse import mybir as _mybir
    from concourse.bass_utils import run_bass_kernel_spmd as _run

    nc = _bacc.Bacc("TRN2", target_bir_lowering=False, num_devices=1)
    arrays, args = {}, {}
    for name, a in inputs.items():
        a = _np.ascontiguousarray(a)
        if a.dtype == bool:
            a = a.view(_np.uint32)
        arrays[f"in_{name}_dram"] = a
        args[name] = nc.dram_tensor(f"in_{name}_dram", a.shape, _mybir.dt.from_np(a.dtype), kind="ExternalInput").ap()
    out = nc.dram_tensor("out_0_dram", (B, S, D), F32, kind="ExternalOutput").ap()
    build(nc, args, out)
    r = _run(nc, [arrays], core_ids=[0])
    return r.results[0]["out_0_dram"]
```

```python
from contextlib import ExitStack, contextmanager

import concourse.bass as bass
from concourse import mybir

F32 = mybir.dt.float32
BF16 = mybir.dt.bfloat16
I32 = mybir.dt.int32
U8 = mybir.dt.uint8
ALU = mybir.AluOpType
ACT = mybir.ActivationFunctionType
AX = mybir.AxisListType
ds = bass.ds

P = 128
B, S, D = 4, 512, 256
T = B * S
NT = T // P
QT = S // P
KD = D // P
H, DH = 16, 64
HP = H // 2
E = 8
EPS = 1e-5
NEG = -1e30
REV = 640
NKEY = [1 + P * (q + 1) for q in range(QT)]


class Memory:

    cleared = []
    pool_dma_semaphores = {}

    def __init__(self, nc, stack, prefix):
        self.nc, self.stack, self.prefix = nc, stack, prefix
        self.semaphores = []
        stack.callback(self.release)

    def release(self):
        for semaphore in Memory.cleared:
            self.nc.release_semaphore(semaphore)
        for run in runs(self.semaphores):
            self.nc.gpsimd.sem_clear(run)
        Memory.cleared = self.semaphores

    def sb(self, name, shape, dt=F32):
        return self.stack.enter_context(self.nc.sbuf_tensor(f"{self.prefix}_{name}", shape, dt))

    def ps(self, name, shape, dt=F32):
        return self.stack.enter_context(self.nc.psum_tensor(f"{self.prefix}_{name}", shape, dt))

    def sem(self, name):
        self.semaphores.append(self.nc.alloc_semaphore(name=f"{self.prefix}_{name}"))
        return self.semaphores[-1]

    def start_at_one(self, *semaphores):
        for semaphore in semaphores:
            self.nc.gpsimd.sem_inc(semaphore, 1)
        self.nc.all_engine_barrier()

    def pool_dma_sem(self, name, dmas):
        kept = Memory.pool_dma_semaphores
        semaphore, value = kept.get(name) or (self.nc.alloc_semaphore(name=name), 0)
        kept[name] = semaphore, value + 16 * dmas
        return semaphore, value


@contextmanager
def stage(nc):
    with ExitStack() as stack:
        with nc.Block() as block:
            yield stack, block


def runs(semaphores):
    numbers = sorted(s.num for s in semaphores)
    starts = [n for n in numbers if n - 1 not in numbers]
    ends = [n + 1 for n in numbers if n + 1 not in numbers]
    return [range(a, b) for a, b in zip(starts, ends)]


def inverse_root(pool, c, value, op, constant, summed, n, ready):
    pool.tensor_scalar(value, value, constant, None, op).then_inc(summed, 1)
    pool.wait_ge(summed, n)
    pool.tensor_tensor(value, value, c.minus_half[0:value.shape[0], 0:1].to_broadcast(list(value.shape)), ALU.pow).then_inc(ready, 1)


def row(ap_1d, partitions=P):
    n = ap_1d.shape[0]
    return ap_1d.rearrange("(a n) -> a n", a=1).to_broadcast([partitions, n])


def make_constants(nc, c, x):
    with ExitStack() as stack:
        m = Memory(nc, stack, "const")
        filled = m.sem("filled")
        done = m.sem("done")
        block = stack.enter_context(nc.Block())

        @block.sync
        def _(sp):
            sp.dma_start(c.x[:], x.rearrange("b (t p) d -> p (b t) d", p=P)).then_inc(c.x_loaded, 16)

        @block.gpsimd
        def _(pool):
            pool.memset(c.ident[:], 0.0).then_inc(filled, 1)
            pool.memset(c.before[:], 1.0).then_inc(filled, 1)
            pool.memset(c.row0[:], 1.0).then_inc(filled, 1)
            pool.memset(c.ones_b[:], 1.0).then_inc(done, 1)
            pool.memset(c.ones_f[:], 1.0).then_inc(done, 1)
            pool.memset(c.minus_half[:], -0.5).then_inc(done, 1)
            pool.wait_ge(filled, 3)
            pool.affine_select(out=c.ident[:], in_=c.ident[:], compare_op=ALU.not_equal, fill=1.0, base=0,
                               pattern=[[-1, P]], channel_multiplier=1).then_inc(done, 1)
            pool.affine_select(out=c.before[:], in_=c.before[:], compare_op=ALU.is_gt, fill=0.0, base=0,
                               pattern=[[1, P]], channel_multiplier=-1).then_inc(done, 1)
            pool.affine_select(out=c.row0[:], in_=c.row0[:], compare_op=ALU.is_ge, fill=0.0, base=0,
                               pattern=[[0, P]], channel_multiplier=-1).then_inc(done, 1)
            pool.wait_ge(done, 6)


def relative_bias(nc, c, layers):
    with ExitStack() as stack:
        m = Memory(nc, stack, "rel")
        J = range(len(layers))

        def each(name, shape, dt=F32):
            return [m.sb(f"{name}{j}", shape, dt) for j in J]

        w0, b0, g0, b1, g1 = (each(n, [P, D]) for n in ("w0", "b0", "g0", "b1", "g1"))
        w1, w2, b2 = each("w1", [P, KD, D]), each("w2", [P, KD, H]), each("b2", [H, 1])
        dist_i, dist = m.sb("dist_i", [P, QT], I32), m.sb("dist", [P, QT])
        hid, act, act_t = each("hid", [P, QT, D]), each("act", [P, QT, D]), each("act_t", [P, KD, S])
        stats, mv = each("stats", [P, QT, 6]), each("mv", [P, QT, 2])
        out_row = each("out_row", [H, REV])
        t_ps = [m.ps(f"t_ps{j}", [P, KD, S]) for j in J]
        h_ps = [m.ps(f"h_ps{j}", [P, QT, D]) for j in J]
        o_ps = [h_ps[j][0:H, 0:S // D, :].rearrange("p t d -> p (t d)") for j in J]
        loaded = [m.sem(f"loaded{j}") for j in J]
        rev_stored = [m.sem(f"rev_stored{j}") for j in J]
        names = "dist_made link mv_ready rooting rstd_ready pre_ready act_ready t_ready t_copied h_ready o_ready row_ready".split()
        (dist_made, link_s, mv_ready, rooting, rstd_ready, pre_ready, act_ready, t_ready, t_copied, h_ready, o_ready, row_ready) = (m.sem(x) for x in names)
        block = stack.enter_context(nc.Block())
        N = len(layers)

        @block.sync
        def _(sp):
            for j, (w, _) in enumerate(layers):
                for dst, src in ((w0, w["w0"].rearrange("a n -> (a n)")), (b0, w["b0"]), (g0, w["g0"]), (b1, w["b1"]), (g1, w["g1"])):
                    sp.dma_start(dst[j][:], row(src)).then_inc(loaded[j], 16)
                sp.dma_start(w1[j][:], w["w1"].rearrange("(k p) n -> p k n", p=P)).then_inc(loaded[j], 16)
                sp.dma_start(w2[j][:], w["w2"].rearrange("(k p) n -> p k n", p=P)).then_inc(loaded[j], 16)
                sp.dma_start(b2[j][:], w["b2"].rearrange("(n a) -> n a", a=1)).then_inc(loaded[j], 16)
            for j, (_, rev) in enumerate(layers):
                sp.wait_ge(row_ready, N + j + 1)
                sp.dma_start(rev, out_row[j][:]).then_inc(rev_stored[j], 16)
            for j in J:
                sp.wait_ge(rev_stored[j], 16)

        @block.gpsimd
        def _(pool):
            pool.iota(dist_i[:], pattern=[[-P, QT]], base=S - 1, channel_multiplier=-1).then_inc(dist_made, 1)
            for n in range(2):
                for j in J:
                    pool.wait_ge(mv_ready, QT * (N * n + j + 1))
                    inverse_root(pool, c, mv[j][:, :, 1], ALU.add, EPS, rooting, N * n + j + 1, rstd_ready)

        @block.vector
        def _(dve):
            linked = [0]

            def link(ins):
                linked[0] += 1
                ins.then_inc(link_s, 1)
                dve.wait_ge(link_s, linked[0])

            def statistics(j):
                for t in range(QT):
                    nc.vector.bn_stats(stats[j][:, t, :], hid[j][:, t, :]).then_inc(link_s, 1)
                linked[0] += QT
                dve.wait_ge(link_s, linked[0])
                for t in range(QT):
                    nc.vector.bn_aggr(mv[j][:, t, :], stats[j][:, t, :]).then_inc(mv_ready, 1)

            def normalise(n, j, g):
                dve.wait_ge(rstd_ready, N * n + j + 1)
                for t in range(QT):
                    nc.vector.tensor_scalar(hid[j][:, t, :], hid[j][:, t, :], mv[j][:, t, 0:1], mv[j][:, t, 1:2],
                                            ALU.subtract, ALU.mult).then_inc(link_s, 1)
                linked[0] += QT
                dve.wait_ge(link_s, linked[0])
                nc.vector.tensor_tensor(hid[j][:], hid[j][:], g[:].unsqueeze(1).to_broadcast([P, QT, D]), ALU.mult).then_inc(pre_ready, 1)

            def copy_turned(n, j):
                dve.wait_ge(t_ready, N * n + j + 1)
                for k in range(KD):
                    nc.vector.tensor_copy(act_t[j][:, k, :], t_ps[j][:, k, :]).then_inc(t_copied, 1)

            dve.wait_ge(dist_made, 1)
            link(nc.vector.tensor_copy(dist[:], dist_i[:]))
            for j in J:
                nc.vector.memset(out_row[j][:, S:REV], NEG).then_inc(row_ready, 1)
            for j in J:
                dve.wait_ge(loaded[j], 16 * 8)
                for t in range(QT):
                    nc.vector.scalar_tensor_tensor(out=hid[j][:, t, :], in0=w0[j][:], scalar=dist[:, t:t + 1], in1=b0[j][:],
                                                   op0=ALU.mult, op1=ALU.add).then_inc(link_s, 1)
                linked[0] += QT
                dve.wait_ge(link_s, linked[0])
                statistics(j)
            for j in J:
                normalise(0, j, g0[j])
            for j in J:
                copy_turned(0, j)
            for j in J:
                dve.wait_ge(h_ready, j + 1)
                dve.wait_ge(act_ready, j + 1)
                link(nc.vector.tensor_tensor(hid[j][:], h_ps[j][:], b1[j][:].unsqueeze(1).to_broadcast([P, QT, D]), ALU.add))
                statistics(j)
            for j in J:
                normalise(1, j, g1[j])
            for j in J:
                copy_turned(1, j)
            for j in J:
                dve.wait_ge(o_ready, j + 1)
                nc.vector.tensor_scalar(out_row[j][:, 0:S], o_ps[j], b2[j][:, 0:1], None, ALU.add).then_inc(row_ready, 1)

        @block.scalar
        def _(a):
            for n in range(2):
                for j in J:
                    a.wait_ge(pre_ready, N * n + j + 1)
                    if n:
                        a.wait_ge(t_ready, j + 1)
                    nc.scalar.activation(act[j][:], hid[j][:], ACT.Silu).then_inc(act_ready, 1)

        @block.tensor
        def _(pe):
            for n in range(2):
                for j in J:
                    pe.wait_ge(act_ready, N * n + j + 1)
                    if n:
                        pe.wait_ge(t_copied, KD * (j + 1))
                    for k in range(KD):
                        for t in range(QT):
                            last = nc.tensor.transpose(t_ps[j][:, k, t * P:(t + 1) * P], act[j][:, t, k * P:(k + 1) * P], c.ident[:])
                    last.then_inc(t_ready, 1)
                for j in J:
                    pe.wait_ge(t_copied, KD * (N * n + j + 1))
                    if n == 0:
                        pe.wait_ge(loaded[j], 16 * 8)
                        for t in range(QT):
                            for k in range(KD):
                                last = nc.tensor.matmul(h_ps[j][:, t, :], act_t[j][:, k, t * P:(t + 1) * P], w1[j][:, k, :],
                                                        start=(k == 0), stop=(k == KD - 1))
                        last.then_inc(h_ready, 1)
                    else:
                        for k in range(KD):
                            last = nc.tensor.matmul(o_ps[j], w2[j][:, k, :], act_t[j][:, k, :], start=(k == 0), stop=(k == KD - 1))
                        last.then_inc(o_ready, 1)


def attention_inputs(nc, c, l, w, cond, mask, stack, block):
    cosine = l != 0
    m = Memory(nc, stack, f"in{l}")
    g = m.sb("g", [P, KD])
    wkv = m.sb("wkv", [P, KD, 2 * DH])
    mask_w = m.sb("mask_w", [1, T // 4], mybir.dt.uint32)
    mask_u = mask_w[:].bitcast(U8)
    null_k = m.sb("null_k", [1, DH])
    qs, ks = m.sb("qs", [P, DH]), m.sb("ks", [P, DH])
    stats, mv = m.sb("stats", [P, B, QT, 6]), m.sb("mv", [P, B, QT, 2])
    xn = c.h
    kf, ksq, kn = m.sb("kf", [P, B, QT, DH]), m.sb("ksq", [P, QT, DH]), m.sb("kn", [P, B, QT])
    kdup = [m.sb(f"kdup{n}", [P, QT, 2, DH]) for n in range(2)]
    nsq, nn, nkdup = m.sb("nsq", [1, DH]), m.sb("nn", [1, 1]), m.sb("nkdup", [1, 2, DH])
    x_ps = [m.ps(f"x_ps{n}", [P, KD, S]) for n in range(2)]
    kv_ps = [m.ps(f"kv_ps{n}", [P, QT, 2 * DH]) for n in range(2)]
    kt_ps = m.ps("kt_ps", [P, S])
    nk_ps = m.ps("nk_ps", [P, 1])
    loaded, cleared, link_s = m.sem("loaded"), m.sem("cleared"), m.sem("link")
    xn_ready, xt_ready, xt_copied = m.sem("xn_ready"), m.sem("xt_ready"), m.sem("xt_copied")
    kv_ready, kv_read, kdup_ready = m.sem("kv_ready"), m.sem("kv_read"), m.sem("kdup_ready")
    kt_ready, kt_copied, null_ready, nk_ready, nk_copied = (m.sem(s) for s in ("kt_ready", "kt_copied", "null_ready", "nk_ready", "nk_copied"))
    mv_ready, rooting, rstd_ready, square_ready, floored, root_ready = (m.sem(s) for s in ("mv_ready", "rooting", "rstd_ready", "square_ready", "floored", "root_ready"))
    n_loads = 6 + (2 if cosine else 0)

    def kt_ps_of(b):
        return kt_ps if b % 2 == 0 else x_ps[0][:, 0, :]


    @block.sync
    def _(sp):
        sp.dma_start(g[:], w["g"].rearrange("(k p) -> p k", p=P)).then_inc(loaded, 16)
        sp.dma_start(wkv[:], w["Wkv"].rearrange("(k p) n -> p k n", p=P)).then_inc(loaded, 16)
        sp.dma_start(mask_w[:], mask.rearrange("b s -> (b s)").rearrange("(a n) -> a n", a=1)).then_inc(loaded, 16)
        sp.dma_start(null_k[:], cond[0:1, :]).then_inc(loaded, 16)
        if cosine:
            sp.dma_start(qs[:], row(w["q_scale"])).then_inc(loaded, 16)
            sp.dma_start(ks[:], row(w["k_scale"])).then_inc(loaded, 16)
        sp.dma_start(c.null_bias[:], row(w["null_attn_bias"])).then_inc(loaded, 16)
        sp.dma_start(c.wq[:], w["Wq"].rearrange("(k p) n -> p k n", p=P)).then_inc(loaded, 16)

    @block.gpsimd
    def _(pool):
        pool.memset(c.kt[:], 0.0).then_inc(cleared, 1)
        pool.memset(c.kmask[:], 0.0).then_inc(cleared, 1)

        def root(n, t):
            pool.wait_ge(square_ready, n)
            inverse_root(pool, c, t, ALU.max, 1e-24, floored, n, root_ready)

        for b in range(B):
            pool.wait_ge(mv_ready, QT * (b + 1))
            inverse_root(pool, c, mv[:, b, :, 1], ALU.add, EPS, rooting, b + 1, rstd_ready)
        if cosine:
            root(1, nn[:])
            for b in range(B):
                root(b + 2, kn[:, b, :])

    @block.vector
    def _(dve):
        linked = [0]

        def link(ins):
            linked[0] += 1
            ins.then_inc(link_s, 1)
            dve.wait_ge(link_s, linked[0])

        def null_and_mask():
            dve.wait_ge(loaded, 16 * n_loads)
            dve.wait_ge(cleared, 2)
            link(nc.vector.tensor_scalar(c.kmask[0:1, :, 1:], mask_u.rearrange("a (b s) -> a b s", b=B), 1.0, -NEG,
                                         ALU.subtract, ALU.mult))
            pair = null_k[:].unsqueeze(1).to_broadcast([1, 2, DH])
            if cosine:
                link(nc.vector.scalar_tensor_tensor(out=ks[:], in0=qs[:], scalar=8.0, in1=ks[:], op0=ALU.mult, op1=ALU.mult))
                link(nc.vector.tensor_tensor(nsq[:], null_k[:], null_k[:], ALU.mult))
                nc.vector.tensor_reduce(nn[:], nsq[:], AX.X, ALU.add).then_inc(square_ready, 1)
                dve.wait_ge(root_ready, 1)
                link(nc.vector.tensor_scalar(null_k[:], null_k[:], nn[:, 0:1], None, ALU.mult))
                nc.vector.tensor_tensor(nkdup[:], pair, ks[0:1, :].unsqueeze(1).to_broadcast([1, 2, DH]), ALU.mult).then_inc(null_ready, 1)
            else:
                nc.vector.tensor_scalar(nkdup[:], pair, DH ** -0.5, None, ALU.mult).then_inc(null_ready, 1)

        def statistics(b):
            if l == 0:
                dve.wait_ge(c.x_loaded, 16)
            for t in range(QT):
                nc.vector.bn_stats(stats[:, b, t, :], c.x[:, QT * b + t, :]).then_inc(link_s, 1)
            linked[0] += QT
            dve.wait_ge(link_s, linked[0])
            for t in range(QT):
                nc.vector.bn_aggr(mv[:, b, t, :], stats[:, b, t, :]).then_inc(mv_ready, 1)

        def normalise(b):
            dve.wait_ge(rstd_ready, b + 1)
            for t in range(QT):
                nc.vector.tensor_scalar(xn[:, QT * b + t, :], c.x[:, QT * b + t, :], mv[:, b, t, 0:1], mv[:, b, t, 1:2],
                                        ALU.subtract, ALU.mult).then_inc(xn_ready, 1)

        def square_keys(b):
            dve.wait_ge(kv_read, 2 * (b + 1))
            dve.wait_ge(square_ready, b + 1)
            link(nc.vector.tensor_tensor(ksq[:], kf[:, b, :, :], kf[:, b, :, :], ALU.mult))
            nc.vector.tensor_reduce(kn[:, b, :], ksq[:], AX.X, ALU.add).then_inc(square_ready, 1)

        def keys(b):
            dve.wait_ge(kv_read, 2 * (b + 1))
            if cosine:
                dve.wait_ge(root_ready, b + 2)
                link(nc.vector.tensor_tensor(kf[:, b, :, :], kf[:, b, :, :], kn[:, b, :].unsqueeze(2).to_broadcast([P, QT, DH]), ALU.mult))
            if b >= 2:
                dve.wait_ge(kt_ready, b - 1)
            for n in range(2):
                if cosine:
                    nc.vector.tensor_tensor(kdup[b % 2][:, :, n, :], kf[:, b, :, :], ks[:].unsqueeze(1).to_broadcast([P, QT, DH]), ALU.mult).then_inc(kdup_ready, 1)
                else:
                    nc.vector.tensor_scalar(kdup[b % 2][:, :, n, :], kf[:, b, :, :], DH ** -0.5, None, ALU.mult).then_inc(kdup_ready, 1)

        statistics(0)
        for b in range(B):
            if b + 1 < B:
                statistics(b + 1)
            normalise(b)
        null_and_mask()
        if cosine:
            for b in range(B):
                square_keys(b)
        for b in range(B):
            keys(b)

    @block.scalar
    def _(a):
        a.wait_ge(loaded, 16 * n_loads)
        a.wait_ge(cleared, 2)
        for b in range(B + 1):
            if b < B:
                a.wait_ge(xt_ready, b + 1)
                for k in range(KD):
                    nc.scalar.activation(c.xt[:, k, S * b:S * (b + 1)], x_ps[b % 2][:, k, :], ACT.Copy,
                                         scale=g[:, k:k + 1]).then_inc(xt_copied, 1)
            if b >= 1:
                v = b - 1
                a.wait_ge(kv_ready, v + 1)
                nc.scalar.activation(kf[:, v, :, :], kv_ps[v % 2][:, :, 0:DH], ACT.Copy).then_inc(kv_read, 1)
                nc.scalar.activation(c.v[:, QT * v:QT * (v + 1), :], kv_ps[v % 2][:, :, DH:], ACT.Copy).then_inc(kv_read, 1)
        a.wait_ge(nk_ready, 1)
        for n in range(2):
            h = slice(DH * n, DH * (n + 1))
            nc.scalar.activation(c.kt[h, n, :, 0], nk_ps[h, :].to_broadcast([DH, B]), ACT.Copy).then_inc(nk_copied, 1)
        for b in range(B):
            a.wait_ge(kt_ready, b + 1)
            for n in range(2):
                h = slice(DH * n, DH * (n + 1))
                nc.scalar.activation(c.kt[h, n, b, 1:], kt_ps_of(b)[h, :], ACT.Copy).then_inc(kt_copied, 1)
        a.wait_ge(kt_copied, 2 * B)
        a.wait_ge(nk_copied, 2)

    @block.tensor
    def _(pe):
        for b in range(B + 1):
            if b < B:
                pe.wait_ge(xn_ready, QT * (b + 1))
                if b >= 2:
                    pe.wait_ge(xt_copied, KD * (b - 1))
                for k in range(KD):
                    for t in range(QT):
                        last = nc.tensor.transpose(x_ps[b % 2][:, k, t * P:(t + 1) * P], xn[:, QT * b + t, k * P:(k + 1) * P], c.ident[:])
                last.then_inc(xt_ready, 1)
            if b >= 1:
                pe.wait_ge(xt_copied, KD * b)
                if b == 1:
                    pe.wait_ge(loaded, 16 * n_loads)
                if b >= 3:
                    pe.wait_ge(kv_read, 2 * (b - 2))
                for t in range(QT):
                    tok = slice(S * (b - 1) + t * P, S * (b - 1) + (t + 1) * P)
                    for k in range(KD):
                        last = nc.tensor.matmul(kv_ps[(b - 1) % 2][:, t, :], c.xt[:, k, tok], wkv[:, k, :], start=(k == 0), stop=(k == KD - 1))
                last.then_inc(kv_ready, 1)
        pe.wait_ge(null_ready, 1)
        nc.tensor.matmul(nk_ps[:], nkdup[:].rearrange("a n d -> a (n d)"), c.ident[0:1, 0:1], start=True, stop=True).then_inc(nk_ready, 1)
        for b in range(B):
            pe.wait_ge(kdup_ready, 2 * (b + 1))
            if b >= 2:
                pe.wait_ge(kt_copied, 2 * (b - 1))
            for t in range(QT):
                last = nc.tensor.transpose(kt_ps_of(b)[:, t * P:(t + 1) * P], kdup[b % 2][:, t, :, :].rearrange("p n d -> p (n d)"), c.ident[:])
            last.then_inc(kt_ready, 1)


def rounds(engine, n, one):
    one(0, True, False)
    with engine.Fori(1, n - 1) as i:
        one(i, False, False)
    one(n - 1, False, True)


def counted(engine, value):
    return value if isinstance(value, int) else engine.to_reg(value)


def attention(nc, c, l, bias_of, causal_select):
    cosine = l != 0
    U = QT * B * 2
    SU = B * 2
    N = 4
    LAG = 3
    DRAIN = 6
    with ExitStack() as stack:
        m = Memory(nc, stack, f"att{l}")
        bias = [[m.sb(f"bias{hh}{q}", [P, NKEY[q]]) for q in range(QT)] for hh in range(2)]
        q_sb = m.sb("q_sb", [P, B, 2, DH])
        sq = m.sb("sq", [P, B, 2, DH]) if cosine else None
        qn = m.sb("qn", [P, B, 2])
        q_t = [m.sb(f"q_t{n}", [P, B, P]) for n in range(2)]
        sc = [c.h[:, QT * n:QT * (n + 1), :].rearrange("p t d -> p (t d)") for n in range(N)]
        pr = [m.sb(f"pr{n}", [P, NKEY[-1]]) for n in range(N)]
        pt = [m.sb(f"pt{n}", [P, S]) for n in range(N)]
        nmax, rsum = m.sb("nmax", [P, 2, SU]), m.sb("rsum", [P, 2, SU])
        pnull = m.sb("pnull", [P, 2, SU])
        rinv = m.sb("rinv", [P, 2, SU])
        rexp = m.sb("rexp", [P, B, 2, DH])
        rb_sb = m.sb("rb_sb", [P, B, P])
        s_ps = m.ps("s_ps", [P, 4 * 512])
        rb_ps = s_ps[:, 768:768 + B * P]
        pt_ps = [m.ps(f"pt_ps{n}", [P, S]) for n in range(2)]
        o_ps = m.ps("o_ps", [P, B, P])
        q_ps = m.ps("q_ps", [P, B, P])
        bias_loaded = [[m.sem(f"bias_loaded{hh}{q}") for q in range(QT)] for hh in range(2)]
        names = ("bias_ready s_ready s_read p_ready pt_ready pt_copied_a pt_copied_v pv_done q_ready q_squared q_kept "
                 "qt_ready qt_copied rinv_ready rexp_ready rb_ready rb_copied out_ready null_kept null_out qn_summed qn_floored qn_ready").split()
        (bias_ready, s_ready, s_read, p_ready, pt_ready, pt_copied_a, pt_copied_v, pv_done, q_ready, q_squared, q_kept,
         qt_ready, qt_copied, rinv_ready, rexp_ready, rb_ready, rb_copied, out_ready, null_kept, null_out, qn_summed, qn_floored, qn_ready) = (m.sem(x) for x in names)
        block = stack.enter_context(nc.Block())
        units = [(u // SU, (u % SU) // 2, u % 2) for u in range(U)]

        def scores_ap(u, q):
            first = ((512 - 257) if u % 2 == 0 else 1024 + 256) if q == QT - 1 else (0, 3 * 512)[u % 2]
            return s_ps[:, first:first + NKEY[q]]

        @block.sync
        def _(sp):
            def load(i, hh, q):
                sp.dma_start(bias[hh][q][:, 1:], bias_of(i, hh, q)).then_inc(bias_loaded[hh][q], 16)

            if cosine:
                sp.wait_ge(c.bands_stored, 32)
            for q in range(QT):
                for hh in range(2):
                    load(0, hh, q)
            with sp.Fori(0, HP - 1) as i:
                for q in range(QT):
                    uses = sp.to_reg(i * U + SU * (q + 1))
                    sp.wait_ge(s_read, 1)
                    sp.wait_ge(s_read, uses)
                    for hh in range(2):
                        load(i + 1, hh, q)

        @block.gpsimd
        def _(pool):
            def finish_bias(i, q):
                for hh in range(2):
                    loads = counted(pool, i * 16 + 16)
                    pool.wait_ge(bias_loaded[hh][q], 16)
                    pool.wait_ge(bias_loaded[hh][q], loads)
                    if causal_select:
                        diag = bias[hh][q][:, 1 + P * q:1 + P * (q + 1)]
                        pool.affine_select(out=diag, in_=diag, compare_op=ALU.is_ge, fill=NEG, base=0,
                                           pattern=[[-1, P]], channel_multiplier=1).then_inc(bias_ready, 1)
                    pool.tensor_copy(bias[hh][q][:, 0:1], c.null_bias[:, ds(i * 2 + hh, 1)]).then_inc(bias_ready, 1)

            def root_q(n):
                if cosine:
                    sums = counted(pool, n + 1)
                    pool.wait_ge(qn_summed, 1)
                    pool.wait_ge(qn_summed, sums)
                    inverse_root(pool, c, qn[:], ALU.max, 1e-24, qn_floored, n + 1, qn_ready)

            def one(i, first, last):
                for u in range(U + (DRAIN if last else 0)):
                    q, at = u // SU, u % SU
                    more = u < U and not (last and q == QT - 1)
                    if u < U:
                        if at == 0 and not (first and q < 2):
                            pool.wait_ge(null_out, i * QT + q - 1)
                        if at == 1 and more:
                            finish_bias(i + (q + 1) // QT, (q + 1) % QT)
                        if at == 2 and more:
                            root_q(i * QT + (q + 1))
                        made = counted(pool, i * U + u + 1)
                        pool.wait_ge(p_ready, 1)
                        pool.wait_ge(p_ready, made)
                        pool.tensor_copy(pnull[:, q % 2, at:at + 1], pr[u % N][:, 0:1]).then_inc(null_kept, 1)
                    if at == 5 and not (first and q == 0):
                        p, half = q - 1, (q - 1) % 2
                        pool.wait_ge(rinv_ready, i * QT + q)
                        pool.wait_ge(null_kept, i * U + SU * q)
                        pool.tensor_tensor(c.p_null[:, :, p % QT, ds((i + p // QT) * 2, 2)],
                                           pnull[:, half, :].rearrange("p (b n) -> p b n", n=2),
                                           rinv[:, half, :].rearrange("p (b n) -> p b n", n=2), ALU.mult).then_inc(null_out, 1)

            root_q(0)
            finish_bias(0, 0)
            rounds(pool, HP, one)
            pool.wait_ge(null_out, HP * QT)

        per_step_bias = 4 if causal_select else 2

        @block.vector
        def _(dve):
            def sum_q(n):
                if cosine:
                    dve.wait_ge(q_squared, n + 1)
                    nc.vector.tensor_reduce(qn[:], sq[:], AX.X, ALU.add).then_inc(qn_summed, 1)

            def keep_q(n):
                if cosine:
                    dve.wait_ge(qn_ready, n + 1)
                    nc.vector.tensor_tensor(q_sb[:], q_ps[:].rearrange("p b (n d) -> p b n d", n=2),
                                            qn[:].unsqueeze(3).to_broadcast([P, B, 2, DH]), ALU.mult).then_inc(q_kept, 1)

            def one(i, first, last):
                for u in range(U + (DRAIN if last else 0)):
                    q, at = u // SU, u % SU
                    more = u < U and not (last and q == QT - 1)
                    v = u - LAG - 1
                    if v % 2 and v < U and not (first and v < 0):
                        n = P * (v % U // SU + 1)
                        dve.wait_ge(pt_ready, i * U + v + 1)
                        if not (first and v < N):
                            dve.wait_ge(pv_done, i * (U // 2) + v // 2 - 1)
                        nc.vector.tensor_copy(pt[v % N][:, 0:n], pt_ps[v % 2][:, 0:n]).then_inc(pt_copied_v, 1)
                    if u < U:
                        hh = units[u][2]
                        if at == 0:
                            biases = counted(dve, i * (QT * per_step_bias) + per_step_bias * (q + 1))
                        scored, read = counted(dve, i * U + u + 1), counted(dve, i * U + u - N + 1)
                        dve.wait_ge(s_ready, 1)
                        if at == 0:
                            dve.wait_ge(bias_ready, biases)
                        dve.wait_ge(s_ready, scored)
                        if not (first and u < N):
                            dve.wait_ge(p_ready, read)
                        nc.vector.tensor_tensor_reduce(sc[u % N][:, 0:NKEY[q]], scores_ap(u, q), bias[hh][q][:], -1.0, 3e38,
                                                       ALU.add, ALU.min, nmax[:, q % 2, at:at + 1]).then_inc(s_read, 1)
                    if at == 2 and more:
                        sum_q(i * QT + (q + 1))
                    if at == 4 and more:
                        keep_q(i * QT + (q + 1))
                    if at == 1 and not (first and q == 0):
                        half = (q - 1) % 2
                        dve.wait_ge(p_ready, i * U + SU * q)
                        if not (first and q < 3):
                            dve.wait_ge(null_out, i * QT + q - 2)
                        nc.vector.reciprocal(rinv[:, half, :], rsum[:, half, :]).then_inc(rinv_ready, 1)
                        dve.wait_ge(rinv_ready, i * QT + q)
                        if not (first and q < 2):
                            dve.wait_ge(rb_ready, i * QT + q - 1)
                        nc.vector.tensor_copy(rexp[:], rinv[:, half, :].rearrange("p (b n) -> p b n", n=2).unsqueeze(3)
                                              .to_broadcast([P, B, 2, DH])).then_inc(rexp_ready, 1)
                    if at == 5 and not (first and q == 0):
                        p = q - 1
                        dve.wait_ge(rb_copied, i * QT + q)
                        dve.wait_ge(pv_done, i * (U // 2) + B * q)
                        nc.vector.tensor_tensor(c.out_t[:, ds(i + p // QT, 1), :].rearrange("p a (b q s) -> p (a b) q s", b=B, q=QT)[:, :, p % QT, :],
                                                o_ps[:], rb_sb[:], ALU.mult).then_inc(out_ready, 1)

            sum_q(0)
            keep_q(0)
            rounds(dve, HP, one)
            dve.wait_ge(out_ready, HP * QT)

        @block.scalar
        def _(a):
            def take_q(n):
                a.wait_ge(q_ready, n + 1)
                if cosine:
                    nc.scalar.activation(sq[:], q_ps[:].rearrange("p b (n d) -> p b n d", n=2), ACT.Square).then_inc(q_squared, 1)
                else:
                    nc.scalar.activation(q_sb[:], q_ps[:].rearrange("p b (n d) -> p b n d", n=2), ACT.Copy).then_inc(q_kept, 1)

            def take_qt(n, half):
                a.wait_ge(qt_ready, n + 1)
                nc.scalar.activation(q_t[half][:], q_ps[:], ACT.Copy).then_inc(qt_copied, 1)

            def one(i, first, last):
                for u in range(U + (DRAIN if last else 0)):
                    q, at = u // SU, u % SU
                    more = u < U and not (last and q == QT - 1)
                    v = u - LAG - 1
                    if v % 2 == 0 and v < U and not (first and v < 0):
                        n = P * (v % U // SU + 1)
                        a.wait_ge(pt_ready, i * U + v + 1)
                        if not (first and v < N):
                            a.wait_ge(pv_done, i * (U // 2) + v // 2 - 1)
                        nc.scalar.activation(pt[v % N][:, 0:n], pt_ps[v % 2][:, 0:n], ACT.Copy).then_inc(pt_copied_a, 1)
                    if at == 1 and more:
                        take_q(i * QT + (q + 1))
                    if at == 6 and more:
                        take_qt(i * QT + (q + 1), (q + 1) % 2)
                    if u < U:
                        a.wait_ge(s_read, i * U + u + 1)
                        if not (first and u < N):
                            a.wait_ge(null_kept, i * U + u - N + 1)
                            a.wait_ge(pt_ready, i * U + u - N + 1)
                        nc.scalar.activation(pr[u % N][:, 0:NKEY[q]], sc[u % N][:, 0:NKEY[q]], ACT.Exp, scale=-1.0,
                                             bias=nmax[:, q % 2, at:at + 1],
                                             accum_out=rsum[:, q % 2, at:at + 1]).then_inc(p_ready, 1)
                    if at == 2 and not (first and q == 0):
                        a.wait_ge(rb_ready, i * QT + q)
                        if not (first and q < 2):
                            a.wait_ge(out_ready, i * QT + q - 1)
                        nc.scalar.activation(rb_sb[:].rearrange("p b n -> p (b n)"), rb_ps, ACT.Copy).then_inc(rb_copied, 1)

            take_q(0)
            take_qt(0, 0)
            rounds(a, HP, one)

        @block.tensor
        def _(pe):
            def project_q(i, q):
                for b in range(B):
                    tok = slice(S * b + P * q, S * b + P * (q + 1))
                    for k in range(KD):
                        last = nc.tensor.matmul(q_ps[:, b, :], c.xt[:, k, tok], c.wq[:, k, ds(i * P, P)], start=(k == 0), stop=(k == KD - 1))
                last.then_inc(q_ready, 1)

            def turn_q(n):
                pe.wait_ge(q_kept, n + 1)
                for b in range(B):
                    last = nc.tensor.transpose(q_ps[:, b, :], q_sb[:, b, :, :].rearrange("p n d -> p (n d)"), c.ident[:])
                last.then_inc(qt_ready, 1)

            def one(i, first, last_round):
                for u in range(U + (DRAIN if last_round else 0)):
                    q, at = u // SU, u % SU
                    more = u < U and not (last_round and q == QT - 1)
                    if u < U:
                        _, b, hh = units[u]
                        if at == 0:
                            pe.wait_ge(qt_copied, i * QT + q + 1)
                        if not (first and u < 2):
                            pe.wait_ge(s_read, i * U + u - 1)
                        if q == QT - 1 and at == 3:
                            pe.wait_ge(rb_copied, i * QT + q)
                        out = scores_ap(u, q)
                        cuts = [0, 257 - u % 2, NKEY[q]] if q == QT - 1 else [0, NKEY[q]]
                        for lo, hi in zip(cuts, cuts[1:]):
                            nc.tensor.matmul(out[:, lo:hi], c.row0[:], c.kmask[:, b, lo:hi], start=True, stop=False)
                            last = nc.tensor.matmul(out[:, lo:hi], q_t[q % 2][:, b, :], c.kt[:, hh, b, lo:hi], start=False, stop=True)
                        last.then_inc(s_ready, 1)
                    if at == 0 and more:
                        project_q(i + (q + 1) // QT, (q + 1) % QT)
                    v = u - LAG
                    if v < U and not (first and v < 0):
                        pe.wait_ge(p_ready, i * U + v + 1)
                        if not (first and v < 2):
                            pe.wait_ge(pt_copied_v if v % 2 else pt_copied_a, i * (U // 2) + v // 2)
                        for kb in range(v % U // SU + 1):
                            last = nc.tensor.transpose(pt_ps[v % 2][:, P * kb:P * (kb + 1)], pr[v % N][:, 1 + P * kb:1 + P * (kb + 1)], c.ident[:])
                        last.then_inc(pt_ready, 1)
                    v = u - LAG - 2
                    if v % 2 and v < U and not (first and v < 0):
                        qv, bv, _ = units[v % U]
                        pe.wait_ge(pt_copied_a, i * (U // 2) + v // 2 + 1)
                        pe.wait_ge(pt_copied_v, i * (U // 2) + v // 2 + 1)
                        if v % SU == 1 and not (first and v < SU):
                            pe.wait_ge(out_ready, i * QT + v // SU)
                        for kb in range(qv + 1):
                            for hv in range(2):
                                last = nc.tensor.matmul(o_ps[DH * hv:DH * (hv + 1), bv, :], c.v[:, QT * bv + kb, :],
                                                        pt[(v - 1 + hv) % N][:, P * kb:P * (kb + 1)], start=(kb == 0), stop=(kb == qv))
                        last.then_inc(pv_done, 1)
                    if at == 5 and more:
                        turn_q(i * QT + q + 1)
                    if at == 2 and not (first and q == 0):
                        pe.wait_ge(rexp_ready, i * QT + q)
                        if q == QT - 1:
                            pe.wait_ge(s_read, i * U + u + 1)
                        if not (first and q < 2):
                            pe.wait_ge(rb_copied, i * QT + q - 1)
                        for b in range(B):
                            last = nc.tensor.transpose(rb_ps[:, P * b:P * (b + 1)], rexp[:, b, :, :].rearrange("p n d -> p (n d)"), c.ident[:])
                        last.then_inc(rb_ready, 1)

            project_q(0, 0)
            turn_q(0)
            rounds(pe, HP, one)


def attention_output(nc, c, l, w_out, g_out, cond, later, stack, block):
    m = Memory(nc, stack, f"out{l}")
    wo = m.sb("wo", [P, HP, D])
    g = m.sb("g", [P, D])
    null_v = m.sb("null_v", [P, 1])
    null_cols = m.sb("null_cols", [P, HP, H])
    null_w = m.sb("null_w", [H, D])
    pn_t = m.sb("pn_t", [H, 2, S])
    yn = m.sb("yn", [P, 2, QT, D])
    stats, mv = m.sb("stats", [P, QT, 6]), m.sb("mv", [P, QT, 2])
    y_ps = [m.ps(f"y_ps{n}", [P, QT, D]) for n in range(2)]
    two_banks = m.ps("two_banks", [P, KD, S])
    pn_ps, nw_ps = two_banks[:, 0, :], two_banks[:, 1, 0:D]
    loaded, cleared, cols_ready, nw_ready, nw_copied = (m.sem(x) for x in ("loaded", "cleared", "cols_ready", "nw_ready", "nw_copied"))
    pn_ready, pn_copied, y_ready, yn_ready, h_ready, link_s = (m.sem(x) for x in ("pn_ready", "pn_copied", "y_ready", "yn_ready", "h_ready", "link"))
    mv_ready, rooting, rstd_ready = m.sem("mv_ready"), m.sem("rooting"), m.sem("rstd_ready")

    @block.sync
    def _(sp):
        sp.dma_start(wo[:], w_out.rearrange("(c p) n -> p c n", p=P)).then_inc(loaded, 16)
        sp.dma_start(g[:], row(g_out)).then_inc(loaded, 16)
        for n in range(2):
            sp.dma_start(null_v[DH * n:DH * (n + 1), :], cond[1:2, :].rearrange("a d -> d a")).then_inc(loaded, 16)
        for dst, src, semaphore in later:
            sp.dma_start(dst, src).then_inc(semaphore, 16)

    @block.gpsimd
    def _(pool):
        pool.memset(null_cols[:], 0.0).then_inc(cleared, 1)
        pool.wait_ge(loaded, 64)
        for b in range(B):
            pool.wait_ge(mv_ready, QT * (b + 1))
            inverse_root(pool, c, mv[:, :, 1], ALU.add, EPS, rooting, b + 1, rstd_ready)
            pool.wait_ge(yn_ready, QT * (b + 1))
            pool.tensor_tensor(c.h[:, QT * b:QT * (b + 1), :], yn[:, b % 2, :, :], g[:].unsqueeze(1).to_broadcast([P, QT, D]),
                               ALU.mult).then_inc(h_ready, 1)
        pool.wait_ge(h_ready, B)

    @block.scalar
    def _(a):
        a.wait_ge(nw_ready, 1)
        nc.scalar.activation(null_w[:], nw_ps[0:H, :], ACT.Copy).then_inc(nw_copied, 1)
        for b in range(B):
            a.wait_ge(pn_ready, b + 1)
            if b >= 2:
                a.wait_ge(y_ready, b - 1)
            nc.scalar.activation(pn_t[:, b % 2, :], pn_ps[0:H, :], ACT.Copy).then_inc(pn_copied, 1)

    @block.vector
    def _(dve):
        linked = [0]

        def link(ins):
            linked[0] += 1
            ins.then_inc(link_s, 1)
            dve.wait_ge(link_s, linked[0])

        dve.wait_ge(loaded, 64)
        dve.wait_ge(cleared, 1)
        flat = null_cols[:].rearrange("p c h -> p (c h)")
        for n in range(2):
            rows = slice(DH * n, DH * (n + 1))
            nc.vector.tensor_copy(flat[rows, n:n + (H + 2) * (HP - 1) + 1:H + 2], null_v[rows, :].to_broadcast([DH, HP])).then_inc(cols_ready, 1)
        for b in range(B):
            dve.wait_ge(y_ready, b + 1)
            for t in range(QT):
                nc.vector.bn_stats(stats[:, t, :], y_ps[b % 2][:, t, :]).then_inc(link_s, 1)
            linked[0] += QT
            dve.wait_ge(link_s, linked[0])
            for t in range(QT):
                nc.vector.bn_aggr(mv[:, t, :], stats[:, t, :]).then_inc(mv_ready, 1)
            dve.wait_ge(rstd_ready, b + 1)
            if b >= 2:
                dve.wait_ge(h_ready, b - 1)
            for t in range(QT):
                nc.vector.tensor_scalar(yn[:, b % 2, t, :], y_ps[b % 2][:, t, :], mv[:, t, 0:1], mv[:, t, 1:2],
                                        ALU.subtract, ALU.mult).then_inc(yn_ready, 1)

    @block.tensor
    def _(pe):
        pe.wait_ge(loaded, 64)
        pe.wait_ge(cols_ready, 2)
        for p in range(HP):
            last = nc.tensor.matmul(nw_ps[0:H, :], null_cols[:, p, :], wo[:, p, :], start=(p == 0), stop=(p == HP - 1))
        last.then_inc(nw_ready, 1)
        for b in range(B):
            if b >= 1:
                pe.wait_ge(pn_copied, b)
            for q in range(QT):
                last = nc.tensor.transpose(pn_ps[0:H, P * q:P * (q + 1)], c.p_null[:, b, q, :], c.ident[:])
            last.then_inc(pn_ready, 1)
            if b >= 2:
                pe.wait_ge(yn_ready, QT * (b - 1))
            if b == 0:
                pe.wait_ge(nw_copied, 1)
            pe.wait_ge(pn_copied, b + 1)
            for q in range(QT):
                for p in range(HP):
                    nc.tensor.matmul(y_ps[b % 2][:, q, :], c.out_t[:, p, S * b + P * q:S * b + P * (q + 1)], wo[:, p, :],
                                     start=(p == 0), stop=False)
                last = nc.tensor.matmul(y_ps[b % 2][:, q, :], pn_t[:, b % 2, P * q:P * (q + 1)], null_w[:], start=False, stop=True)
            last.then_inc(y_ready, 1)

    return h_ready, two_banks, y_ps, yn_ready


class TernaryLinear:

    def __init__(self, nc, c, weight, stack):
        m = Memory(nc, stack, "ter")
        self.nc, self.c, self.weight = nc, c, weight
        self.w, self.w_t = m.sb("w", [P, KD, D]), m.sb("w_t", [P, KD, D])
        self.part, self.scale = m.sb("part", [P, 1]), m.sb("scale", [P, 1])
        self.h_t = m.sb("h_t", [P, 2, KD, S])
        self.s_ps = m.ps("s_ps", [P, 1])
        names = "loaded part_ready sum_ready w_ready wt_ready wt_copied ht_ready ht_copied y_ready x_ready link".split()
        (self.loaded, self.part_ready, self.sum_ready, self.w_ready, self.wt_ready, self.wt_copied, self.ht_ready, self.ht_copied,
         self.y_ready, self.x_ready, self.link_s) = (m.sem(x) for x in names)

    def prepare(self, block):
        nc, c, w, part, scale = self.nc, self.c, self.w, self.part, self.scale
        ROUND = 12582912.0

        @block.sync
        def _(sp):
            sp.dma_start(w[:], self.weight.rearrange("(k p) n -> p k n", p=P)).then_inc(self.loaded, 16)

        @block.vector
        def _(dve):
            linked = [0]

            def link(ins):
                linked[0] += 1
                ins.then_inc(self.link_s, 1)
                dve.wait_ge(self.link_s, linked[0])

            dve.wait_ge(self.loaded, 16)
            nc.vector.tensor_reduce(part[:], w[:], AX.XY, ALU.add, apply_absolute_value=True).then_inc(self.part_ready, 1)
            dve.wait_ge(self.sum_ready, 1)
            link(nc.vector.tensor_scalar(scale[:], self.s_ps[:], 1.0 / (D * D), EPS, ALU.mult, ALU.max))
            link(nc.vector.reciprocal(part[:], scale[:]))
            link(nc.vector.tensor_scalar(w[:], w[:], part[:, 0:1], ROUND, ALU.mult, ALU.add))
            link(nc.vector.tensor_scalar(w[:], w[:], ROUND, -1.0, ALU.subtract, ALU.max))
            nc.vector.tensor_scalar(w[:], w[:], 1.0, None, ALU.min).then_inc(self.w_ready, 1)

        @block.tensor
        def _(pe):
            pe.wait_ge(self.part_ready, 1)
            nc.tensor.matmul(self.s_ps[:], c.ones_f[:], part[:], start=True, stop=True).then_inc(self.sum_ready, 1)

    def apply(self, block, h_ready, h_ps, y_ps, y_read):
        nc, c, w, w_t, h_t = self.nc, self.c, self.w, self.w_t, self.h_t

        @block.vector
        def _(dve):
            for b in range(B):
                dve.wait_ge(self.y_ready, b + 1)
                nc.vector.scalar_tensor_tensor(out=c.x[:, QT * b:QT * (b + 1), :], in0=y_ps[b % 2][:], scalar=self.scale[:, 0:1],
                                               in1=c.x[:, QT * b:QT * (b + 1), :], op0=ALU.mult, op1=ALU.add).then_inc(self.x_ready, 1)
            dve.wait_ge(self.x_ready, B)

        @block.scalar
        def _(a):
            a.wait_ge(self.wt_ready, 1)
            for k in range(KD):
                nc.scalar.activation(w_t[:, k, :], h_ps[:, k, 0:D], ACT.Copy).then_inc(self.wt_copied, 1)
            for b in range(B):
                a.wait_ge(self.ht_ready, b + 1)
                if b >= 2:
                    a.wait_ge(self.y_ready, b - 1)
                for k in range(KD):
                    nc.scalar.activation(h_t[:, b % 2, k, :], h_ps[:, k, :], ACT.Copy).then_inc(self.ht_copied, 1)

        @block.tensor
        def _(pe):
            pe.wait_ge(self.w_ready, 1)
            for k in range(KD):
                for o in range(KD):
                    last = nc.tensor.transpose(h_ps[:, k, P * o:P * (o + 1)], w[:, o, P * k:P * (k + 1)], c.ident[:])
            last.then_inc(self.wt_ready, 1)
            pe.wait_ge(self.wt_copied, KD)
            for b in range(B):
                pe.wait_ge(h_ready, b + 1)
                if b >= 1:
                    pe.wait_ge(self.ht_copied, KD * b)
                for k in range(KD):
                    for t in range(QT):
                        last = nc.tensor.transpose(h_ps[:, k, P * t:P * (t + 1)], c.h[:, QT * b + t, P * k:P * (k + 1)], c.ident[:])
                last.then_inc(self.ht_ready, 1)
                pe.wait_ge(self.ht_copied, KD * (b + 1))
                if b < 2:
                    pe.wait_ge(y_read, QT * (B - 1 + b))
                else:
                    pe.wait_ge(self.x_ready, b - 1)
                for t in range(QT):
                    for k in range(KD):
                        last = nc.tensor.matmul(y_ps[b % 2][:, t, :], h_t[:, b % 2, k, P * t:P * (t + 1)], w_t[:, k, :],
                                                start=(k == 0), stop=(k == KD - 1))
                last.then_inc(self.y_ready, 1)


class Shared:
    pass


def shared(nc, stack):
    c = Shared()
    m = Memory(nc, stack, "all")
    c.ident, c.ones_f, c.minus_half = m.sb("ident", [P, P]), m.sb("ones_f", [P, P]), m.sb("minus_half", [P, 1])
    c.before, c.row0, c.ones_b = m.sb("before", [P, P], BF16), m.sb("row0", [P, P], BF16), m.sb("ones_b", [P, P], BF16)
    c.x, c.h = m.sb("x", [P, NT, D]), m.sb("h", [P, NT, D])
    c.xt = m.sb("xt", [P, KD, T])
    c.zero = m.sb("zero", [P, D])
    c.x_loaded, c.bands_stored, c.rows_cleared = m.sem("x_loaded"), m.sem("bands_stored"), m.sem("rows_cleared")
    return c


def attention_memory(nc, stack, c, l):
    m = Memory(nc, stack, f"mem{l}")
    c.kt = m.sb("kt", [P, 2, B, NKEY[-1]])
    c.v = m.sb("v", [P, NT, DH])
    c.wq = m.sb("wq", [P, KD, H * DH])
    c.kmask = m.sb("kmask", [P, B, NKEY[-1]], BF16)
    c.null_bias = m.sb("null_bias", [P, H])
    c.p_null = m.sb("p_null", [P, B, QT, H])
    c.out_t = m.sb("out_t", [P, HP, T])


def band_bias(band):
    def bias_of(i, hh, q):
        return band[ds(i * 2 + hh, 1), :, P * (QT - 1 - q):S].rearrange("a p n -> (a p) n")
    return bias_of


class Mixture:

    def __init__(self, name, top, cap, hidden, temperature=1.0, normalised=False, by_rows=False, gate=False):
        self.name, self.top, self.cap, self.hidden = name, top, cap, hidden
        self.temperature, self.normalised, self.by_rows, self.gate = temperature, normalised, by_rows, gate
        self.tiles = E * cap // P if cap else top * NT + E
        self.rows = self.tiles * P


def route(nc, c, mx, src, w_router, sorted_rows, r, ahead, stack, block, after=None, beside=None, cond=None, w_cond=None):
    m = Memory(nc, stack, f"route_{mx.name}")
    wr = m.sb("wr", [P, KD, E])
    wr_rows = m.sb("wr_rows", [E, D])
    g_t, wg_t = m.sb("g_t", [DH, B]), m.sb("wg_t", [DH, E])
    lg, ex = m.sb("lg", [P, NT, E]), m.sb("ex", [P, NT, E])
    top = [m.sb(f"top{k}", [P, NT]) for k in range(mx.top)]
    hot = [m.sb(f"hot{k}", [P, NT, E]) for k in range(mx.top)]
    tmp, tmp2, red, total = m.sb("tmp", [P, NT, E]), m.sb("tmp2", [P, NT, E]), m.sb("red", [P, NT]), m.sb("total", [P, NT])
    sel = m.sb("sel", [P, NT + 1, E], BF16)
    desc_i, desc = m.sb("desc_i", [P, E], I32), m.sb("desc", [P, E])
    base_i, base = m.sb("base_i", [P, E], I32), m.sb("base", [P, E])
    edge_i, edge = m.sb("edge_i", [P, NT], I32), m.sb("edge", [P, NT])
    tile_i, tile_n = m.sb("tile_i", [P, mx.tiles], I32), m.sb("tile_n", [P, mx.tiles])
    over, ntile, cum = m.sb("over", [P, E, NT]), m.sb("ntile", [P, E]), m.sb("cum", [P, E])
    before_t, owner = m.sb("before_t", [P, mx.tiles, E]), m.sb("owner", [P, mx.tiles])
    rank = m.sb("rank", [P, NT, E])
    pos_f = m.sb("pos_f", [P, NT])
    full = [m.sb(f"full{k}", [P, NT]) for k in range(mx.top)]
    x_ps = [m.ps(f"x_ps{n}", [P, S]) for n in range(2)]
    l_ps, r_ps = m.ps("l_ps", [P, NT, E]), m.ps("r_ps", [P, NT + 1, E])
    w_ps = r_ps[:, 0:KD, :]
    names = "loaded iota_ready iota_f wt_ready wr_ready xt_ready xt_copied logits_ready lg_ready exp_ready sel_ready rank_ready pos_ready link".split()
    (loaded, iota_ready, iota_f, wt_ready, wr_ready, xt_ready, xt_copied, logits_ready, lg_ready, exp_ready, sel_ready, rank_ready,
     pos_ready, link_s) = (m.sem(x) for x in names)
    scattered, scattered_0 = m.pool_dma_sem("scattered", NT * mx.top)
    n_loads = 3 if cond is not None else 1

    @block.sync
    def _(sp):
        if mx.by_rows:
            sp.dma_start(wr_rows[:], w_router).then_inc(loaded, 16)
        else:
            sp.dma_start(wr[:], w_router.rearrange("(k p) e -> p k e", p=P)).then_inc(loaded, 16)
        if cond is not None:
            sp.dma_start(g_t[:], cond.rearrange("b g -> g b")).then_inc(loaded, 16)
            sp.dma_start(wg_t[:], w_cond.rearrange("e g -> g e")).then_inc(loaded, 16)
        for dst, weight, semaphore in ahead:
            sp.dma_start(dst, weight).then_inc(semaphore, 16)

    @block.gpsimd
    def _(pool):
        pool.iota(desc_i[:], pattern=[[-1, E]], base=E, channel_multiplier=0).then_inc(iota_ready, 1)
        pool.iota(base_i[:], pattern=[[mx.cap, E]], base=0, channel_multiplier=0).then_inc(iota_ready, 1)
        pool.iota(edge_i[:], pattern=[[P, NT]], base=0, channel_multiplier=0).then_inc(iota_ready, 1)
        pool.iota(tile_i[:], pattern=[[1, mx.tiles]], base=0, channel_multiplier=0).then_inc(iota_ready, 1)
        pool.memset(sel[:], 0.0).then_inc(iota_ready, 1)
        pool.wait_ge(iota_ready, 5)
        for dst, s in ((desc, desc_i), (base, base_i), (edge, edge_i), (tile_n, tile_i)):
            pool.tensor_copy(dst[:], s[:]).then_inc(iota_f, 1)
        pool.wait_ge(c.rows_cleared, 16)
        for k in range(mx.top):
            pool.wait_ge(pos_ready, k + 1)
            for t in range(NT):
                pool.indirect_dma_start(sorted_rows, bass.IndirectOffsetOnAxis(ap=r.pos[k][:, t:t + 1], axis=0), src[:, t, :], None,
                                        bounds_check=mx.rows - 1, oob_is_err=False).then_inc(scattered, 16)
        pool.wait_ge(scattered, scattered_0 + 16 * NT * mx.top)

    @block.scalar
    def _(a):
        if mx.by_rows:
            a.wait_ge(wt_ready, 1)
            nc.scalar.activation(wr[:], w_ps, ACT.Copy).then_inc(wr_ready, 1)
        for b in range(B):
            for k in range(KD):
                a.wait_ge(xt_ready, KD * b + k + 1)
                nc.scalar.activation(c.xt[:, k, S * b:S * (b + 1)], x_ps[k][:], ACT.Copy).then_inc(xt_copied, 1)
        a.wait_ge(lg_ready, 1)
        nc.scalar.activation(ex[:], ex[:], ACT.Exp, scale=mx.temperature).then_inc(exp_ready, 1)
        if beside is not None:
            beside.scalar(a)

    @block.tensor
    def _(pe):
        if mx.by_rows:
            pe.wait_ge(loaded, 16 * n_loads)
            for k in range(KD):
                last = nc.tensor.transpose(w_ps[:, k, :], wr_rows[:, P * k:P * (k + 1)], c.ident[0:E, 0:E])
            last.then_inc(wt_ready, 1)
        for b in range(B + 1):
            if b < B:
                if after is not None:
                    pe.wait_ge(after[0], after[1] * QT * (b + 1))
                for k in range(KD):
                    if b >= 1:
                        pe.wait_ge(xt_copied, KD * (b - 1) + k + 1)
                    for t in range(QT):
                        last = nc.tensor.transpose(x_ps[k][:, P * t:P * (t + 1)], src[:, QT * b + t, P * k:P * (k + 1)], c.ident[:])
                    last.then_inc(xt_ready, 1)
            if b >= 1:
                pe.wait_ge(xt_copied, KD * b)
                if b == 1:
                    pe.wait_ge(loaded, 16 * n_loads)
                    if mx.by_rows:
                        pe.wait_ge(wr_ready, 1)
                for t in range(QT * (b - 1), QT * b):
                    for k in range(KD):
                        last = nc.tensor.matmul(l_ps[:, t, :], c.xt[:, k, P * t:P * (t + 1)], wr[:, k, :], start=(k == 0),
                                                stop=(k == KD - 1 and cond is None))
                    if cond is not None:
                        last = nc.tensor.matmul(l_ps[:, t, :], g_t[:, b - 1:b].to_broadcast([DH, P]), wg_t[:], start=False, stop=True)
        last.then_inc(logits_ready, 1)
        pe.wait_ge(sel_ready, 1)
        nc.tensor.matmul(r_ps[:], c.before[:], sel[:], start=True, stop=False)
        for t in range(NT):
            last = nc.tensor.matmul(r_ps[:, t + 1:, :], c.ones_b[:], sel[:, t:t + 1, :].to_broadcast([P, NT - t, E]), start=False, stop=(t == NT - 1))
        last.then_inc(rank_ready, 1)
        if beside is not None:
            beside.tensor(pe)

    @block.vector
    def _(dve):
        linked = [0]
        V = nc.vector

        def link(ins):
            linked[0] += 1
            ins.then_inc(link_s, 1)
            dve.wait_ge(link_s, linked[0])

        def wide(t):
            return t[:].unsqueeze(2).to_broadcast([P, NT, E])

        def per_expert(t):
            return t[:].unsqueeze(1).to_broadcast([P, NT, E])

        dve.wait_ge(logits_ready, 1)
        dve.wait_ge(iota_f, 4)
        link(V.tensor_copy(lg[:], l_ps[:]))
        for k in range(mx.top):
            link(V.tensor_reduce(top[k][:], lg[:], AX.X, ALU.max))
            if k == 0:
                link(V.tensor_tensor(ex[:], lg[:], wide(top[0]), ALU.subtract))
                dve.sem_inc(lg_ready, 1)
            link(V.tensor_tensor(tmp[:], lg[:], wide(top[k]), ALU.is_ge))
            link(V.tensor_tensor(tmp[:], tmp[:], per_expert(desc), ALU.mult))
            link(V.tensor_reduce(red[:], tmp[:], AX.X, ALU.max))
            link(V.tensor_tensor(hot[k][:], tmp[:], wide(red), ALU.is_equal))
            if k + 1 < mx.top:
                link(V.scalar_tensor_tensor(out=lg[:], in0=hot[k][:], scalar=2 * NEG, in1=lg[:], op0=ALU.mult, op1=ALU.add))
        if mx.top == 2:
            V.tensor_tensor(sel[:, 0:NT, :], hot[0][:], hot[1][:], ALU.add).then_inc(sel_ready, 1)
        else:
            V.tensor_copy(sel[:, 0:NT, :], hot[0][:]).then_inc(sel_ready, 1)
        dve.wait_ge(rank_ready, 1)
        link(V.tensor_copy(rank[:], r_ps[:, 0:NT, :]))
        if not mx.cap:
            link(V.tensor_copy(base[:], r_ps[:, NT, :]))
            link(V.tensor_tensor(over[:], base[:].unsqueeze(2).to_broadcast([P, E, NT]), edge[:].unsqueeze(1).to_broadcast([P, E, NT]), ALU.is_gt))
            link(V.tensor_reduce(ntile[:], over[:], AX.X, ALU.add))
            link(V.tensor_copy(cum[:], ntile[:]))
            for e in range(1, E):
                link(V.tensor_tensor(cum[:, e:e + 1], cum[:, e:e + 1], cum[:, e - 1:e], ALU.add))
            link(V.tensor_tensor(base[:], cum[:], ntile[:], ALU.subtract))
            link(V.tensor_scalar(base[:], base[:], float(P), None, ALU.mult))
        link(V.tensor_tensor(tmp2[:], rank[:], per_expert(base), ALU.add))
        for k in range(mx.top):
            link(V.tensor_tensor(tmp[:], tmp2[:], hot[k][:], ALU.mult))
            link(V.tensor_reduce(pos_f[:], tmp[:], AX.X, ALU.add))
            if mx.cap:
                link(V.tensor_tensor(tmp[:], rank[:], hot[k][:], ALU.mult))
                link(V.tensor_reduce(red[:], tmp[:], AX.X, ALU.add))
                link(V.tensor_scalar(full[k][:], red[:], float(mx.cap), None, ALU.is_ge))
                link(V.scalar_tensor_tensor(out=pos_f[:], in0=full[k][:], scalar=float(1 << 20), in1=pos_f[:], op0=ALU.mult, op1=ALU.add))
            V.tensor_copy(r.pos[k][:], pos_f[:]).then_inc(pos_ready, 1)
            dve.wait_ge(pos_ready, k + 1)
        if not mx.cap:
            link(V.tensor_tensor(before_t[:], tile_n[:].unsqueeze(2).to_broadcast([P, mx.tiles, E]), cum[:].unsqueeze(1).to_broadcast([P, mx.tiles, E]), ALU.is_ge))
            link(V.tensor_reduce(owner[:], before_t[:], AX.X, ALU.add))
            link(V.tensor_scalar(owner[:], owner[:], float(E - 1), None, ALU.min))
            link(V.tensor_copy(r.owner[:], owner[:]))
        dve.wait_ge(exp_ready, 1)
        link(V.tensor_reduce(total[:], ex[:], AX.X, ALU.add))
        link(V.reciprocal(total[:], total[:]))
        for k in range(mx.top):
            link(V.tensor_tensor(tmp[:], ex[:], hot[k][:], ALU.mult))
            link(V.tensor_reduce(red[:], tmp[:], AX.X, ALU.add))
            link(V.tensor_tensor(r.weight[k][:], red[:], total[:], ALU.mult))
        if mx.normalised:
            link(V.scalar_tensor_tensor(out=total[:], in0=r.weight[0][:], scalar=1e-20, in1=r.weight[1][:], op0=ALU.add, op1=ALU.add))
            link(V.reciprocal(total[:], total[:]))
            for k in range(mx.top):
                link(V.tensor_tensor(r.weight[k][:], r.weight[k][:], total[:], ALU.mult))
        if mx.cap:
            for k in range(mx.top):
                link(V.tensor_scalar(red[:], full[k][:], -1.0, 1.0, ALU.mult, ALU.add))
                link(V.tensor_tensor(r.weight[k][:], r.weight[k][:], red[:], ALU.mult))
        if beside is not None:
            beside.vector(dve)


class CapacityWeights:

    def __init__(self, nc, stack, mx, w1, w2):
        m = Memory(nc, stack, f"cw_{mx.name}")
        self.w1_sb = [m.sb(f"w1_{n}", [P, KD, mx.hidden]) for n in range(2)]
        self.w2_sb = [m.sb(f"w2_{n}", [P, mx.hidden // P, D]) for n in range(2)]
        self.w1_loaded, self.w2_loaded = ([m.sem(f"{x}_loaded{n}") for n in range(2)] for x in ("w1", "w2"))
        self.w1, self.w2 = w1.rearrange("e (k p) f -> e p k f", p=P), w2.rearrange("e (k p) f -> e p k f", p=P)
        self.loads = []
        for n in range(2):
            self.loads += [(self.w1_sb[n][:], self.w1[n], self.w1_loaded[n]), (self.w2_sb[n][:], self.w2[n], self.w2_loaded[n])]


def experts_by_capacity(nc, c, mx, cw, sorted_rows, expert_rows, r, func, bias=None):
    cap, F = mx.cap, mx.hidden
    FC, CT = F // P, cap // P
    w1_sb, w2_sb, w1_loaded, w2_loaded = cw.w1_sb, cw.w2_sb, cw.w1_loaded, cw.w2_loaded
    with ExitStack() as stack:
        m = Memory(nc, stack, f"exp_{mx.name}")
        xs = [m.sb(f"xs{n}", [P, CT, D]) for n in range(2)]
        xs_t = [m.sb(f"xs_t{n}", [P, KD, cap]) for n in range(2)]
        hid = [m.sb(f"hid{n}", [P, FC, cap]) for n in range(2)]
        ys = [m.sb(f"ys{n}", [P, CT, D]) for n in range(2)]
        x_ps = [m.ps(f"x_ps{k}", [P, S]) for k in range(KD)]
        h_ps = [m.ps(f"h_ps{n}", [P, S]) for n in range(4)]
        y_ps = [m.ps(f"y_ps{n}", [P, 2, D]) for n in range(2)]
        xs_loaded = [m.sem(f"xs_loaded{n}") for n in range(2)]
        bias_sb = m.sb("bias", [P, D]) if bias is not None else None
        names = "xt_ready xt_copied h_ready hid_ready y_ready y_copied bias_loaded prepared".split()
        (xt_ready, xt_copied, h_ready, hid_ready, y_ready, y_copied, bias_loaded, prepared) = (m.sem(x) for x in names)
        m.start_at_one(xt_copied, h_ready, hid_ready, y_ready, y_copied)
        stored, stored_0 = zip(*(m.pool_dma_sem(f"stored{n}", E // 2) for n in range(2)))
        block = stack.enter_context(nc.Block())
        R = E // 2
        YT = max(CT // 2, 1)
        x_rows = sorted_rows[0:mx.rows, :].rearrange("(e t p) d -> e p t d", e=E, p=P)
        y_rows = expert_rows[0:mx.rows, :].rearrange("(e t p) d -> e p t d", e=E, p=P)

        @block.sync
        def _(sp):
            def load_rows(e, n):
                sp.dma_start(xs[n][:], x_rows[ds(e, 1)].rearrange("a p t d -> (a p) t d")).then_inc(xs_loaded[n], 16)

            for n in range(2):
                load_rows(n, n)
            if bias is not None:
                sp.dma_start(bias_sb[:], row(bias.rearrange("a b d -> (a b d)"))).then_inc(bias_loaded, 16)
            with sp.Fori(0, R - 1) as i:
                for n in range(2):
                    done = sp.to_reg(i * (2 * YT) + YT * (n + 1) + 1)
                    sp.wait_ge(y_ready, 1)
                    sp.wait_ge(y_ready, done)
                    e = i * 2 + 2 + n
                    load_rows(e, n)
                    sp.dma_start(w1_sb[n][:], cw.w1[ds(e, 1)].rearrange("a p k f -> (a p) k f")).then_inc(w1_loaded[n], 16)
                    sp.dma_start(w2_sb[n][:], cw.w2[ds(e, 1)].rearrange("a p k f -> (a p) k f")).then_inc(w2_loaded[n], 16)

        @block.gpsimd
        def _(pool):
            for rows in r.rows:
                pool.memset(rows[:], 0.0).then_inc(prepared, 1)
            if bias is not None:
                pool.wait_ge(bias_loaded, 16)
                pool.tensor_tensor(c.x[:], c.x[:], bias_sb[:].unsqueeze(1).to_broadcast([P, NT, D]), ALU.add).then_inc(prepared, 1)
            if r.rows:
                pool.wait_ge(prepared, len(r.rows) + (bias is not None))
            with pool.Fori(0, R) as i:
                for n in range(2):
                    done = pool.to_reg(i * (2 * YT) + YT * (n + 1) + 1)
                    pool.wait_ge(y_copied, 1)
                    pool.wait_ge(y_copied, done)
                    pool.dma_start(y_rows[ds(i * 2 + n, 1)].rearrange("a p t d -> (a p) t d"), ys[n][:]).then_inc(stored[n], 16)
            for n in range(2):
                pool.wait_ge(stored[n], stored_0[n] + 16 * R)

        @block.tensor
        def _(pe):
            def turn(i, n):
                pe.wait_ge(xs_loaded[n], i * 16 + 16)
                for k in range(KD):
                    pe.wait_ge(xt_copied, i * (2 * KD) + KD * n + 1)
                    for t in range(CT):
                        last = nc.tensor.transpose(x_ps[k][:, P * t:P * (t + 1)], xs[n][:, t, P * k:P * (k + 1)], c.ident[:])
                    last.then_inc(xt_ready, 1)

            def first_products(i, n):
                pe.wait_ge(w1_loaded[n], i * 16 + 16)
                pe.wait_ge(xt_copied, i * (2 * KD) + KD * (n + 1) + 1)
                for f in range(FC):
                    pe.wait_ge(hid_ready, i * (2 * FC) + max(FC * n + f - 3, 0) + 1)
                    for k in range(KD):
                        last = nc.tensor.matmul(h_ps[f % 4][:, 0:cap], w1_sb[n][:, k, P * f:P * (f + 1)], xs_t[n][:, k, :],
                                                start=(k == 0), stop=(k == KD - 1))
                    last.then_inc(h_ready, 1)

            def second_products(i, n):
                pe.wait_ge(w2_loaded[n], i * 16 + 16)
                for t in range(CT):
                    if t % 2 == 0:
                        pe.wait_ge(y_copied, i * (2 * YT) + max(YT * n + t // 2 - 1, 0) + 1)
                    for f in range(FC):
                        if t == 0:
                            pe.wait_ge(hid_ready, i * (2 * FC) + FC * n + f + 1 + 1)
                        last = nc.tensor.matmul(y_ps[(YT * n + t // 2) % 2][:, t % 2, :], hid[n][:, f, P * t:P * (t + 1)], w2_sb[n][:, f, :],
                                                start=(f == 0), stop=(f == FC - 1))
                    if t % 2:
                        last.then_inc(y_ready, 1)

            def one(i, last):
                first_products(i, 0)
                turn(i, 1)
                second_products(i, 0)
                first_products(i, 1)
                if not last:
                    turn(i + 1, 0)
                second_products(i, 1)

            turn(0, 0)
            with pe.Fori(0, R - 1) as i:
                one(i, False)
            one(R - 1, True)

        @block.vector
        def _(dve):
            def take_x(i, n):
                for k in range(KD):
                    dve.wait_ge(xt_ready, i * (2 * KD) + KD * n + k + 1)
                    dve.wait_ge(h_ready, i * (2 * FC) + 1)
                    nc.vector.tensor_copy(xs_t[n][:, k, :], x_ps[k][:, 0:cap]).then_inc(xt_copied, 1)

            def take_y(i, n):
                for y in range(YT):
                    dve.wait_ge(y_ready, i * (2 * YT) + YT * n + y + 1 + 1)
                    dve.wait_ge(stored[n], i * 16 + stored_0[n])
                    nc.vector.tensor_copy(ys[n][:, 2 * y:2 * y + 2, :], y_ps[(YT * n + y) % 2][:]).then_inc(y_copied, 1)

            def one(i, last):
                take_x(i, 1)
                take_y(i, 0)
                if not last:
                    take_x(i + 1, 0)
                take_y(i, 1)

            take_x(0, 0)
            with dve.Fori(0, R - 1) as i:
                one(i, False)
            one(R - 1, True)

        @block.scalar
        def _(a):
            with a.Fori(0, R) as i:
                for n in range(2):
                    for f in range(FC):
                        a.wait_ge(h_ready, i * (2 * FC) + FC * n + f + 1 + 1)
                        a.wait_ge(y_ready, i * (2 * YT) + 1)
                        nc.scalar.activation(hid[n][:, f, :], h_ps[f % 4][:, 0:cap], func).then_inc(hid_ready, 1)


class TileWeights:

    def __init__(self, nc, stack, mx, weights):
        m = Memory(nc, stack, f"tw_{mx.name}")
        F, FC = mx.hidden, mx.hidden // P
        self.wa = m.sb("wa", [P, E * KD, F])
        self.wb = m.sb("wb", [P, E * KD, F])
        self.wd = m.sb("wd", [P, E * FC, D])
        self.loaded = m.sem("loaded")
        self.loads = [(t[:], w.rearrange("e (k p) f -> p (e k) f", p=P), self.loaded)
                      for t, w in zip((self.wa, self.wb, self.wd), weights)]


def experts_by_tile(nc, c, mx, tw, sorted_rows, expert_rows, r):
    F = mx.hidden
    FC = F // P
    G = 4
    wa, wb, wd = tw.wa, tw.wb, tw.wd
    with ExitStack() as stack:
        m = Memory(nc, stack, f"til_{mx.name}")
        xs = [m.sb(f"xs{n}", [P, D]) for n in range(G)]
        xs_t = [m.sb(f"xs_t{n}", [P, KD, P]) for n in range(2)]
        act = [m.sb(f"act{n}", [P, F]) for n in range(2)]
        lin = [m.sb(f"lin{n}", [P, F]) for n in range(2)] if mx.gate else None
        hid = [m.sb(f"hid{n}", [P, F]) for n in range(2)]
        hid_t = [m.sb(f"hid_t{n}", [P, FC, P]) for n in range(2)]
        ys = [m.sb(f"ys{n}", [P, D]) for n in range(G)]
        a_ps = [m.ps(f"a_ps{n}", [P, 512]) for n in range(2)]
        b_ps = [m.ps(f"b_ps{n}", [P, 512]) for n in range(2)]
        x_ps = m.ps("x_ps", [P, KD, P])
        t_ps = m.ps("t_ps", [P, FC, P])
        y_ps = [m.ps(f"y_ps{n}", [P, D]) for n in range(2)]
        xs_loaded = [m.sem(f"xs_loaded{n}") for n in range(G)]
        R = mx.tiles // G
        stored, stored_0 = zip(*(m.pool_dma_sem(f"stored{n}", R) for n in range(G)))
        names = "xt_ready xt_copied ab_ready act_ready lin_ready hid_ready ht_ready ht_copied y_ready y_copied".split()
        (xt_ready, xt_copied, ab_ready, act_ready, lin_ready, hid_ready, ht_ready, ht_copied, y_ready, y_copied) = (m.sem(x) for x in names)
        block = stack.enter_context(nc.Block())
        x_rows = sorted_rows[0:mx.rows, :].rearrange("(t p) d -> t p d", p=P)
        y_rows = expert_rows[0:mx.rows, :].rearrange("(t p) d -> t p d", p=P)

        @block.sync
        def _(sp):
            def load(t, n):
                sp.dma_start(xs[n][:], x_rows[ds(t, 1)].rearrange("a p d -> (a p) d")).then_inc(xs_loaded[n], 16)

            for n in range(G):
                load(n, n)
            with sp.Fori(0, R - 1) as i:
                for n in range(G):
                    turned = sp.to_reg(i * G + n + 1)
                    sp.wait_ge(xt_ready, 1)
                    sp.wait_ge(xt_ready, turned)
                    load(i * G + G + n, n)

        @block.gpsimd
        def _(pool):
            with pool.Fori(0, R) as i:
                for n in range(G):
                    done = pool.to_reg(i * G + n + 1)
                    pool.wait_ge(y_copied, 1)
                    pool.wait_ge(y_copied, done)
                    pool.dma_start(y_rows[ds(i * G + n, 1)].rearrange("a p d -> (a p) d"), ys[n][:]).then_inc(stored[n], 16)
            for n in range(G):
                pool.wait_ge(stored[n], stored_0[n] + 16 * R)

        @block.tensor
        def _(pe):
            def expert_of(t):
                return pe.value_load(r.owner[0:1, ds(t, 1)], min_val=0, max_val=E - 1)

            def turn_x(i, n, first):
                pe.wait_ge(xs_loaded[n % G], i * 16 + 16 * (n // G + 1))
                for k in range(KD):
                    last = nc.tensor.transpose(x_ps[:, k, :], xs[n % G][:, P * k:P * (k + 1)], c.ident[:])
                last.then_inc(xt_ready, 1)

            def first_products(i, n, first, expert):
                pe.wait_ge(xt_copied, i * G + n + 1)
                for ps, w in ((a_ps, wa), (b_ps, wb)):
                    for k in range(KD):
                        last = nc.tensor.matmul(ps[n % 2][:, 0:F], xs_t[n % 2][:, k, :], w[:].rearrange("p (e k) f -> p k e f", k=KD)[:, k, ds(expert, 1), :].rearrange("p a f -> p (a f)"),
                                                start=(k == 0), stop=(k == KD - 1))
                last.then_inc(ab_ready, 1)

            def turn_hidden(i, n, first):
                pe.wait_ge(hid_ready, i * G + n + 1)
                for f in range(FC):
                    last = nc.tensor.transpose(t_ps[:, f, :], hid[n % 2][:, P * f:P * (f + 1)], c.ident[:])
                last.then_inc(ht_ready, 1)

            def last_product(i, n, first, expert):
                pe.wait_ge(ht_copied, i * G + n + 1)
                if not (first and n < 2):
                    pe.wait_ge(y_copied, i * G + n - 1)
                for f in range(FC):
                    last = nc.tensor.matmul(y_ps[n % 2][:], hid_t[n % 2][:, f, :], wd[:].rearrange("p (e k) f -> p k e f", k=FC)[:, f, ds(expert, 1), :].rearrange("p a f -> p (a f)"),
                                            start=(f == 0), stop=(f == FC - 1))
                last.then_inc(y_ready, 1)

            def one(i, first, last):
                for n in range(G + (2 if last else 0)):
                    if n < G:
                        first_products(i, n, first, expert_of(i * G + n))
                    if n + 1 < G or not last:
                        turn_x(i, n + 1, first)
                    if not (first and n < 2):
                        last_product(i, n - 2, first, expert_of(i * G + n - 2))
                    if n < G + 1 and not (first and n < 1):
                        turn_hidden(i, n - 1, first)

            turn_x(0, 0, True)
            pe.wait_ge(tw.loaded, 48)
            rounds(pe, R, one)

        @block.scalar
        def _(a):
            def one(i, first, last):
                for n in range(G + (2 if last else 0)):
                    if n < G:
                        a.wait_ge(ab_ready, i * G + n + 1)
                        if not (first and n < 2):
                            a.wait_ge(hid_ready, i * G + n - 1)
                            if mx.gate:
                                a.wait_ge(lin_ready, i * G + n - 1)
                        nc.scalar.activation(act[n % 2][:], a_ps[n % 2][:, 0:F], ACT.Copy if mx.gate else ACT.Silu).then_inc(act_ready, 1)
                    if n < G + 1 and not (first and n < 1):
                        v = n - 1
                        a.wait_ge(ht_ready, i * G + v + 1)
                        if not (first and v < 2):
                            a.wait_ge(y_ready, i * G + v - 1)
                        nc.scalar.activation(hid_t[v % 2][:], t_ps[:], ACT.Copy).then_inc(ht_copied, 1)
                    if not (first and n < 2):
                        v = n - 2
                        a.wait_ge(y_ready, i * G + v + 1)
                        stores = i * 16 + (stored_0[v % G] if v >= 0 else stored_0[v % G] - 16)
                        a.wait_ge(stored[v % G], stores)
                        nc.scalar.activation(ys[v % G][:], y_ps[v % 2][:], ACT.Copy).then_inc(y_copied, 1)

            rounds(a, R, one)

        @block.vector
        def _(dve):
            def take_x(i, n, first):
                dve.wait_ge(xt_ready, i * G + n + 1)
                if not (first and n < 2):
                    dve.wait_ge(ab_ready, i * G + n - 1)
                nc.vector.tensor_copy(xs_t[n % 2][:], x_ps[:]).then_inc(xt_copied, 1)

            def one(i, first, last):
                for n in range(G):
                    if n + 1 < G or not last:
                        take_x(i, n + 1, first)
                    if n < G:
                        dve.wait_ge(act_ready, i * G + n + 1)
                        if mx.gate:
                            if not (first and n < 2):
                                dve.wait_ge(hid_ready, i * G + n - 1)
                            nc.vector.scalar_tensor_tensor(out=lin[n % 2][:], in0=act[n % 2][:], scalar=0.01, in1=act[n % 2][:], op0=ALU.mult,
                                                           op1=ALU.max).then_inc(lin_ready, 1)
                            dve.wait_ge(lin_ready, i * G + n + 1)
                        if not (first and n < 2):
                            dve.wait_ge(ht_ready, i * G + n - 1)
                        nc.vector.tensor_tensor(hid[n % 2][:], (lin if mx.gate else act)[n % 2][:], b_ps[n % 2][:, 0:F], ALU.mult).then_inc(hid_ready, 1)

            take_x(0, 0, True)
            rounds(dve, R, one)


def combine(nc, c, mx, expert_rows, r, start, dst, stack, block, rows=None):
    m = Memory(nc, stack, f"com_{mx.name}")
    rows = r.rows or rows or [m.sb(f"rows{k}", [P, NT, D]) for k in range(mx.top)]
    clear = mx.cap and not r.rows
    cleared, added = m.sem("cleared"), m.sem("added")
    G = 4
    got = [m.pool_dma_sem(f"got{g}", G * mx.top) for g in range(NT // G)]

    @block.gpsimd
    def _(pool):
        if clear:
            pool.memset(rows[0][:, 0:NT // 2, :], 0.0).then_inc(cleared, 1)
            pool.wait_ge(cleared, 2)
        for t in range(NT):
            for k in range(mx.top):
                pool.indirect_dma_start(rows[k][:, t, :], None, expert_rows[0:mx.rows, :], bass.IndirectOffsetOnAxis(ap=r.pos[k][:, t:t + 1], axis=0),
                                        bounds_check=mx.rows - 1, oob_is_err=False).then_inc(got[t // G][0], 16)

    @block.vector
    def _(dve):
        if clear:
            nc.vector.memset(rows[0][:, NT // 2:, :], 0.0).then_inc(cleared, 1)
        for t in range(NT):
            if t % G == 0:
                dve.wait_ge(got[t // G][0], got[t // G][1] + 16 * G * mx.top)
            for k in range(mx.top):
                nc.vector.scalar_tensor_tensor(out=dst[:, t, :], in0=rows[k][:, t, :], scalar=r.weight[k][:, t:t + 1],
                                               in1=(start if k == 0 else dst)[:, t, :], op0=ALU.mult,
                                               op1=ALU.add).then_inc(added, 1)
                dve.wait_ge(added, mx.top * t + k + 1)

    return added, mx.top


class SharedExpert:

    def __init__(self, nc, c, w_gate, w_up, w_down, stack):
        m = Memory(nc, stack, "shx")
        self.nc, self.c = nc, c
        self.wgu, self.wd = m.sb("wgu", [P, KD, 2, D]), m.sb("wd", [P, KD, D])
        self.act, self.lin, self.hid = ([m.sb(f"{x}{n}", [P, D]) for n in range(2)] for x in ("act", "lin", "hid"))
        self.hid_t = [m.sb(f"hid_t{n}", [P, KD, P]) for n in range(2)]
        self.gu_ps = [m.ps(f"gu_ps{n}", [P, 2, D]) for n in range(2)]
        self.t_ps = m.ps("t_ps", [P, KD, P])
        self.y_ps = m.ps("y_ps", [P, D])
        names = "loaded gu_ready act_ready lin_ready hid_ready ht_ready ht_copied y_ready h_ready".split()
        (self.loaded, self.gu_ready, self.act_ready, self.lin_ready, self.hid_ready, self.ht_ready, self.ht_copied, self.y_ready,
         self.h_ready) = (m.sem(x) for x in names)
        self.loads = [(self.wgu[:, :, 0, :], w_gate.rearrange("(k p) f -> p k f", p=P), self.loaded),
                      (self.wgu[:, :, 1, :], w_up.rearrange("(k p) f -> p k f", p=P), self.loaded),
                      (self.wd[:], w_down.rearrange("(k p) f -> p k f", p=P), self.loaded)]

    def tensor(self, pe):
        nc = self.nc
        for t in range(NT + 2):
            if t == 0:
                pe.wait_ge(self.loaded, 48)
            if t < NT:
                if t >= 2:
                    pe.wait_ge(self.hid_ready, t - 1)
                for k in range(KD):
                    last = nc.tensor.matmul(self.gu_ps[t % 2][:], self.c.xt[:, k, P * t:P * (t + 1)], self.wgu[:, k, :, :], start=(k == 0), stop=(k == KD - 1))
                last.then_inc(self.gu_ready, 1)
            if 1 <= t <= NT:
                v = t - 1
                pe.wait_ge(self.hid_ready, v + 1)
                if v >= 1:
                    pe.wait_ge(self.ht_copied, v)
                for f in range(KD):
                    last = nc.tensor.transpose(self.t_ps[:, f, :], self.hid[v % 2][:, P * f:P * (f + 1)], self.c.ident[:])
                last.then_inc(self.ht_ready, 1)
            if t >= 2:
                v = t - 2
                pe.wait_ge(self.ht_copied, v + 1)
                if v >= 1:
                    pe.wait_ge(self.h_ready, v)
                for f in range(KD):
                    last = nc.tensor.matmul(self.y_ps[:], self.hid_t[v % 2][:, f, :], self.wd[:, f, :], start=(f == 0), stop=(f == KD - 1))
                last.then_inc(self.y_ready, 1)

    def scalar(self, a):
        nc = self.nc
        for t in range(NT + 2):
            if t < NT:
                a.wait_ge(self.gu_ready, t + 1)
                if t >= 2:
                    a.wait_ge(self.lin_ready, t - 1)
                nc.scalar.activation(self.act[t % 2][:], self.gu_ps[t % 2][:, 0, :], ACT.Copy).then_inc(self.act_ready, 1)
            if 1 <= t <= NT:
                a.wait_ge(self.ht_ready, t)
                if t >= 3:
                    a.wait_ge(self.y_ready, t - 2)
                nc.scalar.activation(self.hid_t[(t - 1) % 2][:], self.t_ps[:], ACT.Copy).then_inc(self.ht_copied, 1)

    def vector(self, dve):
        nc = self.nc
        for t in range(NT + 2):
            if t < NT:
                n = t % 2
                dve.wait_ge(self.act_ready, t + 1)
                if t >= 2:
                    dve.wait_ge(self.hid_ready, t - 1)
                nc.vector.scalar_tensor_tensor(out=self.lin[n][:], in0=self.act[n][:], scalar=0.01, in1=self.act[n][:], op0=ALU.mult,
                                               op1=ALU.max).then_inc(self.lin_ready, 1)
                dve.wait_ge(self.lin_ready, t + 1)
                if t >= 2:
                    dve.wait_ge(self.ht_ready, t - 1)
                nc.vector.tensor_tensor(self.hid[n][:], self.lin[n][:], self.gu_ps[n][:, 1, :], ALU.mult).then_inc(self.hid_ready, 1)
            if t >= 2:
                dve.wait_ge(self.y_ready, t - 1)
                nc.vector.tensor_copy(self.c.h[:, t - 2, :], self.y_ps[:]).then_inc(self.h_ready, 1)


class Routing:

    def __init__(self, nc, stack, mx, rows_ahead=False):
        m = Memory(nc, stack, f"r_{mx.name}")
        self.pos = [m.sb(f"pos{k}", [P, NT], I32) for k in range(mx.top)]
        self.weight = [m.sb(f"weight{k}", [P, NT]) for k in range(mx.top)]
        self.owner = m.sb("owner", [P, mx.tiles], I32)
        self.rows = [m.sb(f"rows{k}", [P, NT, D]) for k in range(mx.top)] if rows_ahead else []


def clear_rows(nc, c, rows):
    with ExitStack() as stack:
        m = Memory(nc, stack, "clr")
        zeroed = m.sem("zeroed")
        by_pool = [m.pool_dma_sem(f"stored{n}", 1)[0] for n in range(4)]
        by_sp = rows.shape[0] // P - len(by_pool)
        block = stack.enter_context(nc.Block())

        @block.vector
        def _(dve):
            nc.vector.memset(c.zero[:], 0.0).then_inc(zeroed, 1)

        @block.gpsimd
        def _(pool):
            pool.wait_ge(zeroed, 1)
            for n, semaphore in enumerate(by_pool):
                tile = by_sp + n
                pool.dma_start(rows[P * tile:P * (tile + 1), :], c.zero[:]).then_inc(semaphore, 16)
            for semaphore in by_pool:
                pool.wait_ge(semaphore, 16)

        return rows[0:P * by_sp, :].rearrange("(t p) d -> p t d", p=P), c.zero[:].unsqueeze(1).to_broadcast([P, by_sp, D]), c.rows_cleared


def build(nc, d, out):
    def group(prefix, **more):
        return {**{n[len(prefix):]: ap for n, ap in d.items() if n.startswith(prefix)}, **more}

    mixtures = {
        "f1": Mixture("f1", 2, 2 * T // E, 1024),
        "c2": Mixture("c2", 2, 0, 128, temperature=0.5, normalised=True, by_rows=True, gate=True),
        "f2": Mixture("f2", 1, T // E, 1024),
        "f3": Mixture("f3", 2, 0, 512, by_rows=True),
    }

    def scratch(name, shape):
        return nc.dram_tensor(name, shape, F32, kind="Internal").ap()

    Memory.cleared, Memory.pool_dma_semaphores = [], {}
    with ExitStack() as stack:
        stack.enter_context(nc.allow_non_contiguous_dma(reason="short vectors by column"))
        c = shared(nc, stack)
        rows = scratch("sorted", [max(mx.rows for mx in mixtures.values()), D])
        done = scratch("expert", [max(mx.rows for mx in mixtures.values()), D])
        make_constants(nc, c, d["x"])
        bands = {l: scratch(f"band{l}", [H, P, S]) for l in (1, 3)}
        revs = {l: scratch(f"rev{l}", [H, REV]) for l in (1, 3)}
        relative_bias(nc, c, [(group(f"L{l}_cond_"), revs[l]) for l in (1, 3)])
        later = [(bands[l], bass.AP(tensor=revs[l].tensor, offset=P - 1, ap=[[REV, H], [-1, P], [1, S]]), c.bands_stored) for l in (1, 3)]
        later.append(clear_rows(nc, c, rows))

        def attend(l, w, mask, bias_of, causal, w_out, later=(), beside=None, ternary=None):
            with ExitStack() as inner:
                attention_memory(nc, inner, c, l)
                with stage(nc) as (stack, block):
                    if beside is not None:
                        beside(stack, block)
                    attention_inputs(nc, c, l, w, d["cond_64"], mask, stack, block)
                attention(nc, c, l, bias_of, causal)
                with stage(nc) as (stack, block):
                    if ternary is not None:
                        part = TernaryLinear(nc, c, ternary, stack)
                        part.prepare(block)
                    h_ready, two_banks, y_ps, y_read = attention_output(nc, c, l, w_out, w["g_out"], d["cond_64"], later, stack, block)
                    if ternary is not None:
                        part.apply(block, h_ready, two_banks, y_ps, y_read)

        w = group("L0_cond_", g=d["L0_cond_g_in"])
        given = d["fside_16xSxS_0"]
        attend(0, w, d["mask_BxS_bk0"], lambda i, hh, q: given[ds(i * 2 + hh, 1), P * q:P * (q + 1), 0:P * (q + 1)].rearrange("a p n -> (a p) n"),
               True, w["Wo"], later, ternary=d["L0_ffn_weight"])

        w = group("L1_cond_", g=d["L1_cond_g_norm"])
        attend(1, w, d["mask_BxS_bf1"], band_bias(bands[1]), False, w["Wout"])
        f1, c2, f2, f3 = (mixtures[n] for n in ("f1", "c2", "f2", "f3"))
        with ExitStack() as routed:
            r_c2, r_f2 = Routing(nc, routed, c2), Routing(nc, routed, f2)
            with ExitStack() as inner:
                r_f1 = Routing(nc, inner, f1, rows_ahead=True)
                w = group("L1_ffn_")
                cw = CapacityWeights(nc, inner, f1, w["w1"], w["w2"])
                with stage(nc) as (stack, block):
                    route(nc, c, f1, c.h, w["w_router"], rows, r_f1, cw.loads, stack, block)
                experts_by_capacity(nc, c, f1, cw, rows, done, r_f1, ACT.Gelu_apprx_tanh, bias=w["bias"])

                w = group("L2_cond_")
                tw = TileWeights(nc, inner, c2, (w["w_gate"], w["w_up"], w["w_down"]))
                with stage(nc) as (stack, block):
                    shared_part = SharedExpert(nc, c, w["sw_gate"], w["sw_up"], w["sw_down"], stack)
                    added = combine(nc, c, f1, done, r_f1, c.x, c.x, stack, block)
                    route(nc, c, c2, c.x, w["wt"], rows, r_c2, shared_part.loads + tw.loads, stack, block, after=added, beside=shared_part,
                          cond=d["cond_64"], w_cond=w["wg"])
                experts_by_tile(nc, c, c2, tw, rows, done, r_c2)
            with ExitStack() as inner:
                w = group("L2_ffn_")
                cw = CapacityWeights(nc, inner, f2, w["W1"], w["W2"])
                with stage(nc) as (stack, block):
                    added = combine(nc, c, c2, done, r_c2, c.h, c.h, stack, block)
                    route(nc, c, f2, c.h, w["Wr"], rows, r_f2, cw.loads, stack, block, after=added)
                experts_by_capacity(nc, c, f2, cw, rows, done, r_f2, ACT.Relu)

            w = group("L3_cond_", g=d["L3_cond_g_norm"])

            def beside(stack, block):
                out_rows = c.out_t[:, 0:NT * D // T, :].rearrange("p a (t d) -> p (a t) d", d=D)
                combine(nc, c, f2, done, r_f2, c.x, c.x, stack, block, rows=[out_rows])

            attend(3, w, d["mask_BxS_bf1"], band_bias(bands[3]), False, w["Wout"], beside=beside)
        w = group("L3_ffn_")
        with ExitStack() as inner:
            r = Routing(nc, inner, f3)
            tw = TileWeights(nc, inner, f3, (w["w1"], w["w3"], w["w2"]))
            with stage(nc) as (stack, block):
                route(nc, c, f3, c.h, w["gate_w"], rows, r, tw.loads, stack, block)
            experts_by_tile(nc, c, f3, tw, rows, done, r)
            with stage(nc) as (stack, block):
                added, per_tile = combine(nc, c, f3, done, r, c.x, c.x, stack, block)
                out_stored = Memory(nc, stack, "end").sem("out_stored")

                @block.sync
                def _(sp):
                    for b in range(B):
                        sp.wait_ge(added, per_tile * QT * (b + 1))
                        sp.dma_start(out[b].rearrange("(t p) d -> p t d", p=P), c.x[:, QT * b:QT * (b + 1), :]).then_inc(out_stored, 16)
                    sp.wait_ge(out_stored, 16 * B)


def kernel(**inputs):
    import numpy as _np
    import concourse.bacc as _bacc
    from concourse import mybir as _mybir
    from concourse.bass_utils import run_bass_kernel_spmd as _run

    nc = _bacc.Bacc("TRN2", target_bir_lowering=False, num_devices=1)
    arrays, args = {}, {}
    for name, a in inputs.items():
        a = _np.ascontiguousarray(a)
        if a.dtype == bool:
            a = a.view(_np.uint32)
        arrays[f"in_{name}_dram"] = a
        args[name] = nc.dram_tensor(f"in_{name}_dram", a.shape, _mybir.dt.from_np(a.dtype), kind="ExternalInput").ap()
    out = nc.dram_tensor("out_0_dram", (B, S, D), F32, kind="ExternalOutput").ap()
    build(nc, args, out)
    r = _run(nc, [arrays], core_ids=[0])
    return r.results[0]["out_0_dram"]
```
